# Optimizing a Trainium2 kernel written in Bass

```python
import numpy as np
import jax
import jax.numpy as jnp

def _softmax(x, axis=-1):
    return jax.nn.softmax(x, axis=axis)

def _gelu(x):
    return jax.nn.gelu(x, approximate=True)

def _silu(x):
    return jax.nn.silu(x)

def _sigmoid(x):
    return jax.nn.sigmoid(x)

def _layernorm(x, axis=-1, eps=1e-05):
    m = jnp.mean(x, axis=axis, keepdims=True)
    v = jnp.var(x, axis=axis, keepdims=True)
    return (x - m) / jnp.sqrt(v + eps)

def _scatter_add(tgt, idx, src, axis=0):
    return tgt.at[idx].add(src)

def _segment_sum(src, seg, n):
    return jax.ops.segment_sum(src, seg, n)
kernel_name = 'mk_adaln_ffn_d4_seqx_r4_3e25c4'

def setup_inputs(seed: int=0):
    np.random.seed(seed)
    _w = jnp.asarray

    def _rec_inputs():
        import jax
        import jax.numpy as jnp
        _rk = jax.random.key(seed)
        x = -0.000125 + 0.9999 * jax.random.normal(jax.random.fold_in(_rk, 1), (4, 512, 256), jnp.float32)
        _lenS = 512 - jax.random.randint(jax.random.fold_in(_rk, 7), (4,), 0, max(1, 512 // 4) + 1, jnp.int32)
        _lenS2 = 512 - jax.random.randint(jax.random.fold_in(_rk, 8), (4,), 0, max(1, 512 // 4) + 1, jnp.int32)
        cond_8 = jax.random.uniform(jax.random.fold_in(_rk, 11), (4, 8), jnp.float32, 0.0, 0.983423)
        return (x, cond_8)
    x, cond_8 = _rec_inputs()

    def _L0_cond_setup():
        import jax, jax.numpy as jnp
        import numpy as np
        B, S, D = (16, 512, 256)
        E, H = (8, 512)
        key = jax.random.key(seed)
        ks = jax.random.split(key, 8)
        scale = 0.02
        x = jax.random.normal(ks[0], (B, S, D), dtype=jnp.float32)
        opcode_onehot = jax.random.uniform(ks[1], (B, E), dtype=jnp.float32)
        W_up = jax.random.normal(ks[2], (E, H, D), dtype=jnp.float32) * scale
        b_up = jnp.zeros((E, H), dtype=jnp.float32)
        W_gate = jax.random.normal(ks[3], (E, H, D), dtype=jnp.float32) * scale
        b_gate = jnp.zeros((E, H), dtype=jnp.float32)
        W_down = jax.random.normal(ks[4], (E, D, H), dtype=jnp.float32) * scale
        b_down = jnp.zeros((E, D), dtype=jnp.float32)
        return {'x': x, 'opcode_onehot': opcode_onehot, 'W_up': W_up, 'b_up': b_up, 'W_gate': W_gate, 'b_gate': b_gate, 'W_down': W_down, 'b_down': b_down}
    _L0_cond_all = _L0_cond_setup()
    _L0_cond_in = {k: v for k, v in _L0_cond_all.items() if k in ('W_up', 'b_up', 'W_gate', 'b_gate', 'W_down', 'b_down')}
    del _L0_cond_all

    def _L0_ffn_setup():
        import jax, jax.numpy as jnp
        import numpy as np
        HIDDEN = 256
        HEAD_DIM = 64
        N_EXPERTS = 16
        MIN_EXPERTS = 2
        B, T = (4, 512)

        def _normalize(x, axis):
            n = jnp.sqrt(jnp.sum(x * x, axis=axis, keepdims=True))
            return x / jnp.maximum(n, 1e-12)

        def _ste(x):
            hard = jax.lax.stop_gradient((x > 0).astype(x.dtype))
            return hard + x - jax.lax.stop_gradient(x)

        def _gating(hidden_states, sim_matrix, gates):
            b, t, c = hidden_states.shape
            flat = hidden_states.reshape(b * t, c)
            logits = _normalize(flat, -1) @ _normalize(sim_matrix, 0) - jax.nn.sigmoid(gates)
            gated = jax.nn.relu(logits)
            mask = _ste(gated)
            inactive = jnp.sum(mask, axis=1) == 0
            _, fb_idx = jax.lax.top_k(logits, MIN_EXPERTS)
            fb = jnp.zeros_like(mask).at[jnp.arange(b * t)[:, None], fb_idx].set(1.0)
            fb_applied = inactive[:, None] & (fb > 0)
            mask = jnp.where(fb_applied, 1.0, mask)
            masked_logits = jnp.where(mask > 0, gated, -jnp.inf)
            return jax.nn.softmax(masked_logits, axis=-1).reshape(b, t, -1)
        key = jax.random.key(seed)
        ks = jax.random.split(key, 6)
        xav_qkv = float(np.sqrt(6.0 / (HIDDEN + HEAD_DIM)))
        return {'hidden_states': jax.random.normal(ks[0], (B, T, HIDDEN), dtype=jnp.float32), 'sim_matrix': jax.random.normal(ks[1], (HIDDEN, N_EXPERTS), dtype=jnp.float32), 'gates': jnp.zeros((N_EXPERTS,), dtype=jnp.float32), 'q_proj': jax.random.uniform(ks[2], (N_EXPERTS, HIDDEN, HEAD_DIM), jnp.float32, -xav_qkv, xav_qkv), 'k_proj': jax.random.uniform(ks[3], (N_EXPERTS, HIDDEN, HEAD_DIM), jnp.float32, -xav_qkv, xav_qkv), 'v_proj': jax.random.uniform(ks[4], (N_EXPERTS, HIDDEN, HEAD_DIM), jnp.float32, -xav_qkv, xav_qkv), 'o_proj': jax.random.uniform(ks[5], (N_EXPERTS, HEAD_DIM, HIDDEN), jnp.float32, -xav_qkv, xav_qkv)}
    _L0_ffn_all = _L0_ffn_setup()
    _L0_ffn_in = {k: v for k, v in _L0_ffn_all.items() if k in ('sim_matrix', 'gates', 'q_proj', 'k_proj', 'v_proj', 'o_proj')}
    del _L0_ffn_all

    def _L1_cond_setup():
        import jax, jax.numpy as jnp
        import numpy as np
        key = jax.random.key(seed)
        k1, k2, k3, k4, k5 = jax.random.split(key, 5)
        B, N, T, O, G = (32, 64, 256, 256, 8)
        x = jax.random.normal(k1, (B, N, T), dtype=jnp.float32)
        y = jax.random.uniform(k2, (B, G), dtype=jnp.float32)
        weight = jax.random.normal(k3, (G, O, T), dtype=jnp.float32) * (1.0 / np.sqrt(T))
        mask = jax.random.uniform(k4, (O, T), dtype=jnp.float32)
        bias = jax.random.normal(k5, (O,), dtype=jnp.float32)
        return {'x': x, 'y': y, 'weight': weight, 'mask': mask, 'bias': bias}
    _L1_cond_all = _L1_cond_setup()
    _L1_cond_in = {k: v for k, v in _L1_cond_all.items() if k in ('weight', 'mask', 'bias')}
    del _L1_cond_all

    def _L1_ffn_setup():
        import jax, jax.numpy as jnp
        import numpy as np
        B, L, D = (2, 512, 256)
        E = 15
        H = D * 1
        K = 3
        T = 1.0
        key = jax.random.key(seed)
        ks = jax.random.split(key, 12)
        s = 0.02
        return {'x': jax.random.normal(ks[0], (B, L, D), dtype=jnp.float32), 'router_W': jax.random.normal(ks[1], (D, E), dtype=jnp.float32) * s, 'router_b': jnp.zeros((E,), dtype=jnp.float32), 'sW1': jax.random.normal(ks[2], (D, H), dtype=jnp.float32) * s, 'sb1': jnp.zeros((H,), dtype=jnp.float32), 'sW2': jax.random.normal(ks[3], (H, D), dtype=jnp.float32) * s, 'sb2': jnp.zeros((D,), dtype=jnp.float32), 'eW1': jax.random.normal(ks[4], (E, D, H), dtype=jnp.float32) * s, 'eb1': jnp.zeros((E, H), dtype=jnp.float32), 'eW2': jax.random.normal(ks[5], (E, H, D), dtype=jnp.float32) * s, 'eb2': jnp.zeros((E, D), dtype=jnp.float32)}
    _L1_ffn_all = _L1_ffn_setup()
    _L1_ffn_in = {k: v for k, v in _L1_ffn_all.items() if k in ('router_W', 'router_b', 'sW1', 'sb1', 'sW2', 'sb2', 'eW1', 'eb1', 'eW2', 'eb2')}
    del _L1_ffn_all

    def _L2_cond_setup():
        import jax, jax.numpy as jnp
        import numpy as np
        R = 16
        ALPHA = 32.0
        SCALING = ALPHA / R
        key = jax.random.key(seed)
        ks = jax.random.split(key, 6)
        B, T, C, O, E = (16, 375, 256, 256, 8)
        x = jax.random.normal(ks[0], (B, T, C), dtype=jnp.float32)
        w = jax.random.uniform(ks[1], (B, E), dtype=jnp.float32)
        W_base = jax.random.normal(ks[2], (O, C), dtype=jnp.float32) * 0.02
        b_base = jax.random.normal(ks[3], (O,), dtype=jnp.float32) * 0.02
        As = jax.random.normal(ks[4], (E, R, C), dtype=jnp.float32) * 0.02
        Bs = jax.random.normal(ks[5], (E, O, R), dtype=jnp.float32) * 0.02
        return {'x': x, 'w': w, 'W_base': W_base, 'b_base': b_base, 'As': As, 'Bs': Bs}
    _L2_cond_all = _L2_cond_setup()
    _L2_cond_in = {k: v for k, v in _L2_cond_all.items() if k in ('W_base', 'b_base', 'As', 'Bs')}
    del _L2_cond_all

    def _L2_ffn_setup():
        import jax, jax.numpy as jnp
        import numpy as np
        CAPACITY_FACTOR = 0.5
        key = jax.random.key(seed)
        ks = jax.random.split(key, 5)
        B, S, D, F = (4, 1024, 256, 1024)
        scale_in = 1.0 / np.sqrt(D)
        scale_ff = 1.0 / np.sqrt(F)
        return {'hidden_states': jax.random.normal(ks[0], (B, S, D), dtype=jnp.float32), 'w_router': jax.random.normal(ks[1], (D,), dtype=jnp.float32) * scale_in, 'W1': jax.random.normal(ks[2], (D, F), dtype=jnp.float32) * scale_in, 'b1': jnp.zeros((F,), dtype=jnp.float32), 'W2': jax.random.normal(ks[3], (F, D), dtype=jnp.float32) * scale_ff, 'b2': jnp.zeros((D,), dtype=jnp.float32)}
    _L2_ffn_all = _L2_ffn_setup()
    _L2_ffn_in = {k: v for k, v in _L2_ffn_all.items() if k in ('w_router', 'W1', 'b1', 'W2', 'b2')}
    del _L2_ffn_all

    def _L3_cond_setup():
        import jax, jax.numpy as jnp
        import numpy as np
        TOP_K = 2
        NUM_MOE_LAYERS = 12

        def _gemma_mlp(x, gate_w, up_w, down_w):
            g = jnp.einsum('bsh,hi->bsi', x, gate_w)
            u = jnp.einsum('bsh,hi->bsi', x, up_w)
            return jnp.einsum('bsi,ih->bsh', jax.nn.gelu(g, approximate=True) * u, down_w)
        key = jax.random.key(seed)
        ks = jax.random.split(key, 8)
        B, S, H, I, E = (32, 64, 256, 1024, 8)
        std = 0.02
        return {'x': jax.random.normal(ks[0], (B, S, H), jnp.float32), 'router_logits': jax.random.normal(ks[1], (B, E), jnp.float32), 'skill_gate': jax.random.normal(ks[2], (E, H, I), jnp.float32) * std, 'skill_up': jax.random.normal(ks[3], (E, H, I), jnp.float32) * std, 'skill_down': jax.random.normal(ks[4], (E, I, H), jnp.float32) * std, 'shared_gate': jax.random.normal(ks[5], (H, I), jnp.float32) * std, 'shared_up': jax.random.normal(ks[6], (H, I), jnp.float32) * std, 'shared_down': jax.random.normal(ks[7], (I, H), jnp.float32) * std}
    _L3_cond_all = _L3_cond_setup()
    _L3_cond_in = {k: v for k, v in _L3_cond_all.items() if k in ('skill_gate', 'skill_up', 'skill_down', 'shared_gate', 'shared_up', 'shared_down')}
    del _L3_cond_all

    def _L3_ffn_setup():
        import jax, jax.numpy as jnp
        import numpy as np
        D = 256
        H = 16
        HD = D // H
        L = 64
        E = 8
        B, T = (4, 512)
        EPS = 1e-06

        def _glorot(k, shape):
            fan_in, fan_out = (shape[-2], shape[-1])
            lim = np.sqrt(6.0 / (fan_in + fan_out)).astype(np.float32)
            return jax.random.uniform(k, shape, jnp.float32, -lim, lim)

        def _rmsnorm(x, gamma):
            return gamma * x * jax.lax.rsqrt(jnp.mean(x * x, axis=-1, keepdims=True) + EPS)
        key = jax.random.key(seed)
        ks = jax.random.split(key, 8)
        return {'x': jax.random.normal(ks[0], (B, T, D), jnp.float32), 'gamma1': jnp.ones((D,), jnp.float32), 'Wq': _glorot(ks[1], (D, D)), 'bq': jnp.zeros((D,), jnp.float32), 'Wdown': _glorot(ks[2], (D, L)), 'bdown': jnp.zeros((L,), jnp.float32), 'Wup': _glorot(ks[3], (L, 2 * D)), 'bup': jnp.zeros((2 * D,), jnp.float32), 'Wo': _glorot(ks[4], (D, D)), 'bo': jnp.zeros((D,), jnp.float32), 'gamma2': jnp.ones((D,), jnp.float32), 'Wg': _glorot(ks[5], (D, E)), 'bg': jnp.zeros((E,), jnp.float32), 'We': _glorot(ks[6], (E, D, D))}
    _L3_ffn_all = _L3_ffn_setup()
    _L3_ffn_in = {k: v for k, v in _L3_ffn_all.items() if k in ('gamma1', 'Wq', 'bq', 'Wdown', 'bdown', 'Wup', 'bup', 'Wo', 'bo', 'gamma2', 'Wg', 'bg', 'We')}
    del _L3_ffn_all
    return {'x': x, 'cond_8': cond_8, 'L0_cond_W_up': _L0_cond_in['W_up'], 'L0_cond_b_up': _L0_cond_in['b_up'], 'L0_cond_W_gate': _L0_cond_in['W_gate'], 'L0_cond_b_gate': _L0_cond_in['b_gate'], 'L0_cond_W_down': _L0_cond_in['W_down'], 'L0_cond_b_down': _L0_cond_in['b_down'], 'L0_ffn_sim_matrix': _L0_ffn_in['sim_matrix'], 'L0_ffn_gates': _L0_ffn_in['gates'], 'L0_ffn_q_proj': _L0_ffn_in['q_proj'], 'L0_ffn_k_proj': _L0_ffn_in['k_proj'], 'L0_ffn_v_proj': _L0_ffn_in['v_proj'], 'L0_ffn_o_proj': _L0_ffn_in['o_proj'], 'L1_cond_weight': _L1_cond_in['weight'], 'L1_cond_mask': _L1_cond_in['mask'], 'L1_cond_bias': _L1_cond_in['bias'], 'L1_ffn_router_W': _L1_ffn_in['router_W'], 'L1_ffn_router_b': _L1_ffn_in['router_b'], 'L1_ffn_sW1': _L1_ffn_in['sW1'], 'L1_ffn_sb1': _L1_ffn_in['sb1'], 'L1_ffn_sW2': _L1_ffn_in['sW2'], 'L1_ffn_sb2': _L1_ffn_in['sb2'], 'L1_ffn_eW1': _L1_ffn_in['eW1'], 'L1_ffn_eb1': _L1_ffn_in['eb1'], 'L1_ffn_eW2': _L1_ffn_in['eW2'], 'L1_ffn_eb2': _L1_ffn_in['eb2'], 'L2_cond_W_base': _L2_cond_in['W_base'], 'L2_cond_b_base': _L2_cond_in['b_base'], 'L2_cond_As': _L2_cond_in['As'], 'L2_cond_Bs': _L2_cond_in['Bs'], 'L2_ffn_w_router': _L2_ffn_in['w_router'], 'L2_ffn_W1': _L2_ffn_in['W1'], 'L2_ffn_b1': _L2_ffn_in['b1'], 'L2_ffn_W2': _L2_ffn_in['W2'], 'L2_ffn_b2': _L2_ffn_in['b2'], 'L3_cond_skill_gate': _L3_cond_in['skill_gate'], 'L3_cond_skill_up': _L3_cond_in['skill_up'], 'L3_cond_skill_down': _L3_cond_in['skill_down'], 'L3_cond_shared_gate': _L3_cond_in['shared_gate'], 'L3_cond_shared_up': _L3_cond_in['shared_up'], 'L3_cond_shared_down': _L3_cond_in['shared_down'], 'L3_ffn_gamma1': _L3_ffn_in['gamma1'], 'L3_ffn_Wq': _L3_ffn_in['Wq'], 'L3_ffn_bq': _L3_ffn_in['bq'], 'L3_ffn_Wdown': _L3_ffn_in['Wdown'], 'L3_ffn_bdown': _L3_ffn_in['bdown'], 'L3_ffn_Wup': _L3_ffn_in['Wup'], 'L3_ffn_bup': _L3_ffn_in['bup'], 'L3_ffn_Wo': _L3_ffn_in['Wo'], 'L3_ffn_bo': _L3_ffn_in['bo'], 'L3_ffn_gamma2': _L3_ffn_in['gamma2'], 'L3_ffn_Wg': _L3_ffn_in['Wg'], 'L3_ffn_bg': _L3_ffn_in['bg'], 'L3_ffn_We': _L3_ffn_in['We']}

def reference(x, cond_8, L0_cond_W_up, L0_cond_b_up, L0_cond_W_gate, L0_cond_b_gate, L0_cond_W_down, L0_cond_b_down, L0_ffn_sim_matrix, L0_ffn_gates, L0_ffn_q_proj, L0_ffn_k_proj, L0_ffn_v_proj, L0_ffn_o_proj, L1_cond_weight, L1_cond_mask, L1_cond_bias, L1_ffn_router_W, L1_ffn_router_b, L1_ffn_sW1, L1_ffn_sb1, L1_ffn_sW2, L1_ffn_sb2, L1_ffn_eW1, L1_ffn_eb1, L1_ffn_eW2, L1_ffn_eb2, L2_cond_W_base, L2_cond_b_base, L2_cond_As, L2_cond_Bs, L2_ffn_w_router, L2_ffn_W1, L2_ffn_b1, L2_ffn_W2, L2_ffn_b2, L3_cond_skill_gate, L3_cond_skill_up, L3_cond_skill_down, L3_cond_shared_gate, L3_cond_shared_up, L3_cond_shared_down, L3_ffn_gamma1, L3_ffn_Wq, L3_ffn_bq, L3_ffn_Wdown, L3_ffn_bdown, L3_ffn_Wup, L3_ffn_bup, L3_ffn_Wo, L3_ffn_bo, L3_ffn_gamma2, L3_ffn_Wg, L3_ffn_bg, L3_ffn_We):
    import jax
    import jax.numpy as jnp

    def _L0_cond_ref(x, opcode_onehot, W_up, b_up, W_gate, b_gate, W_down, b_down):
        import jax, jax.numpy as jnp
        import numpy as np
        B, S, D = (16, 512, 256)
        E, H = (8, 512)
        expert = jnp.argmax(opcode_onehot, axis=-1)
        wu, bu = (W_up[expert], b_up[expert])
        wg, bg = (W_gate[expert], b_gate[expert])
        wd, bd = (W_down[expert], b_down[expert])
        up = jnp.einsum('bsd,bhd->bsh', x, wu) + bu[:, None, :]
        gate = jnp.einsum('bsd,bhd->bsh', x, wg) + bg[:, None, :]
        hidden = jax.nn.silu(up) * gate
        out = jnp.einsum('bsh,bdh->bsd', hidden, wd) + bd[:, None, :]
        return out

    def _L0_ffn_ref(hidden_states, sim_matrix, gates, q_proj, k_proj, v_proj, o_proj):
        import jax, jax.numpy as jnp
        import numpy as np
        HIDDEN = 256
        HEAD_DIM = 64
        N_EXPERTS = 16
        MIN_EXPERTS = 2
        B, T = (4, 512)

        def _normalize(x, axis):
            n = jnp.sqrt(jnp.sum(x * x, axis=axis, keepdims=True))
            return x / jnp.maximum(n, 1e-12)

        def _ste(x):
            hard = jax.lax.stop_gradient((x > 0).astype(x.dtype))
            return hard + x - jax.lax.stop_gradient(x)

        def _gating(hidden_states, sim_matrix, gates):
            b, t, c = hidden_states.shape
            flat = hidden_states.reshape(b * t, c)
            logits = _normalize(flat, -1) @ _normalize(sim_matrix, 0) - jax.nn.sigmoid(gates)
            gated = jax.nn.relu(logits)
            mask = _ste(gated)
            inactive = jnp.sum(mask, axis=1) == 0
            _, fb_idx = jax.lax.top_k(logits, MIN_EXPERTS)
            fb = jnp.zeros_like(mask).at[jnp.arange(b * t)[:, None], fb_idx].set(1.0)
            fb_applied = inactive[:, None] & (fb > 0)
            mask = jnp.where(fb_applied, 1.0, mask)
            masked_logits = jnp.where(mask > 0, gated, -jnp.inf)
            return jax.nn.softmax(masked_logits, axis=-1).reshape(b, t, -1)
        b, t, c = hidden_states.shape
        rw = _gating(hidden_states, sim_matrix, gates)
        q = jnp.einsum('bte,bted->btd', rw, jnp.einsum('btc,ecd->bted', hidden_states, q_proj))
        k = jnp.einsum('bte,bted->btd', rw, jnp.einsum('btc,ecd->bted', hidden_states, k_proj))
        v = jnp.einsum('bte,bted->btd', rw, jnp.einsum('btc,ecd->bted', hidden_states, v_proj))
        scale = 1.0 / jnp.sqrt(jnp.asarray(HEAD_DIM, dtype=q.dtype))
        scores = jnp.einsum('bqd,bkd->bqk', q, k) * scale
        causal = jnp.tril(jnp.ones((t, t), dtype=bool))
        scores = jnp.where(causal, scores, -jnp.inf)
        attn = jnp.einsum('bqk,bkd->bqd', jax.nn.softmax(scores, axis=-1), v)
        mixed = attn[:, :, None, :] * rw[..., None]
        return jnp.einsum('bted,edc->btc', mixed, o_proj)

    def _L1_cond_ref(x, y, weight, mask, bias):
        import jax, jax.numpy as jnp
        import numpy as np
        masked_w = weight * mask[None, :, :]
        w_bot = jnp.einsum('bg,got->bot', y, masked_w)
        return jnp.einsum('bnt,bot->bno', x, w_bot) + bias

    def _L1_ffn_ref(x, router_W, router_b, sW1, sb1, sW2, sb2, eW1, eb1, eW2, eb2):
        import jax, jax.numpy as jnp
        import numpy as np
        B, L, D = (2, 512, 256)
        E = 15
        H = D * 1
        K = 3
        T = 1.0
        b, l, d = x.shape
        n = b * l
        xt = x.reshape(n, d)
        shared = jax.nn.relu(xt @ sW1 + sb1) @ sW2 + sb2
        logits = xt @ router_W + router_b
        probs = jax.nn.softmax(logits / T, axis=-1)
        top_p, top_i = jax.lax.top_k(probs, K)
        cw = jnp.zeros((n, E), dtype=probs.dtype)
        cw = cw.at[jnp.arange(n)[:, None], top_i].set(top_p)
        h = jax.nn.relu(jnp.einsum('nd,edh->neh', xt, eW1) + eb1)
        ye = jnp.einsum('neh,ehd->ned', h, eW2) + eb2
        routed = jnp.einsum('ned,ne->nd', ye, cw)
        return (shared + routed).reshape(b, l, d)

    def _L2_cond_ref(x, w, W_base, b_base, As, Bs):
        import jax, jax.numpy as jnp
        import numpy as np
        R = 16
        ALPHA = 32.0
        SCALING = ALPHA / R
        out = jnp.einsum('btc,oc->bto', x, W_base) + b_base
        h = jnp.einsum('btc,erc->bter', x, As)
        lora = jnp.einsum('bter,eor,be->bto', h, Bs, w)
        return out + lora * SCALING

    def _L2_ffn_ref(hidden_states, w_router, W1, b1, W2, b2):
        import jax, jax.numpy as jnp
        import numpy as np
        CAPACITY_FACTOR = 0.5
        'Mixture-of-Depths block: route top-k tokens through an FFN inner block,\n            scatter back with sigmoid router weights; bypassed tokens pass through.'
        B, S, D = hidden_states.shape
        k = int(S * CAPACITY_FACTOR)
        scores = jnp.einsum('bsd,d->bs', hidden_states, w_router)
        top_scores, top_idx = jax.lax.top_k(scores, k)
        weights = jax.nn.sigmoid(top_scores)
        selected = jnp.take_along_axis(hidden_states, top_idx[:, :, None], axis=1)
        h = jax.nn.gelu(jnp.einsum('bkd,df->bkf', selected, W1) + b1)
        processed = jnp.einsum('bkf,fd->bkd', h, W2) + b2
        update = weights[:, :, None] * processed

        def scatter_one(xb, ib, ub):
            return xb.at[ib].add(ub)
        output = jax.vmap(scatter_one)(hidden_states, top_idx, update)
        return output

    def _L3_cond_ref(x, router_logits, skill_gate, skill_up, skill_down, shared_gate, shared_up, shared_down):
        import jax, jax.numpy as jnp
        import numpy as np
        TOP_K = 2
        NUM_MOE_LAYERS = 12

        def _gemma_mlp(x, gate_w, up_w, down_w):
            g = jnp.einsum('bsh,hi->bsi', x, gate_w)
            u = jnp.einsum('bsh,hi->bsi', x, up_w)
            return jnp.einsum('bsi,ih->bsh', jax.nn.gelu(g, approximate=True) * u, down_w)
        B = x.shape[0]
        E = skill_gate.shape[0]
        rw = jax.nn.softmax(router_logits.astype(jnp.float32), axis=-1)
        w, sel = jax.lax.top_k(rw, TOP_K)
        w = w / w.sum(axis=-1, keepdims=True)
        w = w.astype(x.dtype)
        scale = 1.0 / NUM_MOE_LAYERS
        w = scale * w + (1.0 - scale) * jax.lax.stop_gradient(w)
        dense_w = jnp.zeros((B, E), x.dtype).at[jnp.arange(B)[:, None], sel].add(w)

        def step(acc, params):
            g, u, d, we = params
            return (acc + we[:, None, None] * _gemma_mlp(x, g, u, d), None)
        out, _ = jax.lax.scan(step, jnp.zeros_like(x), (skill_gate, skill_up, skill_down, dense_w.T))
        out = out + _gemma_mlp(x, shared_gate, shared_up, shared_down)
        return out

    def _L3_ffn_ref(x, gamma1, Wq, bq, Wdown, bdown, Wup, bup, Wo, bo, gamma2, Wg, bg, We):
        import jax, jax.numpy as jnp
        import numpy as np
        D = 256
        H = 16
        HD = D // H
        L = 64
        E = 8
        B, T = (4, 512)
        EPS = 1e-06

        def _glorot(k, shape):
            fan_in, fan_out = (shape[-2], shape[-1])
            lim = np.sqrt(6.0 / (fan_in + fan_out)).astype(np.float32)
            return jax.random.uniform(k, shape, jnp.float32, -lim, lim)

        def _rmsnorm(x, gamma):
            return gamma * x * jax.lax.rsqrt(jnp.mean(x * x, axis=-1, keepdims=True) + EPS)
        b, t = (x.shape[0], x.shape[1])
        h = _rmsnorm(x, gamma1)
        q = (h @ Wq + bq).reshape(b, t, H, HD)
        kv = ((h @ Wdown + bdown) @ Wup + bup).reshape(b, t, H, 2 * HD)
        k, v = jnp.split(kv, 2, axis=-1)
        att = jnp.einsum('bthd,btgd->bthg', q, k) / np.sqrt(HD).astype(np.float32)
        att = jax.nn.softmax(att, axis=-1)
        out = jnp.einsum('bthg,btgd->bthd', att, v).reshape(b, t, D)
        x = x + (out @ Wo + bo)
        h2 = _rmsnorm(x, gamma2)
        gate = jax.nn.softmax(h2 @ Wg + bg, axis=-1)
        combined = jnp.einsum('btd,edf,bte->btf', h2, We, gate)
        return x + combined
    x = x + _L0_ffn_ref(_L0_cond_ref(x, cond_8, L0_cond_W_up, L0_cond_b_up, L0_cond_W_gate, L0_cond_b_gate, L0_cond_W_down, L0_cond_b_down), L0_ffn_sim_matrix, L0_ffn_gates, L0_ffn_q_proj, L0_ffn_k_proj, L0_ffn_v_proj, L0_ffn_o_proj)
    x = x + _L1_ffn_ref(_L1_cond_ref(x, cond_8, L1_cond_weight, L1_cond_mask, L1_cond_bias), L1_ffn_router_W, L1_ffn_router_b, L1_ffn_sW1, L1_ffn_sb1, L1_ffn_sW2, L1_ffn_sb2, L1_ffn_eW1, L1_ffn_eb1, L1_ffn_eW2, L1_ffn_eb2)
    x = x + _L2_ffn_ref(_L2_cond_ref(x, cond_8, L2_cond_W_base, L2_cond_b_base, L2_cond_As, L2_cond_Bs), L2_ffn_w_router, L2_ffn_W1, L2_ffn_b1, L2_ffn_W2, L2_ffn_b2)
    x = x + _L3_ffn_ref(_L3_cond_ref(x, cond_8, L3_cond_skill_gate, L3_cond_skill_up, L3_cond_skill_down, L3_cond_shared_gate, L3_cond_shared_up, L3_cond_shared_down), L3_ffn_gamma1, L3_ffn_Wq, L3_ffn_bq, L3_ffn_Wdown, L3_ffn_bdown, L3_ffn_Wup, L3_ffn_bup, L3_ffn_Wo, L3_ffn_bo, L3_ffn_gamma2, L3_ffn_Wg, L3_ffn_bg, L3_ffn_We)
    return x

_drawn_inputs = setup_inputs


def setup_inputs(seed=0):
    import zlib

    import numpy as np

    out = dict(_drawn_inputs(seed))
    spreads = {'L0_cond_b_up': (0.0, 0.569),
     'L0_cond_b_gate': (0.0, 0.541),
     'L0_cond_b_down': (0.0, 0.1),
     'L0_ffn_gates': (0.0, 0.1),
     'L1_ffn_router_b': (0.0, 0.438),
     'L1_ffn_sb1': (0.0, 0.285),
     'L1_ffn_sb2': (0.0, 0.1),
     'L1_ffn_eb1': (0.0, 0.8),
     'L1_ffn_eb2': (0.0, 0.279),
     'L2_ffn_b1': (0.0, 0.275),
     'L2_ffn_b2': (0.0, 0.1),
     'L3_ffn_gamma1': (1.0, 0.2),
     'L3_ffn_bq': (0.0, 0.1),
     'L3_ffn_bdown': (0.0, 0.1),
     'L3_ffn_bup': (0.0, 0.1),
     'L3_ffn_bo': (0.0, 0.1),
     'L3_ffn_gamma2': (1.0, 0.2),
     'L3_ffn_bg': (0.0, 0.1)}
    factors = {'L0_cond_W_up': 2.738,
     'L0_cond_W_gate': 2.91,
     'L0_cond_W_down': 2.7,
     'L0_ffn_q_proj': 8.0,
     'L0_ffn_k_proj': 8.0}
    for name, (base, spread) in spreads.items():
        noise = np.random.default_rng([zlib.crc32(name.encode()), seed]).standard_normal(out[name].shape)
        drawn = base * np.exp(spread * noise) if base else spread * noise
        out[name] = jnp.asarray(drawn.astype(out[name].dtype))
    for name, factor in factors.items():
        out[name] = (out[name] * factor).astype(out[name].dtype)
    return out
```

```python
from contextlib import ExitStack

import numpy as np

import concourse.bass as bass
from concourse import mybir

ALU = mybir.AluOpType
ACT = mybir.ActivationFunctionType
AX = mybir.AxisListType
F32 = mybir.dt.float32
F32R = mybir.dt.float32r
U32 = mybir.dt.uint32

P = 128
BATCH, T, D = 4, 512, 256
KD = D // P
NT = T // P
PAIRS = BATCH // 2
COND = 8
H0 = 512
E0, HD0 = 16, 64
QKV = 3 * HD0
E1 = 16
TOP1 = 3
F2 = 1024
TOPK2 = T // 2
RANK2, SCALING2 = 16, 2.0
I3 = 1024
HEADS, HD3, L3LAT, E3 = 16, 16, 64, 8
HH3 = HEADS // 2
EPS3 = 1e-6
CW = 1536
RAW_SLOTS, W_SLOTS = 2, 4
PREP_COND, PREP_STEPS, DVE_STEPS = 11, 29, 193
PRIME = 2

C_L0C, C_QKV, C_O0, C_L1, C_L2C, C_L2F, C_L3C, C_L3SH, C_L3Q, C_L3KV, C_L3O, C_L3E, CHUNKS = np.cumsum(
    [0, 6, 4, 2, 16, 1, 4, 16, 4, 1, 1, 1, 4]).tolist()

WIDTHS = [1024] * 6 + [1536] * 4 + [1024] * (2 + 16 + 5) + [1536] * 20 + [512, 640, 512] + [1024] * 4


class Signal:

    def __init__(self, sem, per_pair, step=1, prime=0):
        self.sem, self.per_pair, self.step, self.prime = sem, per_pair, step, prime

    def __call__(self, it, k):
        assert k + self.prime > 0
        return self.sem, (it * self.per_pair + k + self.prime) * self.step


def build(nc, A):
    with ExitStack() as ctx:
        def sb(name, shape, dt=F32):
            return ctx.enter_context(nc.sbuf_tensor(name, shape, dt))

        def sig(name, per_pair, step=1, prime=0):
            return Signal(ctx.enter_context(nc.semaphore(name)), per_pair, step, prime)

        bank = [ctx.enter_context(nc.psum_tensor(f"bank{i}", [P, 512], F32)) for i in range(8)]

        def B(u, i):
            return bank[4 * u + i]

        U = range(2)
        xT = [sb(f"xT{u}", [P, KD, T]) for u in U]
        x_hi = [sb(f"x_hi{u}", [P, KD, T], F32R) for u in U]
        x_lo = [sb(f"x_lo{u}", [P, KD, T], F32R) for u in U]
        h_hi = [sb(f"h_hi{u}", [P, KD, T], F32R) for u in U]
        h_lo = [sb(f"h_lo{u}", [P, KD, T], F32R) for u in U]
        hid_hi = [sb(f"hid_hi{u}", [P, 4, T], F32R) for u in U]
        hid_lo = [sb(f"hid_lo{u}", [P, 4, T], F32R) for u in U]
        F = [sb(f"F{u}", [P, 2, T]) for u in U]
        acc = [sb(f"acc{u}", [P, NT, D]) for u in U]
        G = [sb(f"G{u}", [P, 4 * T]) for u in U]
        base = [sb(f"base{u}", [P, KD, T]) for u in U]
        VW = sb("VW", [P, 2, NT * HEADS * 32])
        raw = [sb(f"raw{i}", [P, CW]) for i in range(RAW_SLOTS)]
        w_hi = [sb(f"w_hi{i}", [P, CW], F32R) for i in range(W_SLOTS)]
        w_lo = [sb(f"w_lo{i}", [P, CW], F32R) for i in range(W_SLOTS)]
        mask1 = sb("mask1", [P, KD * D])
        ident = sb("ident", [P, P])
        ones = sb("ones", [P, P])
        causal = sb("causal", [P, T])
        before = sb("before", [P, 384 + T])
        vecs = sb("vecs", [P, A["vecs"].shape[1]])
        rows = sb("rows", [P, A["rows"].shape[1]])
        NS = A["small"].shape[1]
        small = base[0][:, 0, 0:NS]
        sm_hi = sb("sm_hi", [P, NS], F32R)
        sm_lo = sb("sm_lo", [P, NS], F32R)
        b2rows = sb("b2rows", [E1, D])
        def s2(name, shape, dt=F32):
            return [sb(f"{name}{u}", shape, dt) for u in U]

        lg, pe_, mk, fb, rw = (s2(n, [P, NT, 16]) for n in ("lg", "pexp", "mk", "fb", "rw"))
        m8 = s2("m8", [P, NT, 8])
        i8 = s2("i8", [P, NT, 8], U32)
        i8f = s2("i8f", [P, NT, 8])
        st = s2("st", [P, 8, NT])
        cond = sb("cond", [P, BATCH, COND])
        cond_er = sb("cond_er", [P, BATCH])
        cidx = sb("cidx", [P, BATCH, 8], U32)
        cm8, ct, cexp = m8[1], m8[0], i8f[0]
        skw = sb("skw", [P, BATCH, 2])
        pair_cond = sb("pair_cond", [P, 2, COND])
        pair_er = sb("pair_er", [P, 2])
        pair_skw = sb("pair_skw", [P, 2, 2])
        l0b = s2("l0b", [P, 10])
        simn = pe_[0][:, 0:KD, :]
        cs = mk[0][:, 0, :]
        sg = sb("sg", [P, E0])

        V, R, S = A["VEC"], A["ROW"], A["SMALL"]

        def vec(name, m):
            return vecs[:, V[name] + m:V[name] + m + 1]

        def row(name, n):
            return rows[:, R[name]:R[name] + n]

        def small_at(t, name, k, n):
            return t[:, S[name] + k * n:S[name] + (k + 1) * n]

        const_in = sig("const_in", 0)
        prep = sig("prep", 0)
        prep_pe = sig("prep_pe", 0)
        prep_act = sig("prep_act", 0)
        prep_pool = sig("prep_pool", 0)
        idx_ready = sig("idx_ready", 0)
        l0b_in = [sig(f"l0b_in{u}", 1, 16) for u in U]
        x_in = [sig(f"x_in{u}", 1, 16) for u in U]
        out_written = sig("out_written", 2, 16)
        l1w_in = sig("l1w_in", 1, 16)
        raw_in = [sig(f"raw_in{i}", CHUNKS // RAW_SLOTS, 16) for i in range(RAW_SLOTS)]
        w_hi_ready = sig("w_hi_ready", CHUNKS)
        w_ready = sig("w_ready", CHUNKS, prime=PRIME)
        w_begun = sig("w_begun", CHUNKS, prime=PRIME)
        passed = sig("passed", 0)
        dve_step = sig("dve_step", DVE_STEPS)
        act_step = sig("act_step", 8)
        x_pair = sig("x_pair", 8)
        up_ready, gate_ready, silu_done, l0_gated, hid_hi_ready, hid_ready = (
            sig(n, 8) for n in ("up_ready", "gate_ready", "silu_done", "l0_gated", "hid_hi_ready", "hid_ready"))
        l0_down, l0_h_hi, l0_sq, l0_h = (sig(n, 4) for n in ("l0_down", "l0_h_hi", "l0_sq", "l0_h"))
        l0_logits, l0_norm, l0_exp_in, l0_exp, l0_rw = (
            sig(n, 2) for n in ("l0_logits", "l0_norm", "l0_exp_in", "l0_exp", "l0_rw"))
        qkv_ready, qkv_half, qkv_done = (sig(n, 64) for n in ("qkv_ready", "qkv_half", "qkv_done"))
        qkT_ready = sig("qkT_ready", 4)
        qkT_sb = sig("qkT_sb", 4)
        s0_ready, s0_masked, s0_max, s0_p, s0_pT, s0_pT_sb, o0_ready, att0 = (
            sig(n, 8) for n in ("s0_ready", "s0_masked", "s0_max", "s0_p", "s0_pT", "s0_pT_sb", "o0_ready", "att0"))
        mixed, mixT_ready, mix_hi, mix_lo = (sig(n, 16) for n in ("mixed", "mixT_ready", "mix_hi", "mix_lo"))
        oproj0 = sig("oproj0", 4)
        wbot_ready = sig("wbot_ready", 2)
        l1c_ready, l1c_hi, l1c_h = (sig(n, 4) for n in ("l1c_ready", "l1c_hi", "l1c_h"))
        l1_logits, l1_exp_in, l1_exp, l1_cw, cwT_ready, cwT_sb, b2_ready, acc1_init = (
            sig(n, 2) for n in ("l1_logits", "l1_exp_in", "l1_exp", "l1_cw", "cwT_ready", "cwT_sb", "b2_ready",
                                "acc1_init"))
        e1_hid_ready = sig("e1_hid_ready", 2 * E1)
        e1_relu = sig("e1_relu", 4 * E1)
        e1_hi = sig("e1_hi", 2 * E1)
        e1_hid = sig("e1_hid", 2 * E1)
        e1_y_ready = sig("e1_y_ready", 4 * E1)
        e1_sum = sig("e1_sum", 8 * E1)
        accT_ready = sig("accT_ready", 8)
        hA_ready, hA_hi, hA = (sig(n, 2) for n in ("hA_ready", "hA_hi", "hA"))
        l2c_ready, l2c_hi, l2c_h, l2c_x = (sig(n, 4) for n in ("l2c_ready", "l2c_hi", "l2c_h", "l2c_x"))
        sc_ready, sc_sb, sel_ready, sig_in, sig_exp, wtok_ready, wbc_ready, wbc_sb = (
            sig(n, 2) for n in ("sc_ready", "sc_sb", "sel_ready", "sig_in", "sig_exp", "wtok_ready", "wbc_ready",
                                "wbc_sb"))
        f2_ready, f2_gelu, f2_hi, f2_hid = (sig(n, 16) for n in ("f2_ready", "f2_gelu", "f2_hi", "f2_hid"))
        f2_down = sig("f2_down", 16)
        g3_ready, u3_ready, g3_gelu, g3_gated, g3_hi, g3_hid = (
            sig(n, 48) for n in ("g3_ready", "u3_ready", "g3_gelu", "g3_gated", "g3_hi", "g3_hid"))
        d3_step = sig("d3_step", 24)
        base_ready, sq3 = (sig(n, 4) for n in ("base_ready", "sq3"))
        ss_ready, nrm3, rs3, rsbc_ready, n3_hi, n3_h = (
            sig(n, 4) for n in ("ss_ready", "nrm3", "rs3", "rsbc_ready", "n3_hi", "n3_h"))
        n3_F = sig("n3_F", 8)
        q3_ready, q3_sb = (sig(n, 4) for n in ("q3_ready", "q3_sb"))
        lat_ready, lat_hi, lat_lo = (sig(n, 2) for n in ("lat_ready", "lat_hi", "lat_lo"))
        kv3_ready, kv3_sb = (sig(n, 8) for n in ("kv3_ready", "kv3_sb"))
        prod_dve, sum_dve, prod_pool, sum_pool = (
            sig(n, 16) for n in ("prod_dve", "sum_dve", "prod_pool", "sum_pool"))
        att3_in, att3_exp, att3 = (sig(n, 2) for n in ("att3_in", "att3_exp", "att3"))
        o3T_ready, o3_hi, o3_lo = (sig(n, 4) for n in ("o3T_ready", "o3_hi", "o3_lo"))
        wo_ready, x1_ready, sq3b = (sig(n, 4) for n in ("wo_ready", "x1_ready", "sq3b"))
        l3_logits, l3_exp_in, l3_exp, l3_gate = (
            sig(n, 2) for n in ("l3_logits", "l3_exp_in", "l3_exp", "l3_gate"))
        we_ready, we_half, we_done = (sig(n, 32) for n in ("we_ready", "we_half", "we_done"))
        x_final = sig("x_final", 4)

        att = [acc[u][:, :, QKV:D] for u in U]
        cw_T = [G[u][0:E1, 0:T] for u in U]
        qT = [F[u][0:HD0, 0, :] for u in U]
        kT = [F[u][0:HD0, 1, :] for u in U]
        s_off = [0, 128, 384, 768]
        pT_sb = [[base[u][:, 0, 0:128], base[u][:, 0, 128:384], base[u][:, 1, 0:384],
                  G[u][:, 1280:1792]] for u in U]
        l1w = VW[:].rearrange("p a n -> p (a n)").rearrange("p (g n) -> p g n", g=COND)
        q3 = [acc[u][:].rearrange("p t (h d) -> p t h d", d=HD3) for u in U]
        kv3 = [VW[:, u, :].rearrange("p (t n) -> p t n", t=NT) for u in U]
        att3_p = [F[u][:].rearrange("p k n -> p (k n)").rearrange("p (t h g) -> p t h g", t=NT, h=HEADS) for u in U]
        prod3 = [G[i][:].rearrange("p (h a b) -> p h a b", h=HH3, a=16) for i in U]
        SWEEP3 = [(phase, u, t) for phase in ("scores", "values") for u in U for t in range(NT)]
        lat_p = [[hid_hi[u][0:L3LAT, 0, :], hid_hi[u][0:L3LAT, 1, :]] for u in U]
        def tok(t):
            return slice(t * P, (t + 1) * P)


        def mm3(out, sh, sl, mh, ml, first, last, begin=False):
            i = nc.tensor.matmul(out, sh, mh, start=first, stop=False)
            if begin:
                i.then_inc(w_begun.sem, 1)
            nc.tensor.matmul(out, sh, ml, start=False, stop=False)
            return nc.tensor.matmul(out, sl, mh, start=False, stop=last)

        steps = [(j, c, u) for j in range(3) for c in range(4) for u in U]
        PB = [(B(0, 0), B(0, 1)), (B(1, 0), B(1, 1))]

        def product3(eng, dst, half, phase, u, t):
            hs, shape = slice(HH3 * half, HH3 * half + HH3), [P, HH3, 16, 16]
            if phase == "scores":
                a = q3[u][:, t, hs, :].unsqueeze(2).broadcast_to(shape)
                b = kv3[u][:, t, 0:D].rearrange("p (g d) -> p g d", d=HD3).unsqueeze(1).broadcast_to(shape)
            else:
                a = att3_p[u][:, t, hs, :].unsqueeze(2).broadcast_to(shape)
                b = kv3[u][:, t, D:2 * D].rearrange("p (g d) -> p d g", d=HD3).unsqueeze(1).broadcast_to(shape)
            return eng.tensor_tensor(dst, a, b, ALU.mult)

        block = ctx.enter_context(nc.Block())

        @block.sync
        def _(sp):
            for dst, name in ((cond[:].rearrange("p b g -> p (b g)"), "cond"), (cond_er[:], "cond_er"),
                              (ident[:], "ident"), (vecs[:], "vecs"), (rows[:], "rows"), (small, "small"),
                              (b2rows[:], "b2rows"), (causal[:], "causal"),
                              (before[:], "before"), (mask1[:], "mask1")):
                sp.dma_start(dst, A[name]).then_inc(const_in.sem, 16)
            sp.wait_ge(idx_ready.sem, 1)
            with sp.Fori(0, PAIRS) as it:
                def store_x(u):
                    sp.dma_start(A["out"][2 * it + u], xT[u][:]).then_inc(out_written.sem, 16)

                for u in U:
                    sp.dma_start(xT[u][:], A["x"][2 * it + u]).then_inc(x_in[u].sem, 16)

                def chunk(c, src, n):
                    sp.wait_ge(*w_ready(it, c + 1 - RAW_SLOTS))
                    sp.dma_start(raw[c % 2][:, 0:n], src).then_inc(raw_in[c % 2].sem, 16)

                top1 = [sp.value_load(cidx[0:1, bass.ds(2 * it + u, 1), 0:1], min_val=0, max_val=COND - 1)
                        for u in U]
                for u in U:
                    sp.dma_start(l0b[u][:], A["l0b"][bass.ds(top1[u], 1)]).then_inc(l0b_in[u].sem, 16)
                for c in range(3):
                    for u in U:
                        chunk(C_L0C + 2 * c + u, A["l0c"][bass.ds(top1[u], 1), c], 1024)
                for c in range(4):
                    chunk(C_QKV + c, A["qkv"][c], 1536)
                sp.dma_start(VW[:].rearrange("p a n -> p (a n)"), A["l1w"]).then_inc(l1w_in.sem, 16)
                for c in range(2):
                    chunk(C_O0 + c, A["o0"][c], 1024)
                for e in range(E1):
                    chunk(C_L1 + e, A["l1"][e], 1024)
                for c in range(5):
                    chunk(C_L2C + c, A["l2"][c], 1024)
                for j in range(2):
                    top = [sp.value_load(cidx[0:1, bass.ds(2 * it + u, 1), j:j + 1], min_val=0, max_val=COND - 1)
                           for u in U]
                    for c in range(4):
                        for u in U:
                            chunk(C_L3C + 8 * j + 2 * c + u, A["skill"][bass.ds(top[u], 1), c], 1536)
                for c in range(4):
                    chunk(C_L3SH + c, A["shared"][c], 1536)
                chunk(C_L3Q, A["l3q"], 512)
                chunk(C_L3KV, A["l3kv"], 640)
                chunk(C_L3O, A["l3o"], 512)
                for c in range(4):
                    chunk(C_L3E + c, A["l3e"][c], 1024)
                for u in U:
                    sp.wait_ge(*x_final(it, 2 * u + 2))
                    store_x(u)
                sp.wait_ge(*out_written(it, 2))
                sp.sem_inc(passed.sem, 1)

        @block.gpsimd
        def _(pool):
            pool.wait_ge(const_in.sem, 16 * 10)
            pool.sem_inc(w_ready.sem, PRIME)
            pool.tensor_copy(sm_hi[:], small).then_inc(prep_pool.sem, 1)
            pool.wait_ge(prep_pool.sem, 1)
            pool.tensor_tensor(sm_lo[:], small, sm_hi[:].bitcast(F32), ALU.subtract).then_inc(prep_pool.sem, 1)
            with pool.Fori(0, PAIRS) as it:
                def split(c, n):
                    pool.wait_ge(*raw_in[c % 2](it, c // 2 + 1))
                    pool.wait_ge(*w_begun(it, c - 1))
                    pool.sem_inc(passed.sem, 1)
                    s = c % W_SLOTS
                    nc.gpsimd.tensor_copy(w_hi[s][:, 0:n], raw[c % 2][:, 0:n]).then_inc(w_hi_ready.sem, 1)
                    pool.wait_ge(*w_hi_ready(it, c + 1))
                    nc.gpsimd.tensor_tensor(w_lo[s][:, 0:n], raw[c % 2][:, 0:n], w_hi[s][:, 0:n].bitcast(F32),
                                            ALU.subtract).then_inc(w_ready.sem, 1)

                for c in range(CHUNKS):
                    split(c, A["widths"][c])
                    if c == C_L3E:
                        for n, (phase, u, t) in enumerate(SWEEP3):
                            if phase == "scores":
                                if t == 0:
                                    pool.wait_ge(*q3_sb(it, 2 * u + 2))
                                pool.wait_ge(*kv3_sb(it, 4 * u + t + 1))
                            elif t == 0:
                                pool.wait_ge(*att3(it, u + 1))
                            if n >= 1:
                                pool.wait_ge(*sum_pool(it, n))
                            else:
                                pool.wait_ge(*w_ready(it, c + 1))
                            product3(nc.gpsimd, prod3[1], 1, phase, u, t).then_inc(prod_pool.sem, 1)
                        pool.wait_ge(*prod_pool(it, len(SWEEP3)))
                        pool.sem_inc(passed.sem, 1)

        @block.tensor
        def _(pe):
            pe.wait_ge(const_in.sem, 16 * 10)
            pe.sem_inc(w_begun.sem, PRIME)
            pe.wait_ge(prep.sem, 2)
            for k in range(KD):
                mm = nc.tensor.matmul(bank[0][:, 0:E0], ones[:], simn[:, k, :], start=k == 0, stop=k == KD - 1)
            mm.then_inc(prep_pe.sem, 1)
            pe.wait_ge(prep.sem, PREP_STEPS)
            with pe.Fori(0, PAIRS) as it:
                def weights(c):
                    pe.wait_ge(*w_ready(it, c + 1))
                    return w_hi[c % W_SLOTS], w_lo[c % W_SLOTS]

                for cc in range(2):
                    for u in U:
                        if cc == 0:
                            pe.wait_ge(*x_pair(it, u + 1))
                        c = C_L0C + 2 * cc + u
                        wh, wl = weights(c)
                        for ml in range(2):
                            if cc == 1:
                                pe.wait_ge(*l0_gated(it, 2 * u + ml + 1))
                            for j, ready in ((0, up_ready), (1, gate_ready)):
                                for k in range(KD):
                                    cols = slice(512 * j + 256 * k + P * ml, 512 * j + 256 * k + P * ml + P)
                                    mm = mm3(B(u, 2 * ml + j)[:], wh[:, cols], wl[:, cols],
                                             x_hi[u][:, k, :], x_lo[u][:, k, :], k == 0, k == KD - 1,
                                             begin=ml == 0 and j == 0 and k == 0)
                                mm.then_inc(ready.sem, 1)
                for u in U:
                    wh, wl = weights(C_L0C + 4 + u)
                    pe.wait_ge(*hid_ready(it, 4 + 2 * u + 2))
                    for m in range(KD):
                        for k in range(4):
                            cols = slice(D * k + P * m, D * k + P * m + P)
                            mm = mm3(B(u, m)[:], wh[:, cols], wl[:, cols], hid_hi[u][:, k, :], hid_lo[u][:, k, :],
                                     k == 0, k == 3, begin=m == 0 and k == 0)
                        mm.then_inc(l0_down.sem, 1)
                for u in U:
                    pe.wait_ge(*l0_h(it, 2 * u + 2))
                    for t in range(NT):
                        for k in range(KD):
                            mm3(B(u, 2)[:, 16 * t:16 * t + 16], h_hi[u][:, k, tok(t)], h_lo[u][:, k, tok(t)],
                                small_at(sm_hi, "sim", k, E0), small_at(sm_lo, "sim", k, E0), k == 0, k == KD - 1)
                    for t in range(NT):
                        for k in range(KD):
                            mm = nc.tensor.matmul(B(u, 2)[:, 64 + t:65 + t], F[u][:, k, tok(t)], ones[:, 0:1],
                                                  start=k == 0, stop=k == KD - 1)
                    mm.then_inc(l0_logits.sem, 1)
                for g in range(8):
                    wh, wl = weights(C_QKV + g // 2)
                    for u in U:
                        for t in range(NT):
                            if g > 0:
                                pe.wait_ge(*qkv_done(it, 8 * (g - 1) + 4 * u + t + 1))
                            elif t == 2:
                                pe.wait_ge(*l0_rw(it, u + 1))
                            for k in range(KD):
                                cols = slice(768 * k + 384 * (g % 2), 768 * k + 384 * (g % 2) + 384)
                                mm = mm3(B(u, t)[:, 0:384], h_hi[u][:, k, tok(t)], h_lo[u][:, k, tok(t)],
                                         wh[:, cols], wl[:, cols], k == 0, k == KD - 1,
                                         begin=g % 2 == 0 and u == 0 and t == 0 and k == 0)
                            mm.then_inc(qkv_ready.sem, 1)
                for u in U:
                    pe.wait_ge(*qkv_done(it, 56 + 4 * u + 4))
                    pe.sem_inc(passed.sem, 1)
                    for j in range(2):
                        for t in range(NT):
                            mm = nc.tensor.transpose(B(u, j)[0:HD0, tok(t)], acc[u][:, t, HD0 * j:HD0 * (j + 1)],
                                                     ident[:])
                        mm.then_inc(qkT_ready.sem, 1)
                for u in U:
                    pe.wait_ge(*qkT_sb(it, 2 * u + 2))
                    for i in range(NT):
                        n = P * (i + 1)
                        nc.tensor.matmul(B(u, (i + 2) % 4)[:, 0:n], qT[u][:, tok(i)], kT[u][:, 0:n],
                                         start=True, stop=True).then_inc(s0_ready.sem, 1)
                for u in U:
                    for i in range(NT):
                        pe.wait_ge(*s0_p(it, 4 * u + i + 1))
                        for j in range(i + 1):
                            o = s_off[i] + P * j
                            mm = nc.tensor.transpose(B(u, (i + 2) % 4)[:, tok(j)], G[u][:, o:o + P], ident[:])
                        mm.then_inc(s0_pT.sem, 1)
                for u in U:
                    for i in range(NT):
                        pe.wait_ge(*s0_pT_sb(it, 4 * u + i + 1))
                        for j in range(i + 1):
                            mm = nc.tensor.matmul(B(u, (i + 2) % 4)[:, 0:HD0], pT_sb[u][i][:, tok(j)],
                                                  acc[u][:, j, 2 * HD0:3 * HD0], start=j == 0, stop=j == i)
                        mm.then_inc(o0_ready.sem, 1)
                for r in range(2):
                    wh, wl = weights(C_O0 + r)
                    for u in U:
                        for k in range(4):
                            pe.wait_ge(*mixed(it, 8 * r + 4 * u + 4))
                            if k == 0 and r == 0:
                                pe.wait_ge(*att0(it, 4 * u + 4))
                            elif k >= 2:
                                pe.wait_ge(*mix_lo(it, 8 * r + 4 * u + k - 1))
                            elif r == 1:
                                pe.wait_ge(*mix_lo(it, 4 * u + k + 3))
                            for t in range(NT):
                                mm = nc.tensor.transpose(B(u, k % 2)[:, tok(t)],
                                                         G[u][:, 512 * t + P * k:512 * t + P * (k + 1)], ident[:])
                            mm.then_inc(mixT_ready.sem, 1)
                    for u in U:
                        pe.wait_ge(*mix_lo(it, 8 * r + 4 * u + 4))
                        for m in range(KD):
                            for k in range(4):
                                cols = slice(D * k + P * m, D * k + P * m + P)
                                mm = mm3(B(u, 2 + m)[:], wh[:, cols], wl[:, cols], hid_hi[u][:, k, :],
                                         hid_lo[u][:, k, :], r == 0 and k == 0, r == 1 and k == 3,
                                         begin=u == 0 and m == 0 and k == 0)
                        mm.then_inc(oproj0.sem, 1)
                for u in U:
                    pe.wait_ge(*wbot_ready(it, u + 1))
                    pe.wait_ge(*x_pair(it, 2 + u + 1))
                    for m in range(KD):
                        for k in range(KD):
                            cols = slice(D * k + P * m, D * k + P * m + P)
                            mm = mm3(B(u, m)[:], hid_hi[u][:, 0, cols], hid_lo[u][:, 0, cols], x_hi[u][:, k, :],
                                     x_lo[u][:, k, :], k == 0, k == KD - 1)
                        mm.then_inc(l1c_ready.sem, 1)
                for u in U:
                    pe.wait_ge(*l1c_h(it, 2 * u + 2))
                    for t in range(NT):
                        for k in range(KD):
                            mm = mm3(B(u, 2)[:, 16 * t:16 * t + 16], h_hi[u][:, k, tok(t)], h_lo[u][:, k, tok(t)],
                                     small_at(sm_hi, "router", k, E1), small_at(sm_lo, "router", k, E1),
                                     k == 0, k == KD - 1)
                    mm.then_inc(l1_logits.sem, 1)

                def l1_hidden(e, u):
                    wh, wl = weights(C_L1 + e)
                    if e > 0:
                        pe.wait_ge(*e1_relu(it, 4 * (e - 1) + 2 * u + 2))
                    for m in range(KD):
                        for k in range(KD):
                            cols = slice(D * k + P * m, D * k + P * m + P)
                            mm = mm3(B(u, m)[:], wh[:, cols], wl[:, cols], h_hi[u][:, k, :], h_lo[u][:, k, :],
                                     k == 0, k == KD - 1, begin=u == 0 and m == 0 and k == 0)
                    mm.then_inc(e1_hid_ready.sem, 1)

                def l1_out(e, u):
                    wh, wl = weights(C_L1 + e)
                    pe.wait_ge(*e1_hid(it, 2 * e + u + 1))
                    for tp in range(2):
                        if e > 0:
                            pe.wait_ge(*e1_sum(it, 8 * (e - 1) + 4 * u + 2 * tp + 2))
                        for t in (2 * tp, 2 * tp + 1):
                            for k in range(KD):
                                cols = slice(512 + D * k, 512 + D * k + D)
                                mm = mm3(B(u, 2 + tp)[:, D * (t % 2):D * (t % 2) + D],
                                         hid_hi[u][:, 2 * (e % 2) + k, tok(t)], hid_lo[u][:, 2 * (e % 2) + k, tok(t)],
                                         wh[:, cols], wl[:, cols], k == 0, k == KD - 1)
                        mm.then_inc(e1_y_ready.sem, 1)

                for u in U:
                    l1_hidden(0, u)
                for u in U:
                    pe.wait_ge(*l1_cw(it, u + 1))
                    for t in range(NT):
                        mm = nc.tensor.transpose(B(u, 2)[0:E1, tok(t)], rw[u][:, t, :], ident[:])
                    mm.then_inc(cwT_ready.sem, 1)
                for u in U:
                    pe.wait_ge(*cwT_sb(it, u + 1))
                    for t in range(NT):
                        mm = nc.tensor.matmul(B(u, 2 + t // 2)[:, D * (t % 2):D * (t % 2) + D], cw_T[u][:, tok(t)],
                                              b2rows[:], start=True, stop=True)
                    mm.then_inc(b2_ready.sem, 1)
                for u in U:
                    pe.wait_ge(*acc1_init(it, u + 1))
                for e in range(E1):
                    for u in U:
                        if e + 1 < E1:
                            l1_hidden(e + 1, u)
                        l1_out(e, u)
                for u in U:
                    pe.wait_ge(*e1_sum(it, 8 * (E1 - 1) + 4 * u + 4))
                    for m in range(KD):
                        for t in range(NT):
                            mm = nc.tensor.transpose(B(u, m)[:, tok(t)], acc[u][:, t, P * m:P * m + P], ident[:])
                        mm.then_inc(accT_ready.sem, 1)
                wh, wl = weights(C_L2C)
                for u in U:
                    pe.wait_ge(*x_pair(it, 4 + u + 1))
                    for k in range(KD):
                        cols = slice(512 + P * k, 512 + P * k + P)
                        mm = mm3(B(u, 2)[:], wh[:, cols], wl[:, cols], x_hi[u][:, k, :], x_lo[u][:, k, :], k == 0,
                                 k == KD - 1, begin=u == 0 and k == 0)
                    mm.then_inc(hA_ready.sem, 1)
                    for m in range(KD):
                        for k in range(KD):
                            cols = slice(D * k + P * m, D * k + P * m + P)
                            mm3(B(u, m)[:], wh[:, cols], wl[:, cols], x_hi[u][:, k, :], x_lo[u][:, k, :], k == 0,
                                False)
                for u in U:
                    pe.wait_ge(*hA(it, u + 1))
                    for m in range(KD):
                        cols = slice(768 + P * m, 768 + P * m + P)
                        mm3(B(u, m)[:], wh[:, cols], wl[:, cols], hid_hi[u][:, 0, :], hid_lo[u][:, 0, :], False,
                            True).then_inc(l2c_ready.sem, 1)
                for u in U:
                    pe.wait_ge(*l2c_h(it, 2 * u + 2))
                    for k in range(KD):
                        mm = mm3(B(u, 2)[:], small_at(sm_hi, "wr", k, P), small_at(sm_lo, "wr", k, P),
                                 h_hi[u][:, k, :], h_lo[u][:, k, :], k == 0, k == KD - 1)
                    mm.then_inc(sc_ready.sem, 1)
                def l2_down(m, u):
                    wh, wl = weights(C_L2F + m // 2)
                    pe.wait_ge(*f2_hid(it, 2 * m + u + 1))
                    if m == 0:
                        pe.wait_ge(*sc_sb(it, u + 1))
                    for n in range(KD):
                        cols = slice(512 + D * (m % 2) + P * n, 512 + D * (m % 2) + P * n + P)
                        mm = mm3(B(u, 2 + n)[:], wh[:, cols], wl[:, cols], hid_hi[u][:, m % 4, :],
                                 hid_lo[u][:, m % 4, :], m == 0, m == 7)
                    mm.then_inc(f2_down.sem, 1)

                for m in range(8):
                    for u in U:
                        wh, wl = weights(C_L2F + m // 2)
                        if m >= 2:
                            pe.wait_ge(*f2_gelu(it, 2 * (m - 2) + u + 1))
                        else:
                            pe.wait_ge(*l2c_x(it, 2 * u + m + 1))
                        for k in range(KD):
                            cols = slice(D * k + P * (m % 2), D * k + P * (m % 2) + P)
                            mm = mm3(B(u, m % 2)[:], wh[:, cols], wl[:, cols], h_hi[u][:, k, :], h_lo[u][:, k, :],
                                     k == 0, k == KD - 1, begin=m % 2 == 0 and u == 0 and k == 0)
                        mm.then_inc(f2_ready.sem, 1)
                        if m >= 1:
                            l2_down(m - 1, u)
                for u in U:
                    l2_down(7, u)
                for u in U:
                    pe.wait_ge(*wtok_ready(it, u + 1))
                    for t in range(NT):
                        mm = nc.tensor.matmul(B(u, 0)[:, tok(t)], st[u][:, 5, t:t + 1].broadcast_to([P, P]),
                                              ident[:], start=True, stop=True)
                    mm.then_inc(wbc_ready.sem, 1)

                def l3_chunk(j, c, u):
                    return C_L3C + 8 * j + 2 * c + u if j < 2 else C_L3SH + c

                def l3_up(n, ml):
                    j, c, u = steps[n]
                    wh, wl = weights(l3_chunk(j, c, u))
                    i = 2 * n + ml
                    if i >= 2:
                        pe.wait_ge(*g3_gated(it, i - 1))
                    for kind, ready in ((0, g3_ready), (1, u3_ready)):
                        for k in range(KD):
                            cols = slice(512 * kind + D * k + P * ml, 512 * kind + D * k + P * ml + P)
                            mm = mm3(PB[ml][kind][:], wh[:, cols], wl[:, cols], x_hi[u][:, k, :], x_lo[u][:, k, :],
                                     k == 0, k == KD - 1,
                                     begin=ml == 0 and kind == 0 and k == 0 and (j < 2 or u == 0))
                        mm.then_inc(ready.sem, 1)

                def l3_down(n, ml):
                    j, c, u = steps[n]
                    wh, wl = weights(l3_chunk(j, c, u))
                    pe.wait_ge(*g3_hid(it, 2 * n + ml + 1))
                    for m in range(KD):
                        cols = slice(1024 + D * ml + P * m, 1024 + D * ml + P * m + P)
                        mm = mm3(B(u, 2 + m)[:], wh[:, cols], wl[:, cols], hid_hi[u][:, 2 * (c % 2) + ml, :],
                                 hid_lo[u][:, 2 * (c % 2) + ml, :], j == 0 and c == 0 and ml == 0,
                                 j == 2 and c == 3 and ml == 1)
                    if ml == 1:
                        mm.then_inc(d3_step.sem, 1)

                for u in U:
                    pe.wait_ge(*x_pair(it, 6 + u + 1))
                for n in range(len(steps) + 1):
                    for ml in range(2):
                        if n < len(steps):
                            l3_up(n, ml)
                        if n >= 1:
                            l3_down(n - 1, ml)

                def norm_stats(i, u):
                    for t in range(NT):
                        for k in range(KD):
                            mm = nc.tensor.matmul(B(u, 0)[:, t:t + 1], F[u][:, k, tok(t)], ones[:, 0:1],
                                                  start=k == 0, stop=k == KD - 1)
                    mm.then_inc(ss_ready.sem, 1)

                def norm_row(i, u):
                    pe.wait_ge(*rs3(it, 2 * i + u + 1))
                    for t in range(NT):
                        mm = nc.tensor.matmul(B(u, 1)[:, tok(t)], st[u][:, 2, t:t + 1].broadcast_to([P, P]),
                                              ident[:], start=True, stop=True)
                    mm.then_inc(rsbc_ready.sem, 1)

                for u in U:
                    pe.wait_ge(*sq3(it, 2 * u + 2))
                    norm_stats(0, u)
                for u in U:
                    norm_row(0, u)
                wh, wl = weights(C_L3Q)
                for u in U:
                    pe.wait_ge(*n3_h(it, u + 1))
                    for t in range(NT):
                        for k in range(KD):
                            mm = mm3(B(u, 2 + t // 2)[:, D * (t % 2):D * (t % 2) + D], h_hi[u][:, k, tok(t)],
                                     h_lo[u][:, k, tok(t)], wh[:, D * k:D * k + D], wl[:, D * k:D * k + D],
                                     k == 0, k == KD - 1, begin=u == 0 and t == 0 and k == 0)
                        if t % 2:
                            mm.then_inc(q3_ready.sem, 1)
                wh, wl = weights(C_L3KV)
                for u in U:
                    for k in range(KD):
                        cols = slice(L3LAT * k, L3LAT * k + L3LAT)
                        i = nc.tensor.matmul(B(u, 0)[0:L3LAT, :], w_hi[C_L3KV % 4][:, cols], h_hi[u][:, k, :],
                                             start=k == 0, stop=False)
                        if u == 0 and k == 0:
                            i.then_inc(w_begun.sem, 1)
                        nc.tensor.matmul(B(u, 0)[0:L3LAT, :], w_hi[C_L3KV % 4][:, cols], h_lo[u][:, k, :],
                                         start=False, stop=False)
                        mm = nc.tensor.matmul(B(u, 0)[0:L3LAT, :], w_lo[C_L3KV % 4][:, cols], h_hi[u][:, k, :],
                                              start=False, stop=k == KD - 1)
                    mm.then_inc(lat_ready.sem, 1)
                for u in U:
                    lh, ll = lat_p[u]
                    pe.wait_ge(*lat_lo(it, u + 1))
                    pe.wait_ge(*n3_h(it, u + 1))
                    for t in range(NT):
                        if t >= 2:
                            pe.wait_ge(*q3_sb(it, 2 * u + t - 1))
                        mm3(B(u, t)[:], lh[:, tok(t)], ll[:, tok(t)], wh[0:L3LAT, 128:128 + 2 * D],
                            wl[0:L3LAT, 128:128 + 2 * D], True, True).then_inc(kv3_ready.sem, 1)
                for u in U:
                    pe.wait_ge(*sum_pool(it, 8 + 4 * u + 4))
                    pe.wait_ge(*sum_dve(it, 8 + 4 * u + 4))
                    pe.wait_ge(*kv3_sb(it, 4 * u + 4))
                    pe.sem_inc(passed.sem, 1)
                    for m in range(KD):
                        for t in range(NT):
                            mm = nc.tensor.transpose(B(u, m)[:, tok(t)], acc[u][:, t, P * m:P * m + P], ident[:])
                        mm.then_inc(o3T_ready.sem, 1)
                wh, wl = weights(C_L3O)
                for u in U:
                    pe.wait_ge(*o3_lo(it, 2 * u + 2))
                    for m in range(KD):
                        for k in range(KD):
                            cols = slice(D * k + P * m, D * k + P * m + P)
                            mm = mm3(B(u, 2 + m)[:], wh[:, cols], wl[:, cols], x_hi[u][:, k, :], x_lo[u][:, k, :],
                                     k == 0, k == KD - 1, begin=u == 0 and m == 0 and k == 0)
                        mm.then_inc(wo_ready.sem, 1)
                for u in U:
                    pe.wait_ge(*sq3b(it, 2 * u + 2))
                    norm_stats(1, u)
                for u in U:
                    norm_row(1, u)
                for u in U:
                    pe.wait_ge(*n3_h(it, 2 + u + 1))
                    for t in range(NT):
                        for k in range(KD):
                            mm = mm3(B(u, 0)[:, E3 * t:E3 * t + E3], h_hi[u][:, k, tok(t)], h_lo[u][:, k, tok(t)],
                                     small_at(sm_hi, "wg", k, E3), small_at(sm_lo, "wg", k, E3), k == 0,
                                     k == KD - 1)
                    mm.then_inc(l3_logits.sem, 1)
                for c in range(4):
                    wh, wl = weights(C_L3E + c)
                    for u in U:
                        for t in range(NT):
                            if c > 0:
                                pe.wait_ge(*we_done(it, 8 * (c - 1) + 4 * u + t + 1))
                            elif t == 0:
                                pe.wait_ge(*l3_gate(it, u + 1))
                            for k in range(KD):
                                mm = mm3(B(u, t)[:], h_hi[u][:, k, tok(t)], h_lo[u][:, k, tok(t)],
                                         wh[:, 512 * k:512 * k + 512], wl[:, 512 * k:512 * k + 512], k == 0,
                                         k == KD - 1, begin=u == 0 and t == 0 and k == 0)
                            mm.then_inc(we_ready.sem, 1)
                for u in U:
                    pe.wait_ge(*we_done(it, 24 + 4 * u + 4))
                    for m in range(KD):
                        for t in range(NT):
                            mm = nc.tensor.transpose(B(u, m)[:, tok(t)], acc[u][:, t, P * m:P * m + P], ident[:])
                        mm.then_inc(accT_ready.sem, 1)

        @block.scalar
        def _(act):
            act.wait_ge(const_in.sem, 16 * 10)
            act.wait_ge(prep.sem, PREP_COND)
            nc.scalar.activation(cexp[:], cexp[:], ACT.Exp).then_inc(prep_act.sem, 1)
            nc.scalar.activation(sg[:], row("gates", E0), ACT.Exp, scale=-1.0).then_inc(prep_act.sem, 1)
            act.wait_ge(prep_pe.sem, 1)
            nc.scalar.activation(cs, bank[0][:, 0:E0], ACT.Sqrt).then_inc(prep_act.sem, 1)
            with act.Fori(0, PAIRS) as it:
                for u in U:
                    act.wait_ge(*l0b_in[u](it, 1))
                for cc in range(2):
                    for u in U:
                        for ml in range(2):
                            m = 2 * cc + ml
                            act.wait_ge(*up_ready(it, 4 * cc + 2 * u + ml + 1))
                            if cc == 1:
                                act.wait_ge(*l0_gated(it, 2 * u + ml + 1))
                            nc.scalar.activation(acc[u][:, 2 * ml:2 * ml + 2, :].rearrange("p a n -> p (a n)"),
                                                 B(u, 2 * ml)[:], ACT.Silu,
                                                 bias=l0b[u][:, m:m + 1]).then_inc(silu_done.sem, 1)
                for u in U:
                    for m in range(KD):
                        act.wait_ge(*l0_down(it, 2 * u + m + 1))
                        nc.scalar.activation(h_hi[u][:, m, :], B(u, m)[:], ACT.Identity,
                                             bias=l0b[u][:, 8 + m:9 + m]).then_inc(l0_h_hi.sem, 1)
                        nc.scalar.activation(F[u][:, m, :], B(u, m)[:], ACT.Square,
                                             bias=l0b[u][:, 8 + m:9 + m]).then_inc(l0_sq.sem, 1)
                for u in U:
                    act.wait_ge(*l0_logits(it, u + 1))
                    nc.scalar.activation(st[u][:, 0, :], B(u, 2)[:, 64:68], ACT.Sqrt).then_inc(l0_norm.sem, 1)
                for u in U:
                    act.wait_ge(*l0_exp_in(it, u + 1))
                    nc.scalar.activation(pe_[u][:], lg[u][:], ACT.Exp).then_inc(l0_exp.sem, 1)
                for u in U:
                    for j, dst in ((0, qT[u]), (1, kT[u])):
                        act.wait_ge(*qkT_ready(it, 2 * u + j + 1))
                        nc.scalar.activation(dst, B(u, j)[0:HD0, :], ACT.Copy).then_inc(qkT_sb.sem, 1)
                for u in U:
                    for i in range(NT):
                        act.wait_ge(*s0_max(it, 4 * u + i + 1))
                        row_i = G[u][:, s_off[i]:s_off[i] + P * (i + 1)]
                        nc.scalar.activation(row_i, row_i, ACT.Exp, bias=st[u][:, 1, i:i + 1],
                                             accum_out=st[u][:, 2, i:i + 1]).then_inc(s0_p.sem, 1)
                for u in U:
                    for i in range(NT):
                        act.wait_ge(*s0_pT(it, 4 * u + i + 1))
                        nc.scalar.activation(pT_sb[u][i], B(u, (i + 2) % 4)[:, 0:P * (i + 1)],
                                             ACT.Copy).then_inc(s0_pT_sb.sem, 1)
                for r in range(2):
                    for u in U:
                        if r == 1:
                            act.wait_ge(*oproj0(it, u + 1))
                        for k in range(4):
                            act.wait_ge(*mixT_ready(it, 8 * r + 4 * u + k + 1))
                            nc.scalar.activation(hid_hi[u][:, k, :], B(u, k % 2)[:],
                                                 ACT.Copy).then_inc(mix_hi.sem, 1)
                for u in U:
                    for m in range(KD):
                        act.wait_ge(*l1c_ready(it, 2 * u + m + 1))
                        nc.scalar.activation(h_hi[u][:, m, :], B(u, m)[:], ACT.Identity,
                                             bias=vec("l1b", m)).then_inc(l1c_hi.sem, 1)
                for u in U:
                    act.wait_ge(*l1_exp_in(it, u + 1))
                    nc.scalar.activation(pe_[u][:, :, 1:E1], lg[u][:, :, 1:E1], ACT.Exp).then_inc(l1_exp.sem, 1)

                def l1_relu(e, u):
                    act.wait_ge(*e1_hid_ready(it, 2 * e + u + 1))
                    if e > 0:
                        act.wait_ge(*e1_hid(it, 2 * (e - 1) + u + 1))
                    for m in range(KD):
                        nc.scalar.activation(F[u][:, m, :], B(u, m)[:], ACT.Relu,
                                             bias=vec("eb1", KD * e + m)).then_inc(e1_relu.sem, 1)
                    act.wait_ge(*e1_relu(it, 4 * e + 2 * u + 2))
                    if e > 1:
                        act.wait_ge(*e1_y_ready(it, 4 * (e - 2) + 2 * u + 2))
                    nc.scalar.activation(hid_hi[u][:, 2 * (e % 2):2 * (e % 2) + 2, :], F[u][:],
                                         ACT.Copy).then_inc(e1_hi.sem, 1)

                for u in U:
                    l1_relu(0, u)
                for u in U:
                    act.wait_ge(*cwT_ready(it, u + 1))
                    nc.scalar.activation(cw_T[u], B(u, 2)[0:E1, :], ACT.Copy).then_inc(cwT_sb.sem, 1)
                for u in U:
                    act.wait_ge(*b2_ready(it, u + 1))
                    nc.scalar.activation(acc[u][:, 0:2, :].rearrange("p a n -> p (a n)"), B(u, 2)[:], ACT.Copy)
                    nc.scalar.activation(acc[u][:, 2:4, :].rearrange("p a n -> p (a n)"), B(u, 3)[:],
                                         ACT.Copy).then_inc(acc1_init.sem, 1)
                for e in range(1, E1):
                    for u in U:
                        l1_relu(e, u)
                for u in U:
                    act.wait_ge(*hA_ready(it, u + 1))
                    nc.scalar.activation(hid_hi[u][:, 0, :], B(u, 2)[:], ACT.Identity,
                                         scale=pair_er[:, u:u + 1]).then_inc(hA_hi.sem, 1)
                for u in U:
                    for m in range(KD):
                        act.wait_ge(*l2c_ready(it, 2 * u + m + 1))
                        nc.scalar.activation(h_hi[u][:, m, :], B(u, m)[:], ACT.Identity,
                                             bias=vec("l2b", m)).then_inc(l2c_hi.sem, 1)
                for u in U:
                    act.wait_ge(*sc_ready(it, u + 1))
                    nc.scalar.activation(G[u][:, 0:T], B(u, 2)[:], ACT.Copy).then_inc(sc_sb.sem, 1)
                for m in range(8):
                    for u in U:
                        act.wait_ge(*f2_ready(it, 2 * m + u + 1))
                        if m >= 2:
                            act.wait_ge(*f2_hid(it, 2 * (m - 2) + u + 1))
                        nc.scalar.activation(F[u][:, m % 2, :], B(u, m % 2)[:], ACT.Gelu_apprx_tanh,
                                             bias=vec("b1", m)).then_inc(f2_gelu.sem, 1)
                for u in U:
                    act.wait_ge(*sig_in(it, u + 1))
                    nc.scalar.activation(st[u][:, 6, :], st[u][:, 3, :], ACT.Exp,
                                         scale=-1.0).then_inc(sig_exp.sem, 1)
                for u in U:
                    act.wait_ge(*wbc_ready(it, u + 1))
                    nc.scalar.activation(G[u][:, T:2 * T], B(u, 0)[:], ACT.Copy).then_inc(wbc_sb.sem, 1)
                for i in range(48):
                    act.wait_ge(*g3_ready(it, i + 1))
                    if i >= 2:
                        act.wait_ge(*g3_gated(it, i - 1))
                    nc.scalar.activation(G[i % 2][:, 0:T], PB[i % 2][0][:],
                                         ACT.Gelu_apprx_tanh).then_inc(g3_gelu.sem, 1)
                act.wait_ge(*g3_hid(it, 48))
                for u in U:
                    act.wait_ge(*d3_step(it, 23 + u))
                    for m in range(KD):
                        nc.scalar.activation(base[u][:, m, :], B(u, 2 + m)[:], ACT.Copy).then_inc(base_ready.sem, 1)
                        nc.scalar.activation(F[u][:, m, :], B(u, 2 + m)[:], ACT.Square).then_inc(sq3.sem, 1)

                def norm_root(i):
                    for u in U:
                        act.wait_ge(*ss_ready(it, 2 * i + u + 1))
                        nc.scalar.activation(st[u][:, 1, :], B(u, 0)[:, 0:NT], ACT.Sqrt, scale=1.0 / D,
                                             bias=vec("eps", 0)).then_inc(nrm3.sem, 1)

                norm_root(0)
                for u in U:
                    act.wait_ge(*lat_ready(it, u + 1))
                    nc.scalar.activation(lat_p[u][0], B(u, 0)[0:L3LAT, :], ACT.Identity,
                                         bias=vec("bdown", 0)[0:L3LAT]).then_inc(lat_hi.sem, 1)
                for u in U:
                    act.wait_ge(*att3_in(it, u + 1))
                    nc.scalar.activation(att3_p[u], att3_p[u], ACT.Exp,
                                         scale=float(HD3) ** -0.5).then_inc(att3_exp.sem, 1)
                for u in U:
                    for m in range(KD):
                        act.wait_ge(*o3T_ready(it, 2 * u + m + 1))
                        nc.scalar.activation(x_hi[u][:, m, :], B(u, m)[:], ACT.Copy).then_inc(o3_hi.sem, 1)
                for u in U:
                    for m in range(KD):
                        act.wait_ge(*x1_ready(it, 2 * u + m + 1))
                        nc.scalar.activation(F[u][:, m, :], base[u][:, m, :], ACT.Square).then_inc(sq3b.sem, 1)
                norm_root(1)
                for u in U:
                    act.wait_ge(*l3_exp_in(it, u + 1))
                    nc.scalar.activation(pe_[u][:, :, 0:E3], lg[u][:, :, 0:E3], ACT.Exp).then_inc(l3_exp.sem, 1)

        @block.vector
        def _(dve):
            v = nc.vector
            done = [0]

            def prepare(ins):
                done[0] += 1
                ins.then_inc(prep.sem, 1)
                dve.wait_ge(prep.sem, done[0])

            sim = small[:, S["sim"]:S["sim"] + KD * E0]
            dve.wait_ge(const_in.sem, 16 * 10)
            prepare(v.memset(ones[:], 1.0))
            prepare(v.tensor_tensor(simn.rearrange("p k e -> p (k e)"), sim, sim, ALU.mult))
            for b in range(BATCH):
                prepare(v.max(cm8[:, b, :], cond[:, b, :]))
                prepare(v.max_index(cidx[:, b, :], cm8[:, b, :], cond[:, b, :]))
            prepare(v.tensor_tensor(cexp[:], cond[:], cm8[:, :, 0:1].broadcast_to([P, BATCH, COND]), ALU.subtract))
            assert done[0] == PREP_COND
            v.tensor_copy(ct[:, :, 7:8], cm8[:, :, 0:1]).then_inc(idx_ready.sem, 1)
            dve.wait_ge(prep_act.sem, 1)
            prepare(v.tensor_reduce(ct[:, :, 0:1], cexp[:], AX.X, ALU.add))
            prepare(v.reciprocal(ct[:, :, 1:2], ct[:, :, 0:1]))
            prepare(v.tensor_tensor(cexp[:], cexp[:], ct[:, :, 1:2].broadcast_to([P, BATCH, COND]), ALU.mult))
            for b in range(BATCH):
                prepare(v.max(cm8[:, b, :], cexp[:, b, :]))
            prepare(v.tensor_tensor(ct[:, :, 2:3], cm8[:, :, 0:1], cm8[:, :, 1:2], ALU.add))
            prepare(v.reciprocal(ct[:, :, 3:4], ct[:, :, 2:3]))
            prepare(v.tensor_tensor(skw[:], cm8[:, :, 0:2], ct[:, :, 3:4].broadcast_to([P, BATCH, 2]), ALU.mult))
            dve.wait_ge(prep_act.sem, 3)
            prepare(v.tensor_scalar(sg[:], sg[:], 1.0, None, ALU.add))
            prepare(v.reciprocal(sg[:], sg[:]))
            prepare(v.tensor_scalar(cs, cs, 1e-12, None, ALU.max))
            prepare(v.reciprocal(cs, cs))
            for k in range(KD):
                prepare(v.tensor_tensor(simn[:, k, :], small_at(small, "sim", k, E0), cs, ALU.mult))
            dve.wait_ge(prep_pool.sem, 2)
            at = slice(S["sim"], S["sim"] + KD * E0)
            prepare(v.tensor_copy(sm_hi[:, at], simn.rearrange("p k e -> p (k e)")))
            prepare(v.tensor_tensor(sm_lo[:, at], simn.rearrange("p k e -> p (k e)"), sm_hi[:, at].bitcast(F32),
                                    ALU.subtract))
            assert done[0] == PREP_STEPS, done[0]

            with dve.Fori(0, PAIRS) as it:
                n_step = [0]

                def step(ins):
                    n_step[0] += 1
                    ins.then_inc(dve_step.sem, 1)
                    dve.wait_ge(*dve_step(it, n_step[0]))

                def step_hold(ins):
                    step(ins)
                    dve.sem_inc(passed.sem, 1)

                def bc(col, n):
                    return col.unsqueeze(2).broadcast_to([P, NT, n])

                def split_x(layer, u):
                    step(v.tensor_copy(x_hi[u][:], xT[u][:]))
                    v.tensor_tensor(x_lo[u][:], xT[u][:], x_hi[u][:].bitcast(F32),
                                    ALU.subtract).then_inc(x_pair.sem, 1)

                step(v.tensor_copy(pair_cond[:], cond[:, bass.ds(2 * it, 2), :]))
                step(v.tensor_scalar(pair_er[:], cond_er[:, bass.ds(2 * it, 2)], SCALING2, None, ALU.mult))
                step(v.tensor_copy(pair_skw[:], skw[:, bass.ds(2 * it, 2), :]))
                for u in U:
                    dve.wait_ge(*x_in[u](it, 1))
                    split_x(0, u)
                for u in U:
                    dve.wait_ge(*l0b_in[u](it, 1))
                for cc in range(2):
                    for u in U:
                        for ml in range(2):
                            n, m = 4 * cc + 2 * u + ml, 2 * cc + ml
                            dve.wait_ge(*gate_ready(it, n + 1))
                            dve.wait_ge(*silu_done(it, n + 1))
                            v.scalar_tensor_tensor(
                                F[u][:, ml, :], B(u, 2 * ml + 1)[:], l0b[u][:, 4 + m:5 + m],
                                acc[u][:, 2 * ml:2 * ml + 2, :].rearrange("p a n -> p (a n)"), ALU.add,
                                ALU.mult).then_inc(l0_gated.sem, 1)
                            dve.wait_ge(*l0_gated(it, n + 1))
                            v.tensor_copy(hid_hi[u][:, m, :], F[u][:, ml, :]).then_inc(hid_hi_ready.sem, 1)
                            dve.wait_ge(*hid_hi_ready(it, n + 1))
                            v.tensor_tensor(hid_lo[u][:, m, :], F[u][:, ml, :], hid_hi[u][:, m, :].bitcast(F32),
                                            ALU.subtract).then_inc(hid_ready.sem, 1)
                for u in U:
                    for m in range(KD):
                        dve.wait_ge(*l0_sq(it, 2 * u + m + 1))
                        v.scalar_tensor_tensor(h_lo[u][:, m, :], B(u, m)[:], l0b[u][:, 8 + m:9 + m],
                                               h_hi[u][:, m, :].bitcast(F32), ALU.add,
                                               ALU.subtract).then_inc(l0_h.sem, 1)
                for u in U:
                    m0 = m8[u][:, :, 0]
                    dve.wait_ge(*l0_norm(it, u + 1))
                    step(v.tensor_scalar(st[u][:, 0, :], st[u][:, 0, :], 1e-12, None, ALU.max))
                    step(v.reciprocal(st[u][:, 1, :], st[u][:, 0, :]))
                    step(v.tensor_tensor(lg[u][:], B(u, 2)[:, 0:64].rearrange("p (t e) -> p t e", t=NT),
                                         bc(st[u][:, 1, :], E0), ALU.mult))
                    step_hold(v.tensor_tensor(lg[u][:], lg[u][:], sg[:].unsqueeze(1).broadcast_to([P, NT, E0]),
                                              ALU.subtract))
                    for t in range(NT):
                        step_hold(v.max(m8[u][:, t, :], lg[u][:, t, :]))
                        step_hold(v.max_index(i8[u][:, t, :], m8[u][:, t, :], lg[u][:, t, :]))
                    step(v.tensor_copy(i8f[u][:], i8[u][:]))
                    iota = row("iota", E0).unsqueeze(1).broadcast_to([P, NT, E0])
                    step(v.tensor_tensor(fb[u][:], iota, bc(i8f[u][:, :, 0], E0), ALU.is_equal))
                    step(v.tensor_tensor(mk[u][:], iota, bc(i8f[u][:, :, 1], E0), ALU.is_equal))
                    step(v.tensor_tensor(fb[u][:], fb[u][:], mk[u][:], ALU.add))
                    step(v.tensor_scalar(st[u][:, 2, :], m0, 0.0, None, ALU.is_le))
                    step(v.tensor_tensor(fb[u][:], fb[u][:], bc(st[u][:, 2, :], E0), ALU.mult))
                    step(v.tensor_scalar(mk[u][:], lg[u][:], 0.0, None, ALU.is_gt))
                    step(v.tensor_tensor(mk[u][:], mk[u][:], fb[u][:], ALU.max))
                    step(v.tensor_scalar(lg[u][:], lg[u][:], 0.0, None, ALU.max))
                    step(v.tensor_scalar(st[u][:, 3, :], m0, 0.0, None, ALU.max))
                    v.tensor_tensor(lg[u][:], lg[u][:], bc(st[u][:, 3, :], E0),
                                    ALU.subtract).then_inc(l0_exp_in.sem, 1)
                for u in U:
                    dve.wait_ge(*l0_exp(it, u + 1))
                    step(v.tensor_tensor(pe_[u][:], pe_[u][:], mk[u][:], ALU.mult))
                    step(v.tensor_reduce(st[u][:, 4, :], pe_[u][:], AX.X, ALU.add))
                    step(v.reciprocal(st[u][:, 5, :], st[u][:, 4, :]))
                    v.tensor_tensor(rw[u][:], pe_[u][:], bc(st[u][:, 5, :], E0), ALU.mult).then_inc(l0_rw.sem, 1)
                for u in U:
                    dve.wait_ge(*l0_rw(it, u + 1))
                for g in range(8):
                    for u in U:
                        for t in range(NT):
                            n = 8 * g + 4 * u + t
                            dst = acc[u][:, t, 0:QKV]
                            dve.wait_ge(*qkv_ready(it, n + 1))
                            if g == 0:
                                v.tensor_scalar(dst, B(u, t)[:, 0:QKV], rw[u][:, t, 0:1], None,
                                                ALU.mult).then_inc(qkv_half.sem, 1)
                            else:
                                dve.wait_ge(*qkv_done(it, n - 7))
                                v.scalar_tensor_tensor(dst, B(u, t)[:, 0:QKV], rw[u][:, t, 2 * g:2 * g + 1], dst,
                                                       ALU.mult, ALU.add).then_inc(qkv_half.sem, 1)
                            dve.wait_ge(*qkv_half(it, n + 1))
                            v.scalar_tensor_tensor(dst, B(u, t)[:, QKV:2 * QKV],
                                                   rw[u][:, t, 2 * g + 1:2 * g + 2], dst, ALU.mult,
                                                   ALU.add).then_inc(qkv_done.sem, 1)
                for u in U:
                    for i in range(NT):
                        n, w = 4 * u + i, P * (i + 1)
                        row_i = G[u][:, s_off[i]:s_off[i] + w]
                        dve.wait_ge(*s0_ready(it, n + 1))
                        v.scalar_tensor_tensor(row_i, B(u, (i + 2) % 4)[:, 0:w], float(HD0) ** -0.5,
                                               causal[:, 384 - P * i:384 - P * i + w], ALU.mult,
                                               ALU.add).then_inc(s0_masked.sem, 1)
                        dve.wait_ge(*s0_masked(it, n + 1))
                        step(v.tensor_reduce(st[u][:, 0, i:i + 1], row_i, AX.X, ALU.max))
                        v.tensor_scalar(st[u][:, 1, i:i + 1], st[u][:, 0, i:i + 1], -1.0, None,
                                        ALU.mult).then_inc(s0_max.sem, 1)
                for u in U:
                    dve.wait_ge(*s0_p(it, 4 * u + 4))
                    step(v.reciprocal(st[u][:, 3, :], st[u][:, 2, :]))
                    for i in range(NT):
                        dve.wait_ge(*o0_ready(it, 4 * u + i + 1))
                        v.tensor_scalar(att[u][:, i, :], B(u, (i + 2) % 4)[:, 0:HD0], st[u][:, 3, i:i + 1], None,
                                        ALU.mult).then_inc(att0.sem, 1)

                def mix(r, u):
                    dve.wait_ge(*att0(it, 4 * u + 4))
                    if r == 1:
                        dve.wait_ge(*mixT_ready(it, 4 * u + 4))
                    for t in range(NT):
                        v.tensor_tensor(G[u][:, T * t:T * t + T].rearrange("p (e d) -> p e d", e=8),
                                        att[u][:, t, :].unsqueeze(1).broadcast_to([P, 8, HD0]),
                                        rw[u][:, t, 8 * r:8 * r + 8].unsqueeze(2).broadcast_to([P, 8, HD0]),
                                        ALU.mult).then_inc(mixed.sem, 1)

                def mix_split(r, u):
                    for k in range(4):
                        dve.wait_ge(*mix_hi(it, 8 * r + 4 * u + k + 1))
                        v.tensor_tensor(hid_lo[u][:, k, :], B(u, k % 2)[:], hid_hi[u][:, k, :].bitcast(F32),
                                        ALU.subtract).then_inc(mix_lo.sem, 1)

                for u in U:
                    mix(0, u)
                for u in U:
                    mix_split(0, u)
                for u in U:
                    mix(1, u)
                dve.wait_ge(*l1w_in(it, 1))
                for u in U:
                    step(v.tensor_scalar(F[u][:, 0, :], l1w[:, 0, :], pair_cond[:, u, 0:1], None, ALU.mult))
                    for g in range(1, COND):
                        step(v.scalar_tensor_tensor(F[u][:, 0, :], l1w[:, g, :], pair_cond[:, u, g:g + 1],
                                                    F[u][:, 0, :], ALU.mult, ALU.add))
                    step(v.tensor_tensor(F[u][:, 0, :], F[u][:, 0, :], mask1[:], ALU.mult))
                for u in U:
                    mix_split(1, u)
                for u in U:
                    dve.wait_ge(*oproj0(it, 2 + u + 1))
                    for m in range(KD):
                        step(v.tensor_tensor(xT[u][:, m, :], xT[u][:, m, :], B(u, 2 + m)[:], ALU.add))
                    step(v.tensor_copy(hid_hi[u][:, 0, :], F[u][:, 0, :]))
                    v.tensor_tensor(hid_lo[u][:, 0, :], F[u][:, 0, :], hid_hi[u][:, 0, :].bitcast(F32),
                                    ALU.subtract).then_inc(wbot_ready.sem, 1)
                    split_x(1, u)
                for u in U:
                    for m in range(KD):
                        dve.wait_ge(*l1c_hi(it, 2 * u + m + 1))
                        v.scalar_tensor_tensor(h_lo[u][:, m, :], B(u, m)[:], vec("l1b", m),
                                               h_hi[u][:, m, :].bitcast(F32), ALU.add,
                                               ALU.subtract).then_inc(l1c_h.sem, 1)
                RE = slice(1, E1)
                for u in U:
                    dve.wait_ge(*l1_logits(it, u + 1))
                    step(v.tensor_tensor(lg[u][:, :, RE], B(u, 2)[:, 0:64].rearrange("p (t e) -> p t e", t=NT)[:, :, RE],
                                         row("rb", E1 - 1).unsqueeze(1).broadcast_to([P, NT, E1 - 1]), ALU.add))
                    step(v.tensor_reduce(st[u][:, 0, :], lg[u][:, :, RE], AX.X, ALU.max))
                    v.tensor_tensor(lg[u][:, :, RE], lg[u][:, :, RE], bc(st[u][:, 0, :], E1 - 1),
                                    ALU.subtract).then_inc(l1_exp_in.sem, 1)
                for u in U:
                    dve.wait_ge(*l1_exp(it, u + 1))
                    step(v.tensor_reduce(st[u][:, 1, :], pe_[u][:, :, RE], AX.X, ALU.add))
                    step(v.reciprocal(st[u][:, 2, :], st[u][:, 1, :]))
                    step_hold(v.tensor_tensor(pe_[u][:, :, RE], pe_[u][:, :, RE], bc(st[u][:, 2, :], E1 - 1),
                                              ALU.mult))
                    for t in range(NT):
                        step_hold(v.max(m8[u][:, t, :], pe_[u][:, t, RE]))
                        step_hold(v.max_index(i8[u][:, t, :], m8[u][:, t, :], pe_[u][:, t, RE]))
                    step(v.tensor_copy(i8f[u][:], i8[u][:]))
                    iota = row("iota", E1 - 1).unsqueeze(1).broadcast_to([P, NT, E1 - 1])
                    step(v.tensor_tensor(mk[u][:, :, RE], iota, bc(i8f[u][:, :, 0], E1 - 1), ALU.is_equal))
                    for j in range(1, TOP1):
                        step(v.tensor_tensor(fb[u][:, :, RE], iota, bc(i8f[u][:, :, j], E1 - 1), ALU.is_equal))
                        step(v.tensor_tensor(mk[u][:, :, RE], mk[u][:, :, RE], fb[u][:, :, RE], ALU.add))
                    step(v.memset(rw[u][:, :, 0:1], 1.0))
                    v.tensor_tensor(rw[u][:, :, RE], pe_[u][:, :, RE], mk[u][:, :, RE],
                                    ALU.mult).then_inc(l1_cw.sem, 1)

                def l1_split(e, u):
                    dve.wait_ge(*e1_hi(it, 2 * e + u + 1))
                    hs = slice(2 * (e % 2), 2 * (e % 2) + 2)
                    v.tensor_tensor(hid_lo[u][:, hs, :], F[u][:], hid_hi[u][:, hs, :].bitcast(F32),
                                    ALU.subtract).then_inc(e1_hid.sem, 1)

                for u in U:
                    l1_split(0, u)
                for u in U:
                    dve.wait_ge(*acc1_init(it, u + 1))
                for e in range(E1):
                    for u in U:
                        if e + 1 < E1:
                            l1_split(e + 1, u)
                        for t in range(NT):
                            dve.wait_ge(*e1_y_ready(it, 4 * e + 2 * u + t // 2 + 1))
                            if e > 0:
                                dve.wait_ge(*e1_sum(it, 8 * (e - 1) + 4 * u + t + 1))
                            v.scalar_tensor_tensor(acc[u][:, t, :],
                                                   B(u, 2 + t // 2)[:, D * (t % 2):D * (t % 2) + D],
                                                   rw[u][:, t, e:e + 1], acc[u][:, t, :], ALU.mult,
                                                   ALU.add).then_inc(e1_sum.sem, 1)
                for u in U:
                    for m in range(KD):
                        dve.wait_ge(*accT_ready(it, 2 * u + m + 1))
                        step(v.tensor_tensor(xT[u][:, m, :], xT[u][:, m, :], B(u, m)[:], ALU.add))
                    split_x(2, u)
                for u in U:
                    dve.wait_ge(*hA_hi(it, u + 1))
                    v.scalar_tensor_tensor(hid_lo[u][:, 0, :], B(u, 2)[:], pair_er[:, u:u + 1],
                                           hid_hi[u][:, 0, :].bitcast(F32), ALU.mult,
                                           ALU.subtract).then_inc(hA.sem, 1)
                for u in U:
                    for m in range(KD):
                        dve.wait_ge(*l2c_hi(it, 2 * u + m + 1))
                        v.scalar_tensor_tensor(h_lo[u][:, m, :], B(u, m)[:], vec("l2b", m),
                                               h_hi[u][:, m, :].bitcast(F32), ALU.add,
                                               ALU.subtract).then_inc(l2c_h.sem, 1)
                for u in U:
                    for m in range(KD):
                        v.scalar_tensor_tensor(xT[u][:, m, :], B(u, m)[:], vec("l2b", m), xT[u][:, m, :], ALU.add,
                                               ALU.add).then_inc(l2c_x.sem, 1)

                def rank_tokens(u):
                    junk = G[u][:, 2 * T:3 * T]
                    dve.wait_ge(*sc_sb(it, u + 1))
                    for t in range(NT):
                        s_in = v.scalar_tensor_tensor(junk[:, 0:P], G[u][:, tok(t)], 1.0, ident[:], ALU.mult, ALU.mult,
                                                      accum_out=st[u][:, 3, t:t + 1])
                        if t < NT - 1:
                            step(s_in)
                    s_in.then_inc(sig_in.sem, 1)
                    dve.wait_ge(*sig_in(it, u + 1))
                    for t in range(NT):
                        step(v.tensor_scalar(junk, G[u][:, 0:T], st[u][:, 3, t:t + 1], None, ALU.is_gt, ALU.add,
                                             accum_out=st[u][:, 4, t:t + 1]))
                        step(v.scalar_tensor_tensor(junk, G[u][:, 0:T], st[u][:, 3, t:t + 1],
                                                    before[:, 384 - P * t:384 - P * t + T], ALU.is_equal, ALU.mult,
                                                    accum_out=st[u][:, 5, t:t + 1]))
                    step(v.tensor_tensor(st[u][:, 4, :], st[u][:, 4, :], st[u][:, 5, :], ALU.add))
                    v.tensor_scalar(st[u][:, 4, :], st[u][:, 4, :], float(TOPK2), None,
                                    ALU.is_lt).then_inc(sel_ready.sem, 1)

                for m in range(8):
                    for u in U:
                        n = 2 * m + u
                        dve.wait_ge(*f2_gelu(it, n + 1))
                        if m >= 4:
                            dve.wait_ge(*f2_down(it, n - 7))
                        v.tensor_copy(hid_hi[u][:, m % 4, :], F[u][:, m % 2, :]).then_inc(f2_hi.sem, 1)
                        dve.wait_ge(*f2_hi(it, n + 1))
                        v.tensor_tensor(hid_lo[u][:, m % 4, :], F[u][:, m % 2, :],
                                        hid_hi[u][:, m % 4, :].bitcast(F32), ALU.subtract).then_inc(f2_hid.sem, 1)
                    if m < 2:
                        rank_tokens(m)
                for u in U:
                    dve.wait_ge(*sig_exp(it, u + 1))
                    dve.wait_ge(*sel_ready(it, u + 1))
                    step(v.tensor_scalar(st[u][:, 6, :], st[u][:, 6, :], 1.0, None, ALU.add))
                    step(v.reciprocal(st[u][:, 7, :], st[u][:, 6, :]))
                    v.tensor_tensor(st[u][:, 5, :], st[u][:, 4, :], st[u][:, 7, :],
                                    ALU.mult).then_inc(wtok_ready.sem, 1)
                for u in U:
                    dve.wait_ge(*f2_down(it, 14 + u + 1))
                    dve.wait_ge(*wbc_sb(it, u + 1))
                    dve.wait_ge(*l2c_x(it, 4))
                    for m in range(KD):
                        step(v.scalar_tensor_tensor(F[u][:, m, :], B(u, 2 + m)[:], vec("b2", m), G[u][:, T:2 * T],
                                                    ALU.add, ALU.mult))
                        step(v.tensor_tensor(xT[u][:, m, :], xT[u][:, m, :], F[u][:, m, :], ALU.add))
                    split_x(3, u)
                for i in range(48):
                    j, c, u = steps[i // 2]
                    f, hs = F[i % 2][:, (i // 2) % 2, :], 2 * (c % 2) + i % 2
                    dve.wait_ge(*u3_ready(it, i + 1))
                    dve.wait_ge(*g3_gelu(it, i + 1))
                    v.scalar_tensor_tensor(f, G[i % 2][:, 0:T], pair_skw[:, u, j:j + 1] if j < 2 else 1.0,
                                           PB[i % 2][1][:], ALU.mult, ALU.mult).then_inc(g3_gated.sem, 1)
                    dve.wait_ge(*g3_gated(it, i + 1))
                    if i // 2 >= 4:
                        dve.wait_ge(*d3_step(it, i // 2 - 3))
                    v.tensor_copy(hid_hi[u][:, hs, :], f).then_inc(g3_hi.sem, 1)
                    dve.wait_ge(*g3_hi(it, i + 1))
                    v.tensor_tensor(hid_lo[u][:, hs, :], f, hid_hi[u][:, hs, :].bitcast(F32),
                                    ALU.subtract).then_inc(g3_hid.sem, 1)

                def norm(i, gamma):
                    for u in U:
                        dve.wait_ge(*nrm3(it, 2 * i + u + 1))
                        v.reciprocal(st[u][:, 2, :], st[u][:, 1, :]).then_inc(rs3.sem, 1)
                    for u in U:
                        n = 2 * i + u
                        dve.wait_ge(*rsbc_ready(it, n + 1))
                        if i == 0:
                            dve.wait_ge(*base_ready(it, 2 * u + 2))
                        for k in range(KD):
                            v.scalar_tensor_tensor(F[u][:, k, :], base[u][:, k, :], vec(gamma, k), B(u, 1)[:],
                                                   ALU.mult, ALU.mult).then_inc(n3_F.sem, 1)
                        dve.wait_ge(*n3_F(it, 2 * n + 2))
                        v.tensor_copy(h_hi[u][:], F[u][:]).then_inc(n3_hi.sem, 1)
                        dve.wait_ge(*n3_hi(it, n + 1))
                        v.tensor_tensor(h_lo[u][:], F[u][:], h_hi[u][:].bitcast(F32),
                                        ALU.subtract).then_inc(n3_h.sem, 1)

                def split_lo(dst, ps, bias, hi, ready):
                    v.scalar_tensor_tensor(dst, ps, bias, hi.bitcast(F32), ALU.add,
                                           ALU.subtract).then_inc(ready.sem, 1)

                norm(0, "gamma1")
                for u in U:
                    for tp in range(2):
                        dve.wait_ge(*q3_ready(it, 2 * u + tp + 1))
                        v.tensor_tensor(acc[u][:, 2 * tp:2 * tp + 2, :],
                                        B(u, 2 + tp)[:].rearrange("p (a n) -> p a n", a=2),
                                        row("bq", D).unsqueeze(1).broadcast_to([P, 2, D]),
                                        ALU.add).then_inc(q3_sb.sem, 1)
                for u in U:
                    dve.wait_ge(*lat_hi(it, u + 1))
                    split_lo(lat_p[u][1], B(u, 0)[0:L3LAT, :], vec("bdown", 0)[0:L3LAT], lat_p[u][0], lat_lo)
                for u in U:
                    for t in range(NT):
                        dve.wait_ge(*kv3_ready(it, 4 * u + t + 1))
                        v.tensor_tensor(kv3[u][:, t, :], B(u, t)[:], row("bkv", 2 * D), ALU.add).then_inc(kv3_sb.sem, 1)

                def heads3(col):
                    return col.unsqueeze(3).broadcast_to([P, NT, HEADS, HEADS])

                def sum3(half, phase, u, t):
                    hs = slice(HH3 * half, HH3 * half + HH3)
                    return v.tensor_reduce((att3_p if phase == "scores" else q3)[u][:, t, hs, :], prod3[half], AX.X,
                                           ALU.add)

                def softmax3_in(u):
                    step(v.tensor_reduce(lg[u][:], att3_p[u], AX.X, ALU.max))
                    v.tensor_tensor(att3_p[u], att3_p[u], heads3(lg[u][:]), ALU.subtract).then_inc(att3_in.sem, 1)

                def softmax3(u):
                    dve.wait_ge(*att3_exp(it, u + 1))
                    step(v.tensor_reduce(pe_[u][:], att3_p[u], AX.X, ALU.add))
                    step(v.reciprocal(mk[u][:], pe_[u][:]))
                    v.tensor_tensor(att3_p[u], att3_p[u], heads3(mk[u][:]), ALU.mult).then_inc(att3.sem, 1)

                for n, (phase, u, t) in enumerate(SWEEP3):
                    if phase == "scores" and t == 0:
                        dve.wait_ge(*q3_sb(it, 2 * u + 2))
                        dve.wait_ge(*kv3_sb(it, 4 * u + 4))
                    if phase == "values" and t == 0:
                        if u == 0:
                            softmax3_in(1)
                        softmax3(u)
                        dve.wait_ge(*att3(it, u + 1))
                    if n >= 1:
                        dve.wait_ge(*sum_dve(it, n))
                    product3(v, prod3[0], 0, phase, u, t).then_inc(prod_dve.sem, 1)
                    dve.wait_ge(*prod_pool(it, n + 1))
                    sum3(1, phase, u, t).then_inc(sum_pool.sem, 1)
                    dve.wait_ge(*prod_dve(it, n + 1))
                    sum3(0, phase, u, t).then_inc(sum_dve.sem, 1)
                    if n in (3, 7):
                        dve.wait_ge(*sum_dve(it, n + 1))
                        dve.wait_ge(*sum_pool(it, n + 1))
                    if n == 3:
                        softmax3_in(0)
                for u in U:
                    for m in range(KD):
                        dve.wait_ge(*o3_hi(it, 2 * u + m + 1))
                        v.tensor_tensor(x_lo[u][:, m, :], B(u, m)[:], x_hi[u][:, m, :].bitcast(F32),
                                        ALU.subtract).then_inc(o3_lo.sem, 1)
                for u in U:
                    for m in range(KD):
                        dve.wait_ge(*wo_ready(it, 2 * u + m + 1))
                        v.scalar_tensor_tensor(base[u][:, m, :], B(u, 2 + m)[:], vec("bo", m), base[u][:, m, :],
                                               ALU.add, ALU.add).then_inc(x1_ready.sem, 1)
                dve.wait_ge(*x1_ready(it, 4))
                norm(1, "gamma2")
                for u in U:
                    lgu, pu = lg[u][:, :, 0:E3], pe_[u][:, :, 0:E3]
                    dve.wait_ge(*l3_logits(it, u + 1))
                    step(v.tensor_tensor(lgu, B(u, 0)[:, 0:NT * E3].rearrange("p (t e) -> p t e", t=NT),
                                         row("bg", E3).unsqueeze(1).broadcast_to([P, NT, E3]), ALU.add))
                    step(v.tensor_reduce(st[u][:, 0, :], lgu, AX.X, ALU.max))
                    v.tensor_tensor(lgu, lgu, bc(st[u][:, 0, :], E3), ALU.subtract).then_inc(l3_exp_in.sem, 1)
                for u in U:
                    pu = pe_[u][:, :, 0:E3]
                    dve.wait_ge(*l3_exp(it, u + 1))
                    step(v.tensor_reduce(st[u][:, 3, :], pu, AX.X, ALU.add))
                    step(v.reciprocal(st[u][:, 4, :], st[u][:, 3, :]))
                    v.tensor_tensor(rw[u][:, :, 0:E3], pu, bc(st[u][:, 4, :], E3), ALU.mult).then_inc(l3_gate.sem, 1)
                for u in U:
                    dve.wait_ge(*l3_gate(it, u + 1))
                for c in range(4):
                    for u in U:
                        for t in range(NT):
                            n = 8 * c + 4 * u + t
                            dve.wait_ge(*we_ready(it, n + 1))
                            if c == 0:
                                v.tensor_scalar(acc[u][:, t, :], B(u, t)[:, 0:D], rw[u][:, t, 0:1], None,
                                                ALU.mult).then_inc(we_half.sem, 1)
                            else:
                                dve.wait_ge(*we_done(it, n - 7))
                                v.scalar_tensor_tensor(acc[u][:, t, :], B(u, t)[:, 0:D],
                                                       rw[u][:, t, 2 * c:2 * c + 1], acc[u][:, t, :], ALU.mult,
                                                       ALU.add).then_inc(we_half.sem, 1)
                            dve.wait_ge(*we_half(it, n + 1))
                            v.scalar_tensor_tensor(acc[u][:, t, :], B(u, t)[:, D:2 * D],
                                                   rw[u][:, t, 2 * c + 1:2 * c + 2], acc[u][:, t, :], ALU.mult,
                                                   ALU.add).then_inc(we_done.sem, 1)
                for u in U:
                    for m in range(KD):
                        step(v.tensor_tensor(base[u][:, m, :], base[u][:, m, :], xT[u][:, m, :], ALU.add))
                for u in U:
                    for m in range(KD):
                        dve.wait_ge(*accT_ready(it, 4 + 2 * u + m + 1))
                        v.tensor_tensor(xT[u][:, m, :], base[u][:, m, :], B(u, m)[:], ALU.add).then_inc(x_final.sem, 1)
                assert n_step[0] == DVE_STEPS, n_step[0]


def layouts(i):
    f = {}

    def cols(w):
        return w.reshape(-1, P, w.shape[-1]).transpose(1, 0, 2)

    def side(*parts):
        return np.concatenate([p.reshape(p.shape[0], -1) for p in parts], axis=1)

    def percol(v):
        return v.reshape(-1, P).T

    def transposed(w):
        return np.swapaxes(w, -1, -2)

    f["x"] = transposed(i["x"]).reshape(BATCH, KD, P, T).transpose(0, 2, 1, 3)
    c = i["cond_8"]
    f["cond"] = np.broadcast_to(c.reshape(1, -1), (P, BATCH * COND))
    f["cond_er"] = np.repeat(c.T, RANK2, axis=0)
    up, gate, down = (transposed(i[f"L0_cond_W_{n}"]) for n in ("up", "gate", "down"))
    f["l0c"] = np.stack([np.stack([side(cols(up[e][:, 256 * a:256 * a + 256]), cols(gate[e][:, 256 * a:256 * a + 256]))
                                   for a in range(2)] + [side(cols(down[e]))]) for e in range(COND)])
    f["l0b"] = np.stack([side(percol(i["L0_cond_b_up"][e]), percol(i["L0_cond_b_gate"][e]),
                              percol(i["L0_cond_b_down"][e])) for e in range(COND)])
    qkv = np.concatenate([i["L0_ffn_q_proj"], i["L0_ffn_k_proj"], i["L0_ffn_v_proj"]], axis=2)
    qkv = qkv.transpose(1, 0, 2).reshape(D, E0 * QKV)
    f["qkv"] = np.stack([side(cols(qkv[:, 768 * a:768 * a + 768])) for a in range(4)])
    o = i["L0_ffn_o_proj"].reshape(E0 * HD0, D)
    f["o0"] = np.stack([side(cols(o[512 * a:512 * a + 512])) for a in range(2)])
    w = transposed(i["L1_cond_weight"])
    f["l1w"] = w.reshape(COND, KD, P, D).transpose(2, 0, 1, 3).reshape(P, -1)
    f["mask1"] = side(cols(i["L1_cond_mask"].T))
    w1 = np.concatenate([i["L1_ffn_sW1"][None], i["L1_ffn_eW1"]])
    w2 = np.concatenate([i["L1_ffn_sW2"][None], i["L1_ffn_eW2"]])
    f["l1"] = np.stack([side(cols(w1[e]), cols(w2[e])) for e in range(E1)])
    f["b2rows"] = np.concatenate([i["L1_ffn_sb2"][None], i["L1_ffn_eb2"]])
    eb1 = np.concatenate([i["L1_ffn_sb1"][None], i["L1_ffn_eb1"]])
    A_er = i["L2_cond_As"].reshape(COND * RANK2, D).T
    B_er = i["L2_cond_Bs"].transpose(0, 2, 1).reshape(COND * RANK2, D)
    W1, W2 = i["L2_ffn_W1"], i["L2_ffn_W2"]
    f["l2"] = np.stack([side(cols(i["L2_cond_W_base"].T), cols(A_er), B_er)] +
                       [side(cols(W1[:, 256 * a:256 * a + 256]), cols(W2[256 * a:256 * a + 256])) for a in range(4)])

    def mlp(g, u, d):
        return np.stack([side(cols(g[:, 256 * a:256 * a + 256]), cols(u[:, 256 * a:256 * a + 256]),
                              cols(d[256 * a:256 * a + 256])) for a in range(4)])

    f["skill"] = np.stack([mlp(i["L3_cond_skill_gate"][e], i["L3_cond_skill_up"][e], i["L3_cond_skill_down"][e])
                           for e in range(COND)])
    f["shared"] = mlp(i["L3_cond_shared_gate"], i["L3_cond_shared_up"], i["L3_cond_shared_down"])
    f["l3q"] = side(cols(i["L3_ffn_Wq"]))
    up = i["L3_ffn_Wup"].reshape(L3LAT, HEADS, 2, HD3)
    kv = np.zeros((P, 2 * D), np.float32)
    kv[:L3LAT] = side(up[:, :, 0].reshape(L3LAT, D), up[:, :, 1].reshape(L3LAT, D))
    f["l3kv"] = side(cols(i["L3_ffn_Wdown"]), kv)
    f["l3o"] = side(cols(i["L3_ffn_Wo"]))
    we = i["L3_ffn_We"].transpose(1, 0, 2).reshape(D, E3 * D)
    f["l3e"] = np.stack([side(cols(we[:, 512 * a:512 * a + 512])) for a in range(4)])
    bup = i["L3_ffn_bup"].reshape(HEADS, 2, HD3)
    bdown = np.zeros(P, np.float32)
    bdown[:L3LAT] = i["L3_ffn_bdown"]
    VEC = [("l1b", percol(i["L1_cond_bias"])), ("eb1", percol(eb1.reshape(-1))), ("l2b", percol(i["L2_cond_b_base"])),
           ("b1", percol(i["L2_ffn_b1"])), ("b2", percol(i["L2_ffn_b2"])), ("gamma1", percol(i["L3_ffn_gamma1"])),
           ("gamma2", percol(i["L3_ffn_gamma2"])), ("bdown", percol(bdown)), ("bo", percol(i["L3_ffn_bo"])),
           ("eps", np.full((P, 1), EPS3, np.float32))]
    bq, bk, bv = i["L3_ffn_bq"], bup[:, 0].reshape(-1), bup[:, 1].reshape(-1)
    ROW = [("iota", np.arange(16, dtype=np.float32)), ("gates", i["L0_ffn_gates"]), ("rb", i["L1_ffn_router_b"]),
           ("bg", i["L3_ffn_bg"]), ("bq", bq), ("bkv", np.concatenate([bk, bv]))]
    router = np.concatenate([np.zeros((D, 1), np.float32), i["L1_ffn_router_W"]], axis=1)
    SMALL = [("sim", side(cols(i["L0_ffn_sim_matrix"]))), ("router", side(cols(router))),
             ("wg", side(cols(i["L3_ffn_Wg"]))),
             ("wr", np.repeat(percol(i["L2_ffn_w_router"]), P, axis=1))]
    offs = {}
    for name, parts in (("vecs", VEC), ("rows", [(n, np.broadcast_to(r.reshape(1, -1), (P, r.size))) for n, r in ROW]),
                        ("small", SMALL)):
        f[name] = np.concatenate([p for _, p in parts], axis=1)
        at = np.cumsum([0] + [p.shape[1] for _, p in parts]).tolist()
        offs[name] = {n: a for (n, _), a in zip(parts, at)}
    f["ident"] = np.eye(P, dtype=np.float32)
    p, j = np.arange(P)[:, None], np.arange(384 + T)[None] - 384
    f["causal"] = np.where(j[:, :T] <= p, 0.0, -1e30).astype(np.float32)
    f["before"] = (j < p).astype(np.float32)
    return {n: np.ascontiguousarray(a, dtype=np.float32) for n, a in f.items()}, offs


def kernel(**inputs):
    import concourse.bacc as bacc
    from concourse.bass_utils import run_bass_kernel_spmd

    arrays, offs = layouts({n: np.asarray(a) for n, a in inputs.items()})
    nc = bacc.Bacc("TRN2", target_bir_lowering=False, num_devices=1)
    A = {n: nc.dram_tensor(f"in_{n}", a.shape, F32, kind="ExternalInput").ap() for n, a in arrays.items()}
    A["out"] = nc.dram_tensor("out_x", (BATCH, P, KD, T), F32, kind="ExternalOutput").ap()
    A["VEC"], A["ROW"], A["SMALL"] = offs["vecs"], offs["rows"], offs["small"]
    A["widths"] = WIDTHS
    nc.disable_value_cache = True
    build(nc, A)
    r = run_bass_kernel_spmd(nc, [{f"in_{n}": a for n, a in arrays.items()}], core_ids=[0])
    out = r.results[0]["out_x"]
    return np.ascontiguousarray(out.transpose(0, 2, 1, 3).reshape(BATCH, D, T).transpose(0, 2, 1))
```

```python
from contextlib import ExitStack

import numpy as np

import concourse.bass as bass
from concourse import mybir

ALU = mybir.AluOpType
ACT = mybir.ActivationFunctionType
AX = mybir.AxisListType
F32 = mybir.dt.float32
F32R = mybir.dt.float32r
U32 = mybir.dt.uint32

P = 128
BATCH, T, D = 4, 512, 256
KD = D // P
NT = T // P
PAIRS = BATCH // 2
COND = 8
H0 = 512
E0, HD0 = 16, 64
QKV = 3 * HD0
E1 = 16
TOP1 = 3
F2 = 1024
TOPK2 = T // 2
RANK2, SCALING2 = 16, 2.0
I3 = 1024
HEADS, HD3, L3LAT, E3 = 16, 16, 64, 8
HQ = HEADS // 4
DVE_Q, POOL_Q = (2, 2), (2, 2)
EPS3 = 1e-6
CW = 1536
RAW_SLOTS, W_SLOTS = 2, 4
PREP_COND, PREP_STEPS, DVE_STEPS = 10, 29, 193
WE_PRIME = 16
WE_LAST = -32 + 16 + 4
PRIME = 2

(C_L0C, C_QKV, C_O0, C_L1, C_L2L, C_L2C, C_L2F, C_L3A, C_L3P0, C_L3B, C_L3P1, C_L3E, CHUNKS) = np.cumsum(
    [0, 6, 4, 2, 16, 1, 1, 4, 16, 1, 8, 1, 4]).tolist()

WIDTHS = ([1024] * 6 + [1536] * 4 + [1024] * (2 + 16) + [512] * 2 + [1024] * 4 + [1536] * 16 + [1152] +
          [1536] * 8 + [1152] + [1536] + [1024] * 3)

STEPS3 = [(j, c, u) for u in range(2) for j in (2, 0, 1) for c in range(4)]
TILES3 = 2 * len(STEPS3)
PROJECT_TILE = 26
SWEEP_TILES = (31, 33, 35, 37, 42, 44)
SOFTMAX_IN_TILE, EXP_TILE, SOFTMAX_TILE = 39, 40, 41


def chunk3(n):
    return C_L3A + n if n < 16 else C_L3B + n - 16


def begun_before(c):
    return {C_L3B + 1: C_L3B + 1, C_L3B + 2: C_L3B + 2, C_L3E + 2: C_L3P1 + 1}.get(c, c - 1)


ACT_SPLIT3 = range(C_L3A + 2, C_L3E + 1)
BEGIN_TILE = {chunk3(n): 2 * n for n in range(len(STEPS3))}
BEGIN_TILE[C_L3P0] = PROJECT_TILE + 4
SPLIT_TILE = {c: BEGIN_TILE[begun_before(c) - 1] for c in ACT_SPLIT3}
SPLIT_TILE[C_L3B + 3] += 1
ACT_SPLIT = [*range(C_L0C + 2, C_QKV), *ACT_SPLIT3]


class Signal:

    def __init__(self, sem, per_pair, step=1, prime=0):
        self.sem, self.per_pair, self.step, self.prime = sem, per_pair, step, prime

    def __call__(self, it, k):
        assert k + self.prime > 0
        return self.sem, (it * self.per_pair + k + self.prime) * self.step


def build(nc, A):
    with ExitStack() as ctx:
        def sb(name, shape, dt=F32):
            return ctx.enter_context(nc.sbuf_tensor(name, shape, dt))

        def sig(name, per_pair, step=1, prime=0):
            return Signal(ctx.enter_context(nc.semaphore(name)), per_pair, step, prime)

        bank = [ctx.enter_context(nc.psum_tensor(f"bank{i}", [P, 512], F32)) for i in range(8)]

        def B(u, i):
            return bank[4 * u + i]

        U = range(2)
        xT = [sb(f"xT{u}", [P, KD, T]) for u in U]
        x_hi = [sb(f"x_hi{u}", [P, KD, T], F32R) for u in U]
        x_lo = [sb(f"x_lo{u}", [P, KD, T], F32R) for u in U]
        h_hi = [sb(f"h_hi{u}", [P, KD, T], F32R) for u in U]
        h_lo = [sb(f"h_lo{u}", [P, KD, T], F32R) for u in U]
        hid_hi = [sb(f"hid_hi{u}", [P, 4, T], F32R) for u in U]
        hid_lo = [sb(f"hid_lo{u}", [P, 4, T], F32R) for u in U]
        F = [sb(f"F{u}", [P, 2, T]) for u in U]
        acc = [sb(f"acc{u}", [P, NT, D]) for u in U]
        G = [sb(f"G{u}", [P, 4 * T]) for u in U]
        base = [sb(f"base{u}", [P, KD, T]) for u in U]
        VW = sb("VW", [P, 2, NT * HEADS * 32])
        raw = [sb(f"raw{i}", [P, CW]) for i in range(RAW_SLOTS)]
        w_hi = [sb(f"w_hi{i}", [P, CW], F32R) for i in range(W_SLOTS)]
        w_lo = [sb(f"w_lo{i}", [P, CW], F32R) for i in range(W_SLOTS)]
        mask1 = sb("mask1", [P, KD * D])
        ident = sb("ident", [P, P])
        ones = sb("ones", [P, P])
        causal = sb("causal", [P, T])
        before = sb("before", [P, 384 + T])
        vecs = sb("vecs", [P, A["vecs"].shape[1]])
        rows = sb("rows", [P, A["rows"].shape[1]])
        NS = A["small"].shape[1]
        small = base[0][:, 0, 0:NS]
        sm_hi = sb("sm_hi", [P, NS], F32R)
        sm_lo = sb("sm_lo", [P, NS], F32R)
        b2rows = sb("b2rows", [E1, D])
        def s2(name, shape, dt=F32):
            return [sb(f"{name}{u}", shape, dt) for u in U]

        lg, pe_, mk, fb, rw = (s2(n, [P, NT, 16]) for n in ("lg", "pexp", "mk", "fb", "rw"))
        m8 = s2("m8", [P, NT, 8])
        i8 = s2("i8", [P, NT, 8], U32)
        i8f = s2("i8f", [P, NT, 8])
        st = s2("st", [P, 8, NT])
        cond = sb("cond", [P, BATCH, COND])
        cond_er = sb("cond_er", [P, BATCH])
        cidx = sb("cidx", [P, BATCH, 8], U32)
        cm8, ct, cexp = m8[1], m8[0], i8f[0]
        skw = sb("skw", [P, BATCH, 2])
        pair_cond = sb("pair_cond", [P, 2, COND])
        pair_er = sb("pair_er", [P, 2])
        pair_skw = sb("pair_skw", [P, 2, 2])
        l0b = s2("l0b", [P, 10])
        simn = pe_[0][:, 0:KD, :]
        cs = mk[0][:, 0, :]
        sg = sb("sg", [P, E0])

        V, R, S = A["VEC"], A["ROW"], A["SMALL"]

        def vec(name, m):
            return vecs[:, V[name] + m:V[name] + m + 1]

        def row(name, n):
            return rows[:, R[name]:R[name] + n]

        def small_at(t, name, k, n):
            return t[:, S[name] + k * n:S[name] + (k + 1) * n]

        cond_in = sig("cond_in", 0)
        const_in = sig("const_in", 0)
        prep = sig("prep", 0)
        prep_pe = sig("prep_pe", 0)
        prep_act = sig("prep_act", 0)
        prep_pool = sig("prep_pool", 0)
        idx_ready = sig("idx_ready", 0)
        l0b_in = [sig(f"l0b_in{u}", 1, 16) for u in U]
        x_in = [sig(f"x_in{u}", 1, 16) for u in U]
        out_written = sig("out_written", 2, 16)
        l1w_in = sig("l1w_in", 1, 16)
        raw_in = [sig(f"raw_in{i}", CHUNKS // RAW_SLOTS, 16) for i in range(RAW_SLOTS)]
        w_hi_ready = sig("w_hi_ready", CHUNKS - len(ACT_SPLIT))
        w_hi_act = sig("w_hi_act", len(ACT_SPLIT))
        w_ready = sig("w_ready", CHUNKS, prime=PRIME)
        w_begun = sig("w_begun", CHUNKS, prime=PRIME)
        passed = sig("passed", 0)
        dve_step = sig("dve_step", DVE_STEPS)
        act_step = sig("act_step", 8)
        x_pair = sig("x_pair", 8)
        up_ready, gate_ready, silu_done, l0_gated, hid_hi_ready, hid_ready = (
            sig(n, 8) for n in ("up_ready", "gate_ready", "silu_done", "l0_gated", "hid_hi_ready", "hid_ready"))
        l0_down, l0_h_hi, l0_sq, l0_h = (sig(n, 4) for n in ("l0_down", "l0_h_hi", "l0_sq", "l0_h"))
        l0_logits, l0_norm, l0_exp_in, l0_exp, l0_rw = (
            sig(n, 2) for n in ("l0_logits", "l0_norm", "l0_exp_in", "l0_exp", "l0_rw"))
        qkv_ready, qkv_half, qkv_done = (sig(n, 64) for n in ("qkv_ready", "qkv_half", "qkv_done"))
        qkT_ready = sig("qkT_ready", 4)
        qkT_sb = sig("qkT_sb", 4)
        s0_ready, s0_masked, s0_max, s0_p, s0_pT, s0_pT_sb, o0_ready, att0 = (
            sig(n, 8) for n in ("s0_ready", "s0_masked", "s0_max", "s0_p", "s0_pT", "s0_pT_sb", "o0_ready", "att0"))
        mixed, mixT_ready, mix_hi, mix_lo = (sig(n, 16) for n in ("mixed", "mixT_ready", "mix_hi", "mix_lo"))
        oproj0 = sig("oproj0", 4)
        wbot_ready = sig("wbot_ready", 2)
        l1c_ready, l1c_hi, l1c_h = (sig(n, 4) for n in ("l1c_ready", "l1c_hi", "l1c_h"))
        l1_logits, l1_exp_in, l1_exp, l1_cw, cwT_ready, cwT_sb, b2_ready, acc1_init = (
            sig(n, 2) for n in ("l1_logits", "l1_exp_in", "l1_exp", "l1_cw", "cwT_ready", "cwT_sb", "b2_ready",
                                "acc1_init"))
        e1_hid_ready = sig("e1_hid_ready", 2 * E1)
        e1_relu = sig("e1_relu", 4 * E1)
        e1_hi = sig("e1_hi", 2 * E1)
        e1_hid = sig("e1_hid", 2 * E1)
        e1_y_ready = sig("e1_y_ready", 4 * E1)
        e1_sum = sig("e1_sum", 8 * E1)
        accT_ready = sig("accT_ready", 8)
        hA_ready, hA_hi, hA = (sig(n, 2) for n in ("hA_ready", "hA_hi", "hA"))
        l2c_ready, l2c_hi, l2c_h, l2c_x = (sig(n, 4) for n in ("l2c_ready", "l2c_hi", "l2c_h", "l2c_x"))
        sc_ready, sc_sb, sel_ready, sig_in, sig_exp, wtok_ready, wbc_ready, wbc_sb = (
            sig(n, 2) for n in ("sc_ready", "sc_sb", "sel_ready", "sig_in", "sig_exp", "wtok_ready", "wbc_ready",
                                "wbc_sb"))
        f2_ready, f2_gelu, f2_hi, f2_hid = (sig(n, 16) for n in ("f2_ready", "f2_gelu", "f2_hi", "f2_hid"))
        f2_down = sig("f2_down", 16)
        g3_ready, u3_ready, g3_gelu, g3_gated, g3_hi, g3_hid = (
            sig(n, 48) for n in ("g3_ready", "u3_ready", "g3_gelu", "g3_gated", "g3_hi", "g3_hid"))
        d3_step = sig("d3_step", 24)
        base_ready, sq3 = (sig(n, 4) for n in ("base_ready", "sq3"))
        ss_ready, nrm3, rs3, rsbc_ready, n3_hi, n3_h = (
            sig(n, 4) for n in ("ss_ready", "nrm3", "rs3", "rsbc_ready", "n3_hi", "n3_h"))
        n3_F = sig("n3_F", 8)
        q3_ready, q3_sb = (sig(n, 4) for n in ("q3_ready", "q3_sb"))
        lat_ready, lat_hi, lat_lo = (sig(n, 2) for n in ("lat_ready", "lat_hi", "lat_lo"))
        kv3_ready, kv3_sb = (sig(n, 8) for n in ("kv3_ready", "kv3_sb"))
        prod_dve, sum_dve = (sig(n, 8 * sum(DVE_Q)) for n in ("prod_dve", "sum_dve"))
        prod_pool = sig("prod_pool", 8 * sum(POOL_Q))
        sum_pool = sig("sum_pool", 8 * (POOL_Q[0] + 1))
        psum3_ready = sig("psum3_ready", 8)
        att3_in, att3_exp, att3 = (sig(n, 2) for n in ("att3_in", "att3_exp", "att3"))
        o3T_ready, o3_hi, o3_lo = (sig(n, 4) for n in ("o3T_ready", "o3_hi", "o3_lo"))
        wo_ready, x1_ready, sq3b = (sig(n, 4) for n in ("wo_ready", "x1_ready", "sq3b"))
        l3_logits, l3_exp_in, l3_exp, l3_gate = (
            sig(n, 2) for n in ("l3_logits", "l3_exp_in", "l3_exp", "l3_gate"))
        we_ready = sig("we_ready", 32, prime=WE_PRIME)
        we_half, we_done = (sig(n, 32) for n in ("we_half", "we_done"))
        x_final = sig("x_final", 4)

        att = [acc[u][:, :, QKV:D] for u in U]
        cw_T = [G[u][0:E1, 0:T] for u in U]
        qT = [F[u][0:HD0, 0, :] for u in U]
        kT = [F[u][0:HD0, 1, :] for u in U]
        s_off = [0, 128, 384, 768]
        pT_sb = [[base[u][:, 0, 0:128], base[u][:, 0, 128:384], base[u][:, 1, 0:384],
                  G[u][:, 1280:1792]] for u in U]
        l1w = VW[:].rearrange("p a n -> p (a n)").rearrange("p (g n) -> p g n", g=COND)
        q3 = [acc[u][:].rearrange("p t (h d) -> p t h d", d=HD3) for u in U]
        kv3 = [VW[:, u, :].rearrange("p (t n) -> p t n", t=NT) for u in U]
        att3_p = [F[u][:].rearrange("p k n -> p (k n)").rearrange("p (t h g) -> p t h g", t=NT, h=HEADS) for u in U]
        def quarter3(t):
            return t.rearrange("p (h a b) -> p h a b", h=HQ, a=16)

        prod3 = [quarter3(G[0][:, 1024 * j:1024 * j + 1024]) for j in U]
        prod3_pool = [[quarter3(VW[:, 1, 0:1024]), quarter3(G[1][:, 1024:2048])],
                      [quarter3(G[1][:, 0:1024]), quarter3(G[1][:, 1024:2048]),
                       quarter3(VW[:, 0, 0:1024]), quarter3(VW[:, 0, 1024:2048])]]
        pool_pair3 = [h.rearrange("p (n b) -> p n b", b=16) for h in (G[1][:], VW[:, 0, :])]
        PS3 = [B(1, 2), B(1, 3)]
        SWEEP3 = [(u, phase, t) for u in U for phase in ("scores", "values") for t in range(NT)]
        lat_p = [[hid_hi[u][0:L3LAT, 0, :], hid_hi[u][0:L3LAT, 1, :]] for u in U]

        def tok(t):
            return slice(t * P, (t + 1) * P)

        def mm3(out, sh, sl, mh, ml, first, last, begin=False):
            i = nc.tensor.matmul(out, sh, mh, start=first, stop=False)
            if begin:
                i.then_inc(w_begun.sem, 1)
            nc.tensor.matmul(out, sh, ml, start=False, stop=False)
            return nc.tensor.matmul(out, sl, mh, start=False, stop=last)

        PB = [(B(0, 0), B(0, 1)), (B(1, 0), B(1, 1))]
        LG3 = [B(1, 0), B(0, 2)]
        gelu3 = [G[1][:, 512 * i:512 * i + T] for i in U]

        def gated3(i):
            return F[i % 2][:, (i // 2) % 2, :] if i < TILES3 // 2 else F[1][:, i % 2, :]

        def slot3(i):
            return 2 * (STEPS3[i // 2][1] % 2) + i % 2

        def steps_of(u):
            return [n for n, st3 in enumerate(STEPS3) if st3[2] == u]

        def slot_free3(i):
            mine = steps_of(STEPS3[i // 2][2])
            k = mine.index(i // 2)
            return mine[k - 2] + 1 if k >= 2 else 0

        def dve_products(n):
            return sum(DVE_Q[u] for u, _, _ in SWEEP3[:n])

        def pool_products(n):
            return sum(POOL_Q[u] for u, _, _ in SWEEP3[:n])

        def pool_sums(n):
            return sum(POOL_Q[u] if u == 0 else 1 for u, _, _ in SWEEP3[:n])

        def product3(eng, dst, quarter, u, phase, t):
            hs, shape = slice(HQ * quarter, HQ * quarter + HQ), [P, HQ, 16, 16]
            if phase == "scores":
                a = q3[u][:, t, hs, :].unsqueeze(2).broadcast_to(shape)
                b = kv3[u][:, t, 0:D].rearrange("p (g d) -> p g d", d=HD3).unsqueeze(1).broadcast_to(shape)
            else:
                a = att3_p[u][:, t, hs, :].unsqueeze(2).broadcast_to(shape)
                b = kv3[u][:, t, D:2 * D].rearrange("p (g d) -> p d g", d=HD3).unsqueeze(1).broadcast_to(shape)
            return eng.tensor_tensor(dst, a, b, ALU.mult)

        block = ctx.enter_context(nc.Block())

        @block.sync
        def _(sp):
            sp.dma_start(cond[:].rearrange("p b g -> p (b g)"), A["cond"]).then_inc(cond_in.sem, 16)
            for dst, name in ((ident[:], "ident"), (vecs[:], "vecs"), (rows[:], "rows")):
                sp.dma_start(dst, A[name]).then_inc(const_in.sem, 16)
            sp.wait_ge(idx_ready.sem, 1)
            with sp.Fori(0, PAIRS) as it:
                def chunk(c, src, n):
                    sp.wait_ge(*w_ready(it, c + 1 - RAW_SLOTS))
                    sp.dma_start(raw[c % 2][:, 0:n], src).then_inc(raw_in[c % 2].sem, 16)

                top1 = [sp.value_load(cidx[0:1, bass.ds(2 * it + u, 1), 0:1], min_val=0, max_val=COND - 1)
                        for u in U]
                for u in U:
                    sp.dma_start(l0b[u][:], A["l0b"][bass.ds(top1[u], 1)]).then_inc(l0b_in[u].sem, 16)
                for c in range(3):
                    for u in U:
                        chunk(C_L0C + 2 * c + u, A["l0c"][bass.ds(top1[u], 1), c], 1024)
                for c in range(4):
                    chunk(C_QKV + c, A["qkv"][c], 1536)
                sp.dma_start(VW[:].rearrange("p a n -> p (a n)"), A["l1w"]).then_inc(l1w_in.sem, 16)
                for c in range(2):
                    chunk(C_O0 + c, A["o0"][c], 1024)
                for e in range(E1):
                    chunk(C_L1 + e, A["l1"][e], 1024)
                chunk(C_L2L, A["l2l"], 512)
                chunk(C_L2C, A["l2c"], 512)
                for c in range(4):
                    chunk(C_L2F + c, A["l2"][c], 1024)
                top = [[sp.value_load(cidx[0:1, bass.ds(2 * it + u, 1), j:j + 1], min_val=0, max_val=COND - 1)
                        for j in range(2)] for u in U]
                for n, (j, c, u) in enumerate(STEPS3):
                    chunk(chunk3(n), A["shared"][c] if j == 2 else A["skill"][bass.ds(top[u][j], 1), c], 1536)
                    if chunk3(n) + 1 == C_L3P0:
                        chunk(C_L3P0, A["l3p"], 1152)
                chunk(C_L3P1, A["l3p"], 1152)
                chunk(C_L3E, A["l3oe"], 1536)
                for c in range(1, 4):
                    chunk(C_L3E + c, A["l3e"][c - 1], 1024)

        @block.gpsimd
        def _(pool):
            pool.wait_ge(const_in.sem, 16 * 9)
            pool.sem_inc(w_ready.sem, PRIME)
            pool.tensor_copy(sm_hi[:], small).then_inc(prep_pool.sem, 1)
            pool.wait_ge(prep_pool.sem, 1)
            pool.tensor_tensor(sm_lo[:], small, sm_hi[:].bitcast(F32), ALU.subtract).then_inc(prep_pool.sem, 1)
            with pool.Fori(0, PAIRS) as it:
                hi_made = [0]

                def split(c, n):
                    s = c % W_SLOTS
                    if c in ACT_SPLIT:
                        pool.wait_ge(*w_hi_act(it, ACT_SPLIT.index(c) + 1))
                        pool.wait_ge(*w_ready(it, c))
                    else:
                        pool.wait_ge(*raw_in[c % 2](it, c // 2 + 1))
                        pool.wait_ge(*w_begun(it, begun_before(c)))
                        if c < 4:
                            pool.wait_ge(*we_ready(it, WE_LAST + 4 * c))
                        pool.sem_inc(passed.sem, 1)
                        nc.gpsimd.tensor_copy(w_hi[s][:, 0:n], raw[c % 2][:, 0:n]).then_inc(w_hi_ready.sem, 1)
                        hi_made[0] += 1
                        pool.wait_ge(*w_hi_ready(it, hi_made[0]))
                    nc.gpsimd.tensor_tensor(w_lo[s][:, 0:n], raw[c % 2][:, 0:n], w_hi[s][:, 0:n].bitcast(F32),
                                            ALU.subtract).then_inc(w_ready.sem, 1)

                def attention3(n):
                    u, phase, t = SWEEP3[n]
                    if phase == "scores":
                        if t == 0:
                            pool.wait_ge(*q3_sb(it, 2 * u + 2))
                        pool.wait_ge(*kv3_sb(it, 4 * u + t + 1))
                    elif t == 0:
                        pool.wait_ge(*att3(it, u + 1))
                    for k in range(POOL_Q[u]):
                        p = pool_products(n) + k
                        if p > 0:
                            pool.wait_ge(*prod_pool(it, p))
                            if 1 < p <= pool_products(8) + 1:
                                pool.wait_ge(*sum_pool(it, min(p - 1, pool_sums(8))))
                            if n >= 10:
                                pool.wait_ge(*psum3_ready(it, n - 9))
                        product3(nc.gpsimd, prod3_pool[u][p % (2 * u + 2)], DVE_Q[u] + k, u, phase,
                                 t).then_inc(prod_pool.sem, 1)

                sweeps = {C_L3B + 1: (0,), C_L3B + 2: (1,), C_L3B + 4: (2,), C_L3B + 5: (3,), C_L3B + 6: (4,),
                          C_L3B + 7: (5,), C_L3P1: (6,), C_L3E: (7,), C_L3E + 2: (8, 9, 10, 11),
                          C_L3E + 3: range(12, 16)}
                for c in range(CHUNKS):
                    split(c, A["widths"][c])
                    for n in sweeps.get(c, ()):
                        pool.wait_ge(*w_ready(it, c + 1))
                        attention3(n)
                    if c in sweeps:
                        pool.wait_ge(*prod_pool(it, pool_products(sweeps[c][-1] + 1)))
                        pool.sem_inc(passed.sem, 1)

        @block.tensor
        def _(pe):
            pe.wait_ge(const_in.sem, 16 * 9)
            pe.sem_inc(w_begun.sem, PRIME)
            pe.sem_inc(we_ready.sem, WE_PRIME)
            pe.wait_ge(prep.sem, PREP_COND + 1)
            for k in range(KD):
                mm = nc.tensor.matmul(bank[0][:, 0:E0], ones[:], simn[:, k, :], start=k == 0, stop=k == KD - 1)
            mm.then_inc(prep_pe.sem, 1)
            pe.wait_ge(prep.sem, PREP_STEPS)
            with pe.Fori(0, PAIRS) as it:
                def weights(c):
                    pe.wait_ge(*w_ready(it, c + 1))
                    return w_hi[c % W_SLOTS], w_lo[c % W_SLOTS]

                for cc in range(2):
                    for u in U:
                        if cc == 0:
                            pe.wait_ge(*x_pair(it, u + 1))
                        c = C_L0C + 2 * cc + u
                        wh, wl = weights(c)
                        for ml in range(2):
                            if cc == 1:
                                pe.wait_ge(*l0_gated(it, 2 * u + ml + 1))
                            for j, ready in ((0, up_ready), (1, gate_ready)):
                                for k in range(KD):
                                    cols = slice(512 * j + 256 * k + P * ml, 512 * j + 256 * k + P * ml + P)
                                    mm = mm3(B(u, 2 * ml + j)[:], wh[:, cols], wl[:, cols],
                                             x_hi[u][:, k, :], x_lo[u][:, k, :], k == 0, k == KD - 1,
                                             begin=ml == 0 and j == 0 and k == 0)
                                mm.then_inc(ready.sem, 1)
                for u in U:
                    wh, wl = weights(C_L0C + 4 + u)
                    pe.wait_ge(*hid_ready(it, 4 + 2 * u + 2))
                    for m in range(KD):
                        for k in range(4):
                            cols = slice(D * k + P * m, D * k + P * m + P)
                            mm = mm3(B(u, m)[:], wh[:, cols], wl[:, cols], hid_hi[u][:, k, :], hid_lo[u][:, k, :],
                                     k == 0, k == 3, begin=m == 0 and k == 0)
                        mm.then_inc(l0_down.sem, 1)
                for u in U:
                    pe.wait_ge(*l0_h(it, 2 * u + 2))
                    for t in range(NT):
                        for k in range(KD):
                            mm3(B(u, 2)[:, 16 * t:16 * t + 16], h_hi[u][:, k, tok(t)], h_lo[u][:, k, tok(t)],
                                small_at(sm_hi, "sim", k, E0), small_at(sm_lo, "sim", k, E0), k == 0, k == KD - 1)
                    for t in range(NT):
                        for k in range(KD):
                            mm = nc.tensor.matmul(B(u, 2)[:, 64 + t:65 + t], F[u][:, k, tok(t)], ones[:, 0:1],
                                                  start=k == 0, stop=k == KD - 1)
                    mm.then_inc(l0_logits.sem, 1)
                for g in range(8):
                    wh, wl = weights(C_QKV + g // 2)
                    for u in U:
                        for t in range(NT):
                            if g > 0:
                                pe.wait_ge(*qkv_done(it, 8 * (g - 1) + 4 * u + t + 1))
                            elif t == 2:
                                pe.wait_ge(*l0_rw(it, u + 1))
                            for k in range(KD):
                                cols = slice(768 * k + 384 * (g % 2), 768 * k + 384 * (g % 2) + 384)
                                mm = mm3(B(u, t)[:, 0:384], h_hi[u][:, k, tok(t)], h_lo[u][:, k, tok(t)],
                                         wh[:, cols], wl[:, cols], k == 0, k == KD - 1,
                                         begin=g % 2 == 0 and u == 0 and t == 0 and k == 0)
                            mm.then_inc(qkv_ready.sem, 1)
                for u in U:
                    pe.wait_ge(*qkv_done(it, 56 + 4 * u + 4))
                    pe.sem_inc(passed.sem, 1)
                    for j in range(2):
                        for t in range(NT):
                            mm = nc.tensor.transpose(B(u, j)[0:HD0, tok(t)], acc[u][:, t, HD0 * j:HD0 * (j + 1)],
                                                     ident[:])
                        mm.then_inc(qkT_ready.sem, 1)
                for u in U:
                    pe.wait_ge(*qkT_sb(it, 2 * u + 2))
                    for i in range(NT):
                        n = P * (i + 1)
                        nc.tensor.matmul(B(u, (i + 2) % 4)[:, 0:n], qT[u][:, tok(i)], kT[u][:, 0:n],
                                         start=True, stop=True).then_inc(s0_ready.sem, 1)
                for u in U:
                    for i in range(NT):
                        pe.wait_ge(*s0_p(it, 4 * u + i + 1))
                        for j in range(i + 1):
                            o = s_off[i] + P * j
                            mm = nc.tensor.transpose(B(u, (i + 2) % 4)[:, tok(j)], G[u][:, o:o + P], ident[:])
                        mm.then_inc(s0_pT.sem, 1)
                for u in U:
                    for i in range(NT):
                        pe.wait_ge(*s0_pT_sb(it, 4 * u + i + 1))
                        for j in range(i + 1):
                            mm = nc.tensor.matmul(B(u, (i + 2) % 4)[:, 0:HD0], pT_sb[u][i][:, tok(j)],
                                                  acc[u][:, j, 2 * HD0:3 * HD0], start=j == 0, stop=j == i)
                        mm.then_inc(o0_ready.sem, 1)
                for r in range(2):
                    wh, wl = weights(C_O0 + r)
                    for u in U:
                        for k in range(4):
                            pe.wait_ge(*mixed(it, 8 * r + 4 * u + 4))
                            if k == 0 and r == 0:
                                pe.wait_ge(*att0(it, 4 * u + 4))
                            elif k >= 2:
                                pe.wait_ge(*mix_lo(it, 8 * r + 4 * u + k - 1))
                            elif r == 1:
                                pe.wait_ge(*mix_lo(it, 4 * u + k + 3))
                            for t in range(NT):
                                mm = nc.tensor.transpose(B(u, k % 2)[:, tok(t)],
                                                         G[u][:, 512 * t + P * k:512 * t + P * (k + 1)], ident[:])
                            mm.then_inc(mixT_ready.sem, 1)
                    for u in U:
                        pe.wait_ge(*mix_lo(it, 8 * r + 4 * u + 4))
                        for m in range(KD):
                            for k in range(4):
                                cols = slice(D * k + P * m, D * k + P * m + P)
                                mm = mm3(B(u, 2 + m)[:], wh[:, cols], wl[:, cols], hid_hi[u][:, k, :],
                                         hid_lo[u][:, k, :], r == 0 and k == 0, r == 1 and k == 3,
                                         begin=u == 0 and m == 0 and k == 0)
                        mm.then_inc(oproj0.sem, 1)
                for u in U:
                    pe.wait_ge(*wbot_ready(it, u + 1))
                    pe.wait_ge(*x_pair(it, 2 + u + 1))
                    for m in range(KD):
                        for k in range(KD):
                            cols = slice(D * k + P * m, D * k + P * m + P)
                            mm = mm3(B(u, m)[:], hid_hi[u][:, 0, cols], hid_lo[u][:, 0, cols], x_hi[u][:, k, :],
                                     x_lo[u][:, k, :], k == 0, k == KD - 1)
                        mm.then_inc(l1c_ready.sem, 1)
                for u in U:
                    pe.wait_ge(*l1c_h(it, 2 * u + 2))
                    for t in range(NT):
                        for k in range(KD):
                            mm = mm3(B(u, 2)[:, 16 * t:16 * t + 16], h_hi[u][:, k, tok(t)], h_lo[u][:, k, tok(t)],
                                     small_at(sm_hi, "router", k, E1), small_at(sm_lo, "router", k, E1),
                                     k == 0, k == KD - 1)
                    mm.then_inc(l1_logits.sem, 1)

                def l1_hidden(e, u):
                    wh, wl = weights(C_L1 + e)
                    if e > 0:
                        pe.wait_ge(*e1_relu(it, 4 * (e - 1) + 2 * u + 2))
                    for m in range(KD):
                        for k in range(KD):
                            cols = slice(D * k + P * m, D * k + P * m + P)
                            mm = mm3(B(u, m)[:], wh[:, cols], wl[:, cols], h_hi[u][:, k, :], h_lo[u][:, k, :],
                                     k == 0, k == KD - 1, begin=u == 0 and m == 0 and k == 0)
                    mm.then_inc(e1_hid_ready.sem, 1)

                def l1_out(e, u):
                    wh, wl = weights(C_L1 + e)
                    pe.wait_ge(*e1_hid(it, 2 * e + u + 1))
                    for tp in range(2):
                        if e > 0:
                            pe.wait_ge(*e1_sum(it, 8 * (e - 1) + 4 * u + 2 * tp + 2))
                        for t in (2 * tp, 2 * tp + 1):
                            for k in range(KD):
                                cols = slice(512 + D * k, 512 + D * k + D)
                                mm = mm3(B(u, 2 + tp)[:, D * (t % 2):D * (t % 2) + D],
                                         hid_hi[u][:, 2 * (e % 2) + k, tok(t)], hid_lo[u][:, 2 * (e % 2) + k, tok(t)],
                                         wh[:, cols], wl[:, cols], k == 0, k == KD - 1)
                        mm.then_inc(e1_y_ready.sem, 1)

                for u in U:
                    l1_hidden(0, u)
                for u in U:
                    pe.wait_ge(*l1_cw(it, u + 1))
                    for t in range(NT):
                        mm = nc.tensor.transpose(B(u, 2)[0:E1, tok(t)], rw[u][:, t, :], ident[:])
                    mm.then_inc(cwT_ready.sem, 1)
                for u in U:
                    pe.wait_ge(*cwT_sb(it, u + 1))
                    for t in range(NT):
                        mm = nc.tensor.matmul(B(u, 2 + t // 2)[:, D * (t % 2):D * (t % 2) + D], cw_T[u][:, tok(t)],
                                              b2rows[:], start=True, stop=True)
                    mm.then_inc(b2_ready.sem, 1)
                for u in U:
                    pe.wait_ge(*acc1_init(it, u + 1))
                for e in range(E1):
                    for u in U:
                        if e + 1 < E1:
                            l1_hidden(e + 1, u)
                        l1_out(e, u)
                for u in U:
                    pe.wait_ge(*e1_sum(it, 8 * (E1 - 1) + 4 * u + 4))
                    for m in range(KD):
                        for t in range(NT):
                            mm = nc.tensor.transpose(B(u, m)[:, tok(t)], acc[u][:, t, P * m:P * m + P], ident[:])
                        mm.then_inc(accT_ready.sem, 1)
                lh, ll = weights(C_L2L)
                for u in U:
                    pe.wait_ge(*x_pair(it, 4 + u + 1))
                    for k in range(KD):
                        cols = slice(P * k, P * k + P)
                        mm = mm3(B(u, 2)[:], lh[:, cols], ll[:, cols], x_hi[u][:, k, :], x_lo[u][:, k, :], k == 0,
                                 k == KD - 1, begin=u == 0 and k == 0)
                    mm.then_inc(hA_ready.sem, 1)
                    if u == 0:
                        wh, wl = weights(C_L2C)
                    for m in range(KD):
                        for k in range(KD):
                            cols = slice(D * k + P * m, D * k + P * m + P)
                            mm3(B(u, m)[:], wh[:, cols], wl[:, cols], x_hi[u][:, k, :], x_lo[u][:, k, :], k == 0,
                                False, begin=u == 0 and m == 0 and k == 0)
                for u in U:
                    pe.wait_ge(*hA(it, u + 1))
                    for m in range(KD):
                        cols = slice(D + P * m, D + P * m + P)
                        mm3(B(u, m)[:], lh[:, cols], ll[:, cols], hid_hi[u][:, 0, :], hid_lo[u][:, 0, :], False,
                            True).then_inc(l2c_ready.sem, 1)
                for u in U:
                    pe.wait_ge(*l2c_h(it, 2 * u + 2))
                    for k in range(KD):
                        mm = mm3(B(u, 2)[:], small_at(sm_hi, "wr", k, P), small_at(sm_lo, "wr", k, P),
                                 h_hi[u][:, k, :], h_lo[u][:, k, :], k == 0, k == KD - 1)
                    mm.then_inc(sc_ready.sem, 1)
                def l2_down(m, u):
                    wh, wl = weights(C_L2F + m // 2)
                    pe.wait_ge(*f2_hid(it, 2 * m + u + 1))
                    if m == 0:
                        pe.wait_ge(*sc_sb(it, u + 1))
                    for n in range(KD):
                        cols = slice(512 + D * (m % 2) + P * n, 512 + D * (m % 2) + P * n + P)
                        mm = mm3(B(u, 2 + n)[:], wh[:, cols], wl[:, cols], hid_hi[u][:, m % 4, :],
                                 hid_lo[u][:, m % 4, :], m == 0, m == 7)
                    mm.then_inc(f2_down.sem, 1)

                for m in range(8):
                    for u in U:
                        wh, wl = weights(C_L2F + m // 2)
                        if m >= 2:
                            pe.wait_ge(*f2_gelu(it, 2 * (m - 2) + u + 1))
                        else:
                            pe.wait_ge(*l2c_x(it, 2 * u + m + 1))
                        for k in range(KD):
                            cols = slice(D * k + P * (m % 2), D * k + P * (m % 2) + P)
                            mm = mm3(B(u, m % 2)[:], wh[:, cols], wl[:, cols], h_hi[u][:, k, :], h_lo[u][:, k, :],
                                     k == 0, k == KD - 1, begin=m % 2 == 0 and u == 0 and k == 0)
                        mm.then_inc(f2_ready.sem, 1)
                        if m >= 1:
                            l2_down(m - 1, u)
                for u in U:
                    l2_down(7, u)
                for u in U:
                    pe.wait_ge(*wtok_ready(it, u + 1))
                    for t in range(NT):
                        mm = nc.tensor.matmul(B(u, 0)[:, tok(t)], st[u][:, 5, t:t + 1].broadcast_to([P, P]),
                                              ident[:], start=True, stop=True)
                    mm.then_inc(wbc_ready.sem, 1)

                def l3_up(i):
                    j, c, u = STEPS3[i // 2]
                    ml = i % 2
                    wh, wl = weights(chunk3(i // 2))
                    if i >= 2:
                        pe.wait_ge(*g3_gated(it, i - 1))
                    for kind, ready in ((0, g3_ready), (1, u3_ready)):
                        for k in range(KD):
                            cols = slice(512 * kind + D * k + P * ml, 512 * kind + D * k + P * ml + P)
                            mm = mm3(PB[ml][kind][:], wh[:, cols], wl[:, cols], x_hi[u][:, k, :], x_lo[u][:, k, :],
                                     k == 0, k == KD - 1,
                                     begin=ml == 0 and kind == 0 and k == 0)
                        mm.then_inc(ready.sem, 1)

                def l3_down(i):
                    j, c, u = STEPS3[i // 2]
                    ml = i % 2
                    wh, wl = weights(chunk3(i // 2))
                    pe.wait_ge(*g3_hid(it, i + 1))
                    for m in range(KD):
                        cols = slice(1024 + D * ml + P * m, 1024 + D * ml + P * m + P)
                        mm = mm3(B(u, 2 + m)[:], wh[:, cols], wl[:, cols], hid_hi[u][:, slot3(i), :],
                                 hid_lo[u][:, slot3(i), :], i == 2 * steps_of(u)[0],
                                 i == 2 * steps_of(u)[-1] + 1)
                    if ml == 1:
                        mm.then_inc(d3_step.sem, 1)

                def norm_stats(x, u):
                    for t in range(NT):
                        for k in range(KD):
                            mm = nc.tensor.matmul(x[:, t:t + 1], F[u][:, k, tok(t)], ones[:, 0:1],
                                                  start=k == 0, stop=k == KD - 1)
                    mm.then_inc(ss_ready.sem, 1)

                def norm_row(i, y, u):
                    pe.wait_ge(*rs3(it, 2 * i + u + 1))
                    for t in range(NT):
                        mm = nc.tensor.matmul(y[:, tok(t)], st[u][:, 2, t:t + 1].broadcast_to([P, P]),
                                              ident[:], start=True, stop=True)
                    mm.then_inc(rsbc_ready.sem, 1)

                def queries(u, tp, dst, wh, wl):
                    for t in (2 * tp, 2 * tp + 1):
                        for k in range(KD):
                            mm = mm3(dst[:, D * (t % 2):D * (t % 2) + D], h_hi[u][:, k, tok(t)],
                                     h_lo[u][:, k, tok(t)], wh[:, D * k:D * k + D], wl[:, D * k:D * k + D],
                                     k == 0, k == KD - 1)
                    mm.then_inc(q3_ready.sem, 1)

                def keys_values(u, t, dst, wh, wl):
                    lh, ll = lat_p[u]
                    mm3(dst[:], lh[:, tok(t)], ll[:, tok(t)], wh[0:L3LAT, 640:640 + 2 * D],
                        wl[0:L3LAT, 640:640 + 2 * D], True, True).then_inc(kv3_ready.sem, 1)

                def project3(u, i):
                    x, y = B(u, 2), B(u, 3)
                    if i == 0:
                        pe.wait_ge(*sq3(it, 2 * u + 2))
                        norm_stats(x, u)
                    if i == 1:
                        norm_row(0, y, u)
                    if i < 4:
                        return
                    wh, wl = weights((C_L3P0, C_L3P1)[u])
                    if i == 4:
                        pe.wait_ge(*n3_h(it, u + 1))
                        pe.sem_inc(passed.sem, 1)
                        for k in range(KD):
                            cols = slice(512 + L3LAT * k, 512 + L3LAT * k + L3LAT)
                            w3h, w3l = (w[(C_L3P0, C_L3P1)[u] % W_SLOTS] for w in (w_hi, w_lo))
                            mm = nc.tensor.matmul(x[0:L3LAT, :], w3h[:, cols], h_hi[u][:, k, :], start=k == 0,
                                                  stop=False)
                            if k == 0:
                                mm.then_inc(w_begun.sem, 1)
                            nc.tensor.matmul(x[0:L3LAT, :], w3h[:, cols], h_lo[u][:, k, :], start=False, stop=False)
                            mm = nc.tensor.matmul(x[0:L3LAT, :], w3l[:, cols], h_hi[u][:, k, :], start=False,
                                                  stop=k == KD - 1)
                        mm.then_inc(lat_ready.sem, 1)
                        queries(u, 0, y, wh, wl)
                    if i == 5:
                        pe.wait_ge(*lat_lo(it, u + 1))
                        queries(u, 1, x, wh, wl)
                        pe.wait_ge(*q3_sb(it, 2 * u + 1))
                        keys_values(u, 0, y, wh, wl)
                    if i == 6:
                        pe.wait_ge(*q3_sb(it, 2 * u + 2))
                        keys_values(u, 1, x, wh, wl)
                        pe.wait_ge(*kv3_sb(it, 4 * u + 1))
                        keys_values(u, 2, y, wh, wl)
                    if i == 7:
                        pe.wait_ge(*kv3_sb(it, 4 * u + 2))
                        keys_values(u, 3, x, wh, wl)

                def pool_sum3(n):
                    pe.wait_ge(*prod_pool(it, pool_products(n + 1)))
                    if n >= 10:
                        pe.wait_ge(*sum_pool(it, pool_sums(n - 1)))
                    for d in range(HD3):
                        mm = nc.tensor.matmul(PS3[n % 2][:, 0:P], ident[:], pool_pair3[n % 2][:, :, d],
                                              start=d == 0, stop=d == HD3 - 1)
                    mm.then_inc(psum3_ready.sem, 1)

                def finish3(u, i):
                    if i == 0:
                        pe.wait_ge(*sum_pool(it, pool_sums(8 * u + 8)))
                        pe.wait_ge(*sum_dve(it, dve_products(8 * u + 8)))
                        pe.sem_inc(passed.sem, 1)
                        for m in range(KD):
                            for t in range(NT):
                                mm = nc.tensor.transpose(B(u, m)[:, tok(t)], acc[u][:, t, P * m:P * m + P], ident[:])
                            mm.then_inc(o3T_ready.sem, 1)
                    if i == 1:
                        wh, wl = weights(C_L3E)
                        pe.wait_ge(*o3_lo(it, 2 * u + 2))
                        pe.wait_ge(*kv3_sb(it, 4 * u + 4))
                        for m in range(KD):
                            for k in range(KD):
                                cols = slice(D * k + P * m, D * k + P * m + P)
                                mm = mm3(B(u, 2 + m)[:], wh[:, cols], wl[:, cols], x_hi[u][:, k, :],
                                         x_lo[u][:, k, :], k == 0, k == KD - 1,
                                         begin=u == 0 and m == 0 and k == 0)
                            mm.then_inc(wo_ready.sem, 1)
                    if i == 2:
                        pe.wait_ge(*sq3b(it, 2 * u + 2))
                        norm_stats(B(u, 0), u)
                    if i == 3:
                        norm_row(1, B(u, 1), u)
                    if i == 4:
                        pe.wait_ge(*n3_h(it, 2 + u + 1))
                        for t in range(NT):
                            for k in range(KD):
                                mm = mm3(LG3[u][:, E3 * t:E3 * t + E3], h_hi[u][:, k, tok(t)],
                                         h_lo[u][:, k, tok(t)], small_at(sm_hi, "wg", k, E3),
                                         small_at(sm_lo, "wg", k, E3), k == 0, k == KD - 1)
                        mm.then_inc(l3_logits.sem, 1)
                    if 5 <= i < 9:
                        for c in (i - 5,):
                            wh, wl = weights(C_L3E + c)
                            o = 512 if c == 0 else 0
                            for t in range(NT):
                                if c > 0:
                                    pe.wait_ge(*we_done(it, 16 * u + 4 * (c - 1) + t + 1))
                                elif t == 0:
                                    pe.wait_ge(*n3_F(it, 2 * (2 + u) + 2))
                                for k in range(KD):
                                    cols = slice(o + 512 * k, o + 512 * k + 512)
                                    mm = mm3(B(u, t)[:], h_hi[u][:, k, tok(t)], h_lo[u][:, k, tok(t)],
                                             wh[:, cols], wl[:, cols], k == 0, k == KD - 1,
                                             begin=u == 0 and c > 0 and t == 0 and k == 0)
                                mm.then_inc(we_ready.sem, 1)
                    if i == 9:
                        pe.wait_ge(*we_done(it, 16 * u + 16))
                        for m in range(KD):
                            for t in range(NT):
                                mm = nc.tensor.transpose(B(u, m)[:, tok(t)], acc[u][:, t, P * m:P * m + P], ident[:])
                            mm.then_inc(accT_ready.sem, 1)

                for u in U:
                    pe.wait_ge(*x_pair(it, 6 + u + 1))
                for i in range(TILES3 + 2):
                    if i < TILES3:
                        l3_up(i)
                        if i >= PROJECT_TILE:
                            project3(0, i - PROJECT_TILE)
                    if i >= 2:
                        l3_down(i - 2)
                project3(1, 0)
                project3(1, 1)
                project3(1, 4)
                finish3(0, 0)
                project3(1, 5)
                finish3(0, 1)
                project3(1, 6)
                finish3(0, 2)
                project3(1, 7)
                finish3(0, 3)
                pe.wait_ge(*kv3_sb(it, 8))
                for n in range(8, 16):
                    pool_sum3(n)
                    if n < 12:
                        finish3(0, n - 4)
                    if n == 11:
                        finish3(0, 8)
                    if n == 12:
                        finish3(0, 9)
                for i in range(10):
                    finish3(1, i)

        @block.scalar
        def _(act):
            for dst, name in ((small, "small"), (cond_er[:], "cond_er"), (b2rows[:], "b2rows"), (causal[:], "causal"),
                              (before[:], "before"), (mask1[:], "mask1")):
                act.dma_start(dst, A[name]).then_inc(const_in.sem, 16)
            act.wait_ge(const_in.sem, 16 * 9)
            act.wait_ge(prep.sem, PREP_COND)
            nc.scalar.activation(cexp[:], cexp[:], ACT.Exp).then_inc(prep_act.sem, 1)
            nc.scalar.activation(sg[:], row("gates", E0), ACT.Exp, scale=-1.0).then_inc(prep_act.sem, 1)
            act.wait_ge(prep_pe.sem, 1)
            nc.scalar.activation(cs, bank[0][:, 0:E0], ACT.Sqrt).then_inc(prep_act.sem, 1)
            with act.Fori(0, PAIRS) as it:
                def store_x(u):
                    act.wait_ge(*x_final(it, 2 * u + 2))
                    act.dma_start(A["out"][2 * it + u], xT[u][:]).then_inc(out_written.sem, 16)

                def split_hi(c):
                    n = A["widths"][c]
                    act.wait_ge(*raw_in[c % 2](it, c // 2 + 1))
                    act.wait_ge(*w_begun(it, begun_before(c)))
                    if c < 4:
                        act.wait_ge(*we_ready(it, WE_LAST + 4 * c))
                    nc.scalar.activation(w_hi[c % W_SLOTS][:, 0:n], raw[c % 2][:, 0:n],
                                         ACT.Copy).then_inc(w_hi_act.sem, 1)

                for u in U:
                    act.dma_start(xT[u][:], A["x"][2 * it + u]).then_inc(x_in[u].sem, 16)
                for u in U:
                    act.wait_ge(*l0b_in[u](it, 1))
                for cc in range(2):
                    for u in U:
                        for ml in range(2):
                            m = 2 * cc + ml
                            act.wait_ge(*up_ready(it, 4 * cc + 2 * u + ml + 1))
                            if cc == 1:
                                act.wait_ge(*l0_gated(it, 2 * u + ml + 1))
                            nc.scalar.activation(acc[u][:, 2 * ml:2 * ml + 2, :].rearrange("p a n -> p (a n)"),
                                                 B(u, 2 * ml)[:], ACT.Silu,
                                                 bias=l0b[u][:, m:m + 1]).then_inc(silu_done.sem, 1)
                            if ml == 0:
                                split_hi(C_L0C + 2 + 2 * cc + u)
                for u in U:
                    for m in range(KD):
                        act.wait_ge(*l0_down(it, 2 * u + m + 1))
                        nc.scalar.activation(h_hi[u][:, m, :], B(u, m)[:], ACT.Identity,
                                             bias=l0b[u][:, 8 + m:9 + m]).then_inc(l0_h_hi.sem, 1)
                        nc.scalar.activation(F[u][:, m, :], B(u, m)[:], ACT.Square,
                                             bias=l0b[u][:, 8 + m:9 + m]).then_inc(l0_sq.sem, 1)
                for u in U:
                    act.wait_ge(*l0_logits(it, u + 1))
                    nc.scalar.activation(st[u][:, 0, :], B(u, 2)[:, 64:68], ACT.Sqrt).then_inc(l0_norm.sem, 1)
                for u in U:
                    act.wait_ge(*l0_exp_in(it, u + 1))
                    nc.scalar.activation(pe_[u][:], lg[u][:], ACT.Exp).then_inc(l0_exp.sem, 1)
                for u in U:
                    for j, dst in ((0, qT[u]), (1, kT[u])):
                        act.wait_ge(*qkT_ready(it, 2 * u + j + 1))
                        nc.scalar.activation(dst, B(u, j)[0:HD0, :], ACT.Copy).then_inc(qkT_sb.sem, 1)
                for u in U:
                    for i in range(NT):
                        act.wait_ge(*s0_max(it, 4 * u + i + 1))
                        row_i = G[u][:, s_off[i]:s_off[i] + P * (i + 1)]
                        nc.scalar.activation(row_i, row_i, ACT.Exp, bias=st[u][:, 1, i:i + 1],
                                             accum_out=st[u][:, 2, i:i + 1]).then_inc(s0_p.sem, 1)
                for u in U:
                    for i in range(NT):
                        act.wait_ge(*s0_pT(it, 4 * u + i + 1))
                        nc.scalar.activation(pT_sb[u][i], B(u, (i + 2) % 4)[:, 0:P * (i + 1)],
                                             ACT.Copy).then_inc(s0_pT_sb.sem, 1)
                for r in range(2):
                    for u in U:
                        if r == 1:
                            act.wait_ge(*oproj0(it, u + 1))
                        for k in range(4):
                            act.wait_ge(*mixT_ready(it, 8 * r + 4 * u + k + 1))
                            nc.scalar.activation(hid_hi[u][:, k, :], B(u, k % 2)[:],
                                                 ACT.Copy).then_inc(mix_hi.sem, 1)
                for u in U:
                    for m in range(KD):
                        act.wait_ge(*l1c_ready(it, 2 * u + m + 1))
                        nc.scalar.activation(h_hi[u][:, m, :], B(u, m)[:], ACT.Identity,
                                             bias=vec("l1b", m)).then_inc(l1c_hi.sem, 1)
                for u in U:
                    act.wait_ge(*l1_exp_in(it, u + 1))
                    nc.scalar.activation(pe_[u][:, :, 1:E1], lg[u][:, :, 1:E1], ACT.Exp).then_inc(l1_exp.sem, 1)

                def l1_relu(e, u):
                    act.wait_ge(*e1_hid_ready(it, 2 * e + u + 1))
                    if e > 0:
                        act.wait_ge(*e1_hid(it, 2 * (e - 1) + u + 1))
                    for m in range(KD):
                        nc.scalar.activation(F[u][:, m, :], B(u, m)[:], ACT.Relu,
                                             bias=vec("eb1", KD * e + m)).then_inc(e1_relu.sem, 1)
                    act.wait_ge(*e1_relu(it, 4 * e + 2 * u + 2))
                    if e > 1:
                        act.wait_ge(*e1_y_ready(it, 4 * (e - 2) + 2 * u + 2))
                    nc.scalar.activation(hid_hi[u][:, 2 * (e % 2):2 * (e % 2) + 2, :], F[u][:],
                                         ACT.Copy).then_inc(e1_hi.sem, 1)

                for u in U:
                    l1_relu(0, u)
                for u in U:
                    act.wait_ge(*cwT_ready(it, u + 1))
                    nc.scalar.activation(cw_T[u], B(u, 2)[0:E1, :], ACT.Copy).then_inc(cwT_sb.sem, 1)
                for u in U:
                    act.wait_ge(*b2_ready(it, u + 1))
                    nc.scalar.activation(acc[u][:, 0:2, :].rearrange("p a n -> p (a n)"), B(u, 2)[:], ACT.Copy)
                    nc.scalar.activation(acc[u][:, 2:4, :].rearrange("p a n -> p (a n)"), B(u, 3)[:],
                                         ACT.Copy).then_inc(acc1_init.sem, 1)
                for e in range(1, E1):
                    for u in U:
                        l1_relu(e, u)
                for u in U:
                    act.wait_ge(*hA_ready(it, u + 1))
                    nc.scalar.activation(hid_hi[u][:, 0, :], B(u, 2)[:], ACT.Identity,
                                         scale=pair_er[:, u:u + 1]).then_inc(hA_hi.sem, 1)
                for u in U:
                    for m in range(KD):
                        act.wait_ge(*l2c_ready(it, 2 * u + m + 1))
                        nc.scalar.activation(h_hi[u][:, m, :], B(u, m)[:], ACT.Identity,
                                             bias=vec("l2b", m)).then_inc(l2c_hi.sem, 1)
                for u in U:
                    act.wait_ge(*sc_ready(it, u + 1))
                    nc.scalar.activation(G[u][:, 0:T], B(u, 2)[:], ACT.Copy).then_inc(sc_sb.sem, 1)
                for m in range(8):
                    for u in U:
                        act.wait_ge(*f2_ready(it, 2 * m + u + 1))
                        if m >= 2:
                            act.wait_ge(*f2_hid(it, 2 * (m - 2) + u + 1))
                        nc.scalar.activation(F[u][:, m % 2, :], B(u, m % 2)[:], ACT.Gelu_apprx_tanh,
                                             bias=vec("b1", m)).then_inc(f2_gelu.sem, 1)
                for u in U:
                    act.wait_ge(*sig_in(it, u + 1))
                    nc.scalar.activation(st[u][:, 6, :], st[u][:, 3, :], ACT.Exp,
                                         scale=-1.0).then_inc(sig_exp.sem, 1)
                for u in U:
                    act.wait_ge(*wbc_ready(it, u + 1))
                    nc.scalar.activation(G[u][:, T:2 * T], B(u, 0)[:], ACT.Copy).then_inc(wbc_sb.sem, 1)
                def project3(u, i):
                    if i == -1:
                        act.wait_ge(*g3_hid(it, TILES3 // 2 * (u + 1)))
                        act.wait_ge(*d3_step(it, steps_of(u)[-1] + 1))
                        for m in range(KD):
                            nc.scalar.activation(F[u][:, m, :], B(u, 2 + m)[:], ACT.Square).then_inc(sq3.sem, 1)
                            nc.scalar.activation(base[u][:, m, :], B(u, 2 + m)[:],
                                                 ACT.Copy).then_inc(base_ready.sem, 1)
                    if i == 0:
                        norm_root(0, B(u, 2), u)
                    if i == 1:
                        norm_hi(0, u)
                    if i == 4:
                        act.wait_ge(*lat_ready(it, u + 1))
                        nc.scalar.activation(lat_p[u][0], B(u, 2)[0:L3LAT, :], ACT.Identity,
                                             bias=vec("bdown", 0)[0:L3LAT]).then_inc(lat_hi.sem, 1)

                def norm_root(i, x, u):
                    act.wait_ge(*ss_ready(it, 2 * i + u + 1))
                    nc.scalar.activation(st[u][:, 1, :], x[:, 0:NT], ACT.Sqrt, scale=1.0 / D,
                                         bias=vec("eps", 0)).then_inc(nrm3.sem, 1)

                def norm_hi(i, u):
                    n = 2 * i + u
                    act.wait_ge(*n3_F(it, 2 * n + 2))
                    nc.scalar.activation(h_hi[u][:], F[u][:], ACT.Copy).then_inc(n3_hi.sem, 1)

                def exp3(u):
                    act.wait_ge(*att3_in(it, u + 1))
                    nc.scalar.activation(att3_p[u], att3_p[u], ACT.Exp,
                                         scale=float(HD3) ** -0.5).then_inc(att3_exp.sem, 1)

                for i in range(TILES3):
                    act.wait_ge(*g3_ready(it, i + 1))
                    if i >= 2:
                        act.wait_ge(*g3_gated(it, i - 1))
                    nc.scalar.activation(gelu3[i % 2], PB[i % 2][0][:], ACT.Gelu_apprx_tanh).then_inc(g3_gelu.sem, 1)
                    for c in ACT_SPLIT3:
                        if SPLIT_TILE[c] == i:
                            split_hi(c)
                    act.wait_ge(*g3_gated(it, i + 1))
                    if slot_free3(i):
                        act.wait_ge(*d3_step(it, slot_free3(i)))
                    nc.scalar.activation(hid_hi[STEPS3[i // 2][2]][:, slot3(i), :], gated3(i),
                                         ACT.Copy).then_inc(g3_hi.sem, 1)
                    if i >= PROJECT_TILE - 1:
                        project3(0, i - PROJECT_TILE)
                    if i == EXP_TILE:
                        exp3(0)
                def output_hi(u):
                    for m in range(KD):
                        act.wait_ge(*o3T_ready(it, 2 * u + m + 1))
                        nc.scalar.activation(x_hi[u][:, m, :], B(u, m)[:], ACT.Copy).then_inc(o3_hi.sem, 1)

                def squares3(u):
                    for m in range(KD):
                        act.wait_ge(*x1_ready(it, 2 * u + m + 1))
                        nc.scalar.activation(F[u][:, m, :], base[u][:, m, :], ACT.Square).then_inc(sq3b.sem, 1)

                def gate_exp(u):
                    act.wait_ge(*l3_exp_in(it, u + 1))
                    nc.scalar.activation(pe_[u][:, :, 0:E3], lg[u][:, :, 0:E3], ACT.Exp).then_inc(l3_exp.sem, 1)

                project3(1, -1)
                project3(1, 0)
                project3(1, 1)
                project3(1, 4)
                output_hi(0)
                squares3(0)
                norm_root(1, B(0, 0), 0)
                norm_hi(1, 0)
                gate_exp(0)
                exp3(1)
                store_x(0)
                output_hi(1)
                squares3(1)
                norm_root(1, B(1, 0), 1)
                norm_hi(1, 1)
                gate_exp(1)
                store_x(1)
                act.wait_ge(*out_written(it, 2))
                act.sem_inc(passed.sem, 1)

        @block.vector
        def _(dve):
            v = nc.vector
            done = [0]

            def prepare(ins):
                done[0] += 1
                ins.then_inc(prep.sem, 1)
                dve.wait_ge(prep.sem, done[0])

            sim = small[:, S["sim"]:S["sim"] + KD * E0]
            prepare(v.memset(ones[:], 1.0))
            dve.wait_ge(cond_in.sem, 16)
            for b in range(BATCH):
                prepare(v.max(cm8[:, b, :], cond[:, b, :]))
                prepare(v.max_index(cidx[:, b, :], cm8[:, b, :], cond[:, b, :]))
            prepare(v.tensor_tensor(cexp[:], cond[:], cm8[:, :, 0:1].broadcast_to([P, BATCH, COND]), ALU.subtract))
            assert done[0] == PREP_COND
            v.tensor_copy(ct[:, :, 7:8], cm8[:, :, 0:1]).then_inc(idx_ready.sem, 1)
            dve.wait_ge(const_in.sem, 16 * 9)
            prepare(v.tensor_tensor(simn.rearrange("p k e -> p (k e)"), sim, sim, ALU.mult))
            dve.wait_ge(prep_act.sem, 1)
            prepare(v.tensor_reduce(ct[:, :, 0:1], cexp[:], AX.X, ALU.add))
            prepare(v.reciprocal(ct[:, :, 1:2], ct[:, :, 0:1]))
            prepare(v.tensor_tensor(cexp[:], cexp[:], ct[:, :, 1:2].broadcast_to([P, BATCH, COND]), ALU.mult))
            for b in range(BATCH):
                prepare(v.max(cm8[:, b, :], cexp[:, b, :]))
            prepare(v.tensor_tensor(ct[:, :, 2:3], cm8[:, :, 0:1], cm8[:, :, 1:2], ALU.add))
            prepare(v.reciprocal(ct[:, :, 3:4], ct[:, :, 2:3]))
            prepare(v.tensor_tensor(skw[:], cm8[:, :, 0:2], ct[:, :, 3:4].broadcast_to([P, BATCH, 2]), ALU.mult))
            dve.wait_ge(prep_act.sem, 3)
            prepare(v.tensor_scalar(sg[:], sg[:], 1.0, None, ALU.add))
            prepare(v.reciprocal(sg[:], sg[:]))
            prepare(v.tensor_scalar(cs, cs, 1e-12, None, ALU.max))
            prepare(v.reciprocal(cs, cs))
            for k in range(KD):
                prepare(v.tensor_tensor(simn[:, k, :], small_at(small, "sim", k, E0), cs, ALU.mult))
            dve.wait_ge(prep_pool.sem, 2)
            at = slice(S["sim"], S["sim"] + KD * E0)
            prepare(v.tensor_copy(sm_hi[:, at], simn.rearrange("p k e -> p (k e)")))
            prepare(v.tensor_tensor(sm_lo[:, at], simn.rearrange("p k e -> p (k e)"), sm_hi[:, at].bitcast(F32),
                                    ALU.subtract))
            assert done[0] == PREP_STEPS, done[0]

            with dve.Fori(0, PAIRS) as it:
                n_step = [0]

                def step(ins):
                    n_step[0] += 1
                    ins.then_inc(dve_step.sem, 1)
                    dve.wait_ge(*dve_step(it, n_step[0]))

                def step_hold(ins):
                    step(ins)
                    dve.sem_inc(passed.sem, 1)

                def bc(col, n):
                    return col.unsqueeze(2).broadcast_to([P, NT, n])

                def split_x(layer, u):
                    step(v.tensor_copy(x_hi[u][:], xT[u][:]))
                    v.tensor_tensor(x_lo[u][:], xT[u][:], x_hi[u][:].bitcast(F32),
                                    ALU.subtract).then_inc(x_pair.sem, 1)

                step(v.tensor_copy(pair_cond[:], cond[:, bass.ds(2 * it, 2), :]))
                step(v.tensor_scalar(pair_er[:], cond_er[:, bass.ds(2 * it, 2)], SCALING2, None, ALU.mult))
                step(v.tensor_copy(pair_skw[:], skw[:, bass.ds(2 * it, 2), :]))
                for u in U:
                    dve.wait_ge(*x_in[u](it, 1))
                    split_x(0, u)
                for u in U:
                    dve.wait_ge(*l0b_in[u](it, 1))
                for cc in range(2):
                    for u in U:
                        for ml in range(2):
                            n, m = 4 * cc + 2 * u + ml, 2 * cc + ml
                            dve.wait_ge(*gate_ready(it, n + 1))
                            dve.wait_ge(*silu_done(it, n + 1))
                            v.scalar_tensor_tensor(
                                F[u][:, ml, :], B(u, 2 * ml + 1)[:], l0b[u][:, 4 + m:5 + m],
                                acc[u][:, 2 * ml:2 * ml + 2, :].rearrange("p a n -> p (a n)"), ALU.add,
                                ALU.mult).then_inc(l0_gated.sem, 1)
                            dve.wait_ge(*l0_gated(it, n + 1))
                            v.tensor_copy(hid_hi[u][:, m, :], F[u][:, ml, :]).then_inc(hid_hi_ready.sem, 1)
                            dve.wait_ge(*hid_hi_ready(it, n + 1))
                            v.tensor_tensor(hid_lo[u][:, m, :], F[u][:, ml, :], hid_hi[u][:, m, :].bitcast(F32),
                                            ALU.subtract).then_inc(hid_ready.sem, 1)
                for u in U:
                    for m in range(KD):
                        dve.wait_ge(*l0_sq(it, 2 * u + m + 1))
                        v.scalar_tensor_tensor(h_lo[u][:, m, :], B(u, m)[:], l0b[u][:, 8 + m:9 + m],
                                               h_hi[u][:, m, :].bitcast(F32), ALU.add,
                                               ALU.subtract).then_inc(l0_h.sem, 1)
                for u in U:
                    m0 = m8[u][:, :, 0]
                    dve.wait_ge(*l0_norm(it, u + 1))
                    step(v.tensor_scalar(st[u][:, 0, :], st[u][:, 0, :], 1e-12, None, ALU.max))
                    step(v.reciprocal(st[u][:, 1, :], st[u][:, 0, :]))
                    step(v.tensor_tensor(lg[u][:], B(u, 2)[:, 0:64].rearrange("p (t e) -> p t e", t=NT),
                                         bc(st[u][:, 1, :], E0), ALU.mult))
                    step_hold(v.tensor_tensor(lg[u][:], lg[u][:], sg[:].unsqueeze(1).broadcast_to([P, NT, E0]),
                                              ALU.subtract))
                    for t in range(NT):
                        step_hold(v.max(m8[u][:, t, :], lg[u][:, t, :]))
                        step_hold(v.max_index(i8[u][:, t, :], m8[u][:, t, :], lg[u][:, t, :]))
                    step(v.tensor_copy(i8f[u][:], i8[u][:]))
                    iota = row("iota", E0).unsqueeze(1).broadcast_to([P, NT, E0])
                    step(v.tensor_tensor(fb[u][:], iota, bc(i8f[u][:, :, 0], E0), ALU.is_equal))
                    step(v.tensor_tensor(mk[u][:], iota, bc(i8f[u][:, :, 1], E0), ALU.is_equal))
                    step(v.tensor_tensor(fb[u][:], fb[u][:], mk[u][:], ALU.add))
                    step(v.tensor_scalar(st[u][:, 2, :], m0, 0.0, None, ALU.is_le))
                    step(v.tensor_tensor(fb[u][:], fb[u][:], bc(st[u][:, 2, :], E0), ALU.mult))
                    step(v.tensor_scalar(mk[u][:], lg[u][:], 0.0, None, ALU.is_gt))
                    step(v.tensor_tensor(mk[u][:], mk[u][:], fb[u][:], ALU.max))
                    step(v.tensor_scalar(lg[u][:], lg[u][:], 0.0, None, ALU.max))
                    step(v.tensor_scalar(st[u][:, 3, :], m0, 0.0, None, ALU.max))
                    v.tensor_tensor(lg[u][:], lg[u][:], bc(st[u][:, 3, :], E0),
                                    ALU.subtract).then_inc(l0_exp_in.sem, 1)
                for u in U:
                    dve.wait_ge(*l0_exp(it, u + 1))
                    step(v.tensor_tensor(pe_[u][:], pe_[u][:], mk[u][:], ALU.mult))
                    step(v.tensor_reduce(st[u][:, 4, :], pe_[u][:], AX.X, ALU.add))
                    step(v.reciprocal(st[u][:, 5, :], st[u][:, 4, :]))
                    v.tensor_tensor(rw[u][:], pe_[u][:], bc(st[u][:, 5, :], E0), ALU.mult).then_inc(l0_rw.sem, 1)
                for u in U:
                    dve.wait_ge(*l0_rw(it, u + 1))
                for g in range(8):
                    for u in U:
                        for t in range(NT):
                            n = 8 * g + 4 * u + t
                            dst = acc[u][:, t, 0:QKV]
                            dve.wait_ge(*qkv_ready(it, n + 1))
                            if g == 0:
                                v.tensor_scalar(dst, B(u, t)[:, 0:QKV], rw[u][:, t, 0:1], None,
                                                ALU.mult).then_inc(qkv_half.sem, 1)
                            else:
                                dve.wait_ge(*qkv_done(it, n - 7))
                                v.scalar_tensor_tensor(dst, B(u, t)[:, 0:QKV], rw[u][:, t, 2 * g:2 * g + 1], dst,
                                                       ALU.mult, ALU.add).then_inc(qkv_half.sem, 1)
                            dve.wait_ge(*qkv_half(it, n + 1))
                            v.scalar_tensor_tensor(dst, B(u, t)[:, QKV:2 * QKV],
                                                   rw[u][:, t, 2 * g + 1:2 * g + 2], dst, ALU.mult,
                                                   ALU.add).then_inc(qkv_done.sem, 1)
                for u in U:
                    for i in range(NT):
                        n, w = 4 * u + i, P * (i + 1)
                        row_i = G[u][:, s_off[i]:s_off[i] + w]
                        dve.wait_ge(*s0_ready(it, n + 1))
                        v.scalar_tensor_tensor(row_i, B(u, (i + 2) % 4)[:, 0:w], float(HD0) ** -0.5,
                                               causal[:, 384 - P * i:384 - P * i + w], ALU.mult,
                                               ALU.add).then_inc(s0_masked.sem, 1)
                        dve.wait_ge(*s0_masked(it, n + 1))
                        step(v.tensor_reduce(st[u][:, 0, i:i + 1], row_i, AX.X, ALU.max))
                        v.tensor_scalar(st[u][:, 1, i:i + 1], st[u][:, 0, i:i + 1], -1.0, None,
                                        ALU.mult).then_inc(s0_max.sem, 1)
                for u in U:
                    dve.wait_ge(*s0_p(it, 4 * u + 4))
                    step(v.reciprocal(st[u][:, 3, :], st[u][:, 2, :]))
                    for i in range(NT):
                        dve.wait_ge(*o0_ready(it, 4 * u + i + 1))
                        v.tensor_scalar(att[u][:, i, :], B(u, (i + 2) % 4)[:, 0:HD0], st[u][:, 3, i:i + 1], None,
                                        ALU.mult).then_inc(att0.sem, 1)

                def mix(r, u):
                    dve.wait_ge(*att0(it, 4 * u + 4))
                    if r == 1:
                        dve.wait_ge(*mixT_ready(it, 4 * u + 4))
                    for t in range(NT):
                        v.tensor_tensor(G[u][:, T * t:T * t + T].rearrange("p (e d) -> p e d", e=8),
                                        att[u][:, t, :].unsqueeze(1).broadcast_to([P, 8, HD0]),
                                        rw[u][:, t, 8 * r:8 * r + 8].unsqueeze(2).broadcast_to([P, 8, HD0]),
                                        ALU.mult).then_inc(mixed.sem, 1)

                def mix_split(r, u):
                    for k in range(4):
                        dve.wait_ge(*mix_hi(it, 8 * r + 4 * u + k + 1))
                        v.tensor_tensor(hid_lo[u][:, k, :], B(u, k % 2)[:], hid_hi[u][:, k, :].bitcast(F32),
                                        ALU.subtract).then_inc(mix_lo.sem, 1)

                for u in U:
                    mix(0, u)
                for u in U:
                    mix_split(0, u)
                for u in U:
                    mix(1, u)
                dve.wait_ge(*l1w_in(it, 1))
                for u in U:
                    step(v.tensor_scalar(F[u][:, 0, :], l1w[:, 0, :], pair_cond[:, u, 0:1], None, ALU.mult))
                    for g in range(1, COND):
                        step(v.scalar_tensor_tensor(F[u][:, 0, :], l1w[:, g, :], pair_cond[:, u, g:g + 1],
                                                    F[u][:, 0, :], ALU.mult, ALU.add))
                    step(v.tensor_tensor(F[u][:, 0, :], F[u][:, 0, :], mask1[:], ALU.mult))
                for u in U:
                    mix_split(1, u)
                for u in U:
                    dve.wait_ge(*oproj0(it, 2 + u + 1))
                    for m in range(KD):
                        step(v.tensor_tensor(xT[u][:, m, :], xT[u][:, m, :], B(u, 2 + m)[:], ALU.add))
                    step(v.tensor_copy(hid_hi[u][:, 0, :], F[u][:, 0, :]))
                    v.tensor_tensor(hid_lo[u][:, 0, :], F[u][:, 0, :], hid_hi[u][:, 0, :].bitcast(F32),
                                    ALU.subtract).then_inc(wbot_ready.sem, 1)
                    split_x(1, u)
                for u in U:
                    for m in range(KD):
                        dve.wait_ge(*l1c_hi(it, 2 * u + m + 1))
                        v.scalar_tensor_tensor(h_lo[u][:, m, :], B(u, m)[:], vec("l1b", m),
                                               h_hi[u][:, m, :].bitcast(F32), ALU.add,
                                               ALU.subtract).then_inc(l1c_h.sem, 1)
                RE = slice(1, E1)
                for u in U:
                    dve.wait_ge(*l1_logits(it, u + 1))
                    step(v.tensor_tensor(lg[u][:, :, RE], B(u, 2)[:, 0:64].rearrange("p (t e) -> p t e", t=NT)[:, :, RE],
                                         row("rb", E1 - 1).unsqueeze(1).broadcast_to([P, NT, E1 - 1]), ALU.add))
                    step(v.tensor_reduce(st[u][:, 0, :], lg[u][:, :, RE], AX.X, ALU.max))
                    v.tensor_tensor(lg[u][:, :, RE], lg[u][:, :, RE], bc(st[u][:, 0, :], E1 - 1),
                                    ALU.subtract).then_inc(l1_exp_in.sem, 1)
                for u in U:
                    dve.wait_ge(*l1_exp(it, u + 1))
                    step(v.tensor_reduce(st[u][:, 1, :], pe_[u][:, :, RE], AX.X, ALU.add))
                    step(v.reciprocal(st[u][:, 2, :], st[u][:, 1, :]))
                    step_hold(v.tensor_tensor(pe_[u][:, :, RE], pe_[u][:, :, RE], bc(st[u][:, 2, :], E1 - 1),
                                              ALU.mult))
                    for t in range(NT):
                        step_hold(v.max(m8[u][:, t, :], pe_[u][:, t, RE]))
                        step_hold(v.max_index(i8[u][:, t, :], m8[u][:, t, :], pe_[u][:, t, RE]))
                    step(v.tensor_copy(i8f[u][:], i8[u][:]))
                    iota = row("iota", E1 - 1).unsqueeze(1).broadcast_to([P, NT, E1 - 1])
                    step(v.tensor_tensor(mk[u][:, :, RE], iota, bc(i8f[u][:, :, 0], E1 - 1), ALU.is_equal))
                    for j in range(1, TOP1):
                        step(v.tensor_tensor(fb[u][:, :, RE], iota, bc(i8f[u][:, :, j], E1 - 1), ALU.is_equal))
                        step(v.tensor_tensor(mk[u][:, :, RE], mk[u][:, :, RE], fb[u][:, :, RE], ALU.add))
                    step(v.memset(rw[u][:, :, 0:1], 1.0))
                    v.tensor_tensor(rw[u][:, :, RE], pe_[u][:, :, RE], mk[u][:, :, RE],
                                    ALU.mult).then_inc(l1_cw.sem, 1)

                def l1_split(e, u):
                    dve.wait_ge(*e1_hi(it, 2 * e + u + 1))
                    hs = slice(2 * (e % 2), 2 * (e % 2) + 2)
                    v.tensor_tensor(hid_lo[u][:, hs, :], F[u][:], hid_hi[u][:, hs, :].bitcast(F32),
                                    ALU.subtract).then_inc(e1_hid.sem, 1)

                for u in U:
                    l1_split(0, u)
                for u in U:
                    dve.wait_ge(*acc1_init(it, u + 1))
                for e in range(E1):
                    for u in U:
                        if e + 1 < E1:
                            l1_split(e + 1, u)
                        for t in range(NT):
                            dve.wait_ge(*e1_y_ready(it, 4 * e + 2 * u + t // 2 + 1))
                            if e > 0:
                                dve.wait_ge(*e1_sum(it, 8 * (e - 1) + 4 * u + t + 1))
                            v.scalar_tensor_tensor(acc[u][:, t, :],
                                                   B(u, 2 + t // 2)[:, D * (t % 2):D * (t % 2) + D],
                                                   rw[u][:, t, e:e + 1], acc[u][:, t, :], ALU.mult,
                                                   ALU.add).then_inc(e1_sum.sem, 1)
                for u in U:
                    for m in range(KD):
                        dve.wait_ge(*accT_ready(it, 2 * u + m + 1))
                        step(v.tensor_tensor(xT[u][:, m, :], xT[u][:, m, :], B(u, m)[:], ALU.add))
                    split_x(2, u)
                for u in U:
                    dve.wait_ge(*hA_hi(it, u + 1))
                    v.scalar_tensor_tensor(hid_lo[u][:, 0, :], B(u, 2)[:], pair_er[:, u:u + 1],
                                           hid_hi[u][:, 0, :].bitcast(F32), ALU.mult,
                                           ALU.subtract).then_inc(hA.sem, 1)
                for u in U:
                    for m in range(KD):
                        dve.wait_ge(*l2c_hi(it, 2 * u + m + 1))
                        v.scalar_tensor_tensor(h_lo[u][:, m, :], B(u, m)[:], vec("l2b", m),
                                               h_hi[u][:, m, :].bitcast(F32), ALU.add,
                                               ALU.subtract).then_inc(l2c_h.sem, 1)
                for u in U:
                    for m in range(KD):
                        v.scalar_tensor_tensor(xT[u][:, m, :], B(u, m)[:], vec("l2b", m), xT[u][:, m, :], ALU.add,
                                               ALU.add).then_inc(l2c_x.sem, 1)

                def rank_tokens(u):
                    junk = G[u][:, 2 * T:3 * T]
                    dve.wait_ge(*sc_sb(it, u + 1))
                    for t in range(NT):
                        s_in = v.scalar_tensor_tensor(junk[:, 0:P], G[u][:, tok(t)], 1.0, ident[:], ALU.mult, ALU.mult,
                                                      accum_out=st[u][:, 3, t:t + 1])
                        if t < NT - 1:
                            step(s_in)
                    s_in.then_inc(sig_in.sem, 1)
                    dve.wait_ge(*sig_in(it, u + 1))
                    for t in range(NT):
                        step(v.tensor_scalar(junk, G[u][:, 0:T], st[u][:, 3, t:t + 1], None, ALU.is_gt, ALU.add,
                                             accum_out=st[u][:, 4, t:t + 1]))
                        step(v.scalar_tensor_tensor(junk, G[u][:, 0:T], st[u][:, 3, t:t + 1],
                                                    before[:, 384 - P * t:384 - P * t + T], ALU.is_equal, ALU.mult,
                                                    accum_out=st[u][:, 5, t:t + 1]))
                    step(v.tensor_tensor(st[u][:, 4, :], st[u][:, 4, :], st[u][:, 5, :], ALU.add))
                    v.tensor_scalar(st[u][:, 4, :], st[u][:, 4, :], float(TOPK2), None,
                                    ALU.is_lt).then_inc(sel_ready.sem, 1)

                for m in range(8):
                    for u in U:
                        n = 2 * m + u
                        dve.wait_ge(*f2_gelu(it, n + 1))
                        if m >= 4:
                            dve.wait_ge(*f2_down(it, n - 7))
                        v.tensor_copy(hid_hi[u][:, m % 4, :], F[u][:, m % 2, :]).then_inc(f2_hi.sem, 1)
                        dve.wait_ge(*f2_hi(it, n + 1))
                        v.tensor_tensor(hid_lo[u][:, m % 4, :], F[u][:, m % 2, :],
                                        hid_hi[u][:, m % 4, :].bitcast(F32), ALU.subtract).then_inc(f2_hid.sem, 1)
                    if m < 2:
                        rank_tokens(m)
                for u in U:
                    dve.wait_ge(*sig_exp(it, u + 1))
                    dve.wait_ge(*sel_ready(it, u + 1))
                    step(v.tensor_scalar(st[u][:, 6, :], st[u][:, 6, :], 1.0, None, ALU.add))
                    step(v.reciprocal(st[u][:, 7, :], st[u][:, 6, :]))
                    v.tensor_tensor(st[u][:, 5, :], st[u][:, 4, :], st[u][:, 7, :],
                                    ALU.mult).then_inc(wtok_ready.sem, 1)
                for u in U:
                    dve.wait_ge(*f2_down(it, 14 + u + 1))
                    dve.wait_ge(*wbc_sb(it, u + 1))
                    dve.wait_ge(*l2c_x(it, 4))
                    for m in range(KD):
                        step(v.scalar_tensor_tensor(F[u][:, m, :], B(u, 2 + m)[:], vec("b2", m), G[u][:, T:2 * T],
                                                    ALU.add, ALU.mult))
                        step(v.tensor_tensor(xT[u][:, m, :], xT[u][:, m, :], F[u][:, m, :], ALU.add))
                    split_x(3, u)
                def hidden_lo(i):
                    u = STEPS3[i // 2][2]
                    dve.wait_ge(*g3_hi(it, i + 1))
                    v.tensor_tensor(hid_lo[u][:, slot3(i), :], gated3(i), hid_hi[u][:, slot3(i), :].bitcast(F32),
                                    ALU.subtract).then_inc(g3_hid.sem, 1)

                def norm_scale(i, u):
                    dve.wait_ge(*nrm3(it, 2 * i + u + 1))
                    v.reciprocal(st[u][:, 2, :], st[u][:, 1, :]).then_inc(rs3.sem, 1)

                def norm(i, gamma, y, u):
                    n = 2 * i + u
                    dve.wait_ge(*rsbc_ready(it, n + 1))
                    if i == 0:
                        dve.wait_ge(*base_ready(it, 2 * u + 2))
                    for k in range(KD):
                        v.scalar_tensor_tensor(F[u][:, k, :], base[u][:, k, :], vec(gamma, k), y[:],
                                               ALU.mult, ALU.mult).then_inc(n3_F.sem, 1)
                    dve.wait_ge(*n3_hi(it, n + 1))
                    v.tensor_tensor(h_lo[u][:], F[u][:], h_hi[u][:].bitcast(F32),
                                    ALU.subtract).then_inc(n3_h.sem, 1)

                def queries_out(u, tp, src):
                    dve.wait_ge(*q3_ready(it, 2 * u + tp + 1))
                    v.tensor_tensor(acc[u][:, 2 * tp:2 * tp + 2, :], src[:].rearrange("p (a n) -> p a n", a=2),
                                    row("bq", D).unsqueeze(1).broadcast_to([P, 2, D]), ALU.add).then_inc(q3_sb.sem, 1)

                def keys_values_out(u, t, src):
                    dve.wait_ge(*kv3_ready(it, 4 * u + t + 1))
                    v.tensor_tensor(kv3[u][:, t, :], src[:], row("bkv", 2 * D), ALU.add).then_inc(kv3_sb.sem, 1)

                def project3(u, i):
                    x, y = B(u, 2), B(u, 3)
                    if i == 0:
                        norm_scale(0, u)
                    if i == 1:
                        norm(0, "gamma1", y, u)
                    if i == 4:
                        dve.wait_ge(*lat_hi(it, u + 1))
                        v.scalar_tensor_tensor(lat_p[u][1], x[0:L3LAT, :], vec("bdown", 0)[0:L3LAT],
                                               lat_p[u][0].bitcast(F32), ALU.add, ALU.subtract).then_inc(lat_lo.sem, 1)
                        queries_out(u, 0, y)
                    if i == 5:
                        queries_out(u, 1, x)
                        keys_values_out(u, 0, y)
                    if i == 6:
                        keys_values_out(u, 1, x)
                        keys_values_out(u, 2, y)
                    if i == 7:
                        keys_values_out(u, 3, x)

                def sum3(src, quarter, u, phase, t):
                    hs = slice(HQ * quarter, HQ * quarter + HQ)
                    return v.tensor_reduce((att3_p if phase == "scores" else q3)[u][:, t, hs, :], src, AX.X, ALU.add)

                def attention3(n):
                    u, phase, t = SWEEP3[n]
                    if phase == "scores" and t == 0:
                        dve.wait_ge(*q3_sb(it, 2 * u + 2))
                    if phase == "scores":
                        dve.wait_ge(*kv3_sb(it, 4 * u + t + 1))
                    elif t == 0:
                        dve.wait_ge(*att3(it, u + 1))
                    first = dve_products(n)
                    for k in range(DVE_Q[u] + 1):
                        if k < DVE_Q[u]:
                            if first + k >= 2:
                                dve.wait_ge(*sum_dve(it, first + k - 1))
                            product3(v, prod3[(first + k) % 2], k, u, phase, t).then_inc(prod_dve.sem, 1)
                        if k >= 1:
                            dve.wait_ge(*prod_dve(it, first + k))
                            sum3(prod3[(first + k - 1) % 2], k - 1, u, phase, t).then_inc(sum_dve.sem, 1)

                def attention3_pool(n):
                    u, phase, t = SWEEP3[n]
                    if u == 1:
                        dve.wait_ge(*psum3_ready(it, n - 7))
                        hs = slice(HQ * DVE_Q[u], HEADS)
                        v.tensor_copy((att3_p if phase == "scores" else q3)[u][:, t, hs, :].rearrange("p h g -> p (h g)"),
                                      PS3[n % 2][:, 0:P]).then_inc(sum_pool.sem, 1)
                        return
                    for k in range(POOL_Q[u]):
                        p = pool_products(n) + k
                        dve.wait_ge(*prod_pool(it, p + 1))
                        sum3(prod3_pool[u][p % 2], DVE_Q[u] + k, u, phase, t).then_inc(sum_pool.sem, 1)

                def heads3(col):
                    return col.unsqueeze(3).broadcast_to([P, NT, HEADS, HEADS])

                def softmax3_in(u):
                    dve.wait_ge(*sum_dve(it, dve_products(8 * u + 4)))
                    dve.wait_ge(*sum_pool(it, pool_sums(8 * u + 4)))
                    step(v.tensor_reduce(lg[u][:], att3_p[u], AX.X, ALU.max))
                    v.tensor_tensor(att3_p[u], att3_p[u], heads3(lg[u][:]), ALU.subtract).then_inc(att3_in.sem, 1)

                def softmax3(u):
                    dve.wait_ge(*att3_exp(it, u + 1))
                    step(v.tensor_reduce(pe_[u][:], att3_p[u], AX.X, ALU.add))
                    step(v.reciprocal(mk[u][:], pe_[u][:]))
                    v.tensor_tensor(att3_p[u], att3_p[u], heads3(mk[u][:]), ALU.mult).then_inc(att3.sem, 1)

                def output_lo(u):
                    for m in range(KD):
                        dve.wait_ge(*o3_hi(it, 2 * u + m + 1))
                        v.tensor_tensor(x_lo[u][:, m, :], B(u, m)[:], x_hi[u][:, m, :].bitcast(F32),
                                        ALU.subtract).then_inc(o3_lo.sem, 1)

                def residual3(u):
                    for m in range(KD):
                        dve.wait_ge(*wo_ready(it, 2 * u + m + 1))
                        v.scalar_tensor_tensor(base[u][:, m, :], B(u, 2 + m)[:], vec("bo", m), base[u][:, m, :],
                                               ALU.add, ALU.add).then_inc(x1_ready.sem, 1)

                def gate_in(u):
                    lgu = lg[u][:, :, 0:E3]
                    dve.wait_ge(*l3_logits(it, u + 1))
                    step(v.tensor_tensor(lgu, LG3[u][:, 0:NT * E3].rearrange("p (t e) -> p t e", t=NT),
                                         row("bg", E3).unsqueeze(1).broadcast_to([P, NT, E3]), ALU.add))
                    step(v.tensor_reduce(st[u][:, 0, :], lgu, AX.X, ALU.max))
                    v.tensor_tensor(lgu, lgu, bc(st[u][:, 0, :], E3), ALU.subtract).then_inc(l3_exp_in.sem, 1)

                def gate(u):
                    pu = pe_[u][:, :, 0:E3]
                    dve.wait_ge(*l3_exp(it, u + 1))
                    step(v.tensor_reduce(st[u][:, 3, :], pu, AX.X, ALU.add))
                    step(v.reciprocal(st[u][:, 4, :], st[u][:, 3, :]))
                    v.tensor_tensor(rw[u][:, :, 0:E3], pu, bc(st[u][:, 4, :], E3), ALU.mult).then_inc(l3_gate.sem, 1)
                    dve.wait_ge(*l3_gate(it, u + 1))

                def experts3(u, c):
                    for half in range(2):
                        for t in range(NT):
                            n = 16 * u + 4 * c + t
                            e = 2 * c + half
                            src, out = B(u, t)[:, D * half:D * half + D], acc[u][:, t, :]
                            if half == 0:
                                dve.wait_ge(*we_ready(it, n + 1))
                            if c == 0 and half == 0:
                                v.tensor_scalar(out, src, rw[u][:, t, 0:1], None, ALU.mult).then_inc(we_half.sem, 1)
                                continue
                            dve.wait_ge(*(we_half(it, n + 1) if half else we_done(it, n - 3)))
                            v.scalar_tensor_tensor(out, src, rw[u][:, t, e:e + 1], out, ALU.mult,
                                                   ALU.add).then_inc((we_done if half else we_half).sem, 1)

                def output3(u):
                    for m in range(KD):
                        step(v.tensor_tensor(base[u][:, m, :], base[u][:, m, :], xT[u][:, m, :], ALU.add))
                    for m in range(KD):
                        dve.wait_ge(*accT_ready(it, 4 + 2 * u + m + 1))
                        v.tensor_tensor(xT[u][:, m, :], base[u][:, m, :], B(u, m)[:], ALU.add).then_inc(x_final.sem, 1)

                for i in range(TILES3 + 1):
                    if i < TILES3:
                        j, c, u = STEPS3[i // 2]
                        dve.wait_ge(*u3_ready(it, i + 1))
                        dve.wait_ge(*g3_gelu(it, i + 1))
                        if i >= 2:
                            dve.wait_ge(*g3_hid(it, i - 1))
                        v.scalar_tensor_tensor(gated3(i), gelu3[i % 2], pair_skw[:, u, j:j + 1] if j < 2 else 1.0,
                                               PB[i % 2][1][:], ALU.mult, ALU.mult).then_inc(g3_gated.sem, 1)
                    if i >= 1:
                        hidden_lo(i - 1)
                    if PROJECT_TILE <= i < TILES3:
                        project3(0, i - PROJECT_TILE)
                    if i in SWEEP_TILES:
                        attention3(SWEEP_TILES.index(i))
                    if i - 1 in SWEEP_TILES:
                        attention3_pool(SWEEP_TILES.index(i - 1))
                    if i == SOFTMAX_IN_TILE:
                        softmax3_in(0)
                    if i == SOFTMAX_TILE:
                        softmax3(0)
                attention3(6)
                project3(1, 0)
                attention3_pool(6)
                project3(1, 1)
                attention3(7)
                attention3_pool(7)
                project3(1, 4)
                output_lo(0)
                project3(1, 5)
                residual3(0)
                project3(1, 6)
                norm_scale(1, 0)
                project3(1, 7)
                attention3(8)
                norm(1, "gamma2", B(0, 1), 0)
                attention3_pool(8)
                attention3(9)
                gate_in(0)
                attention3_pool(9)
                gate(0)
                for c in range(2):
                    attention3(10 + c)
                    experts3(0, c)
                    attention3_pool(10 + c)
                softmax3_in(1)
                experts3(0, 2)
                softmax3(1)
                attention3(12)
                experts3(0, 3)
                attention3_pool(12)
                attention3(13)
                output3(0)
                attention3_pool(13)
                attention3(14)
                attention3(15)
                attention3_pool(14)
                attention3_pool(15)
                output_lo(1)
                residual3(1)
                norm_scale(1, 1)
                norm(1, "gamma2", B(1, 1), 1)
                gate_in(1)
                gate(1)
                for c in range(4):
                    experts3(1, c)
                output3(1)
                assert n_step[0] == DVE_STEPS, n_step[0]


def layouts(i):
    f = {}

    def cols(w):
        return w.reshape(-1, P, w.shape[-1]).transpose(1, 0, 2)

    def side(*parts):
        return np.concatenate([p.reshape(p.shape[0], -1) for p in parts], axis=1)

    def percol(v):
        return v.reshape(-1, P).T

    def transposed(w):
        return np.swapaxes(w, -1, -2)

    f["x"] = transposed(i["x"]).reshape(BATCH, KD, P, T).transpose(0, 2, 1, 3)
    c = i["cond_8"]
    f["cond"] = np.broadcast_to(c.reshape(1, -1), (P, BATCH * COND))
    f["cond_er"] = np.repeat(c.T, RANK2, axis=0)
    up, gate, down = (transposed(i[f"L0_cond_W_{n}"]) for n in ("up", "gate", "down"))
    f["l0c"] = np.stack([np.stack([side(cols(up[e][:, 256 * a:256 * a + 256]), cols(gate[e][:, 256 * a:256 * a + 256]))
                                   for a in range(2)] + [side(cols(down[e]))]) for e in range(COND)])
    f["l0b"] = np.stack([side(percol(i["L0_cond_b_up"][e]), percol(i["L0_cond_b_gate"][e]),
                              percol(i["L0_cond_b_down"][e])) for e in range(COND)])
    qkv = np.concatenate([i["L0_ffn_q_proj"], i["L0_ffn_k_proj"], i["L0_ffn_v_proj"]], axis=2)
    qkv = qkv.transpose(1, 0, 2).reshape(D, E0 * QKV)
    f["qkv"] = np.stack([side(cols(qkv[:, 768 * a:768 * a + 768])) for a in range(4)])
    o = i["L0_ffn_o_proj"].reshape(E0 * HD0, D)
    f["o0"] = np.stack([side(cols(o[512 * a:512 * a + 512])) for a in range(2)])
    w = transposed(i["L1_cond_weight"])
    f["l1w"] = w.reshape(COND, KD, P, D).transpose(2, 0, 1, 3).reshape(P, -1)
    f["mask1"] = side(cols(i["L1_cond_mask"].T))
    w1 = np.concatenate([i["L1_ffn_sW1"][None], i["L1_ffn_eW1"]])
    w2 = np.concatenate([i["L1_ffn_sW2"][None], i["L1_ffn_eW2"]])
    f["l1"] = np.stack([side(cols(w1[e]), cols(w2[e])) for e in range(E1)])
    f["b2rows"] = np.concatenate([i["L1_ffn_sb2"][None], i["L1_ffn_eb2"]])
    eb1 = np.concatenate([i["L1_ffn_sb1"][None], i["L1_ffn_eb1"]])
    A_er = i["L2_cond_As"].reshape(COND * RANK2, D).T
    B_er = i["L2_cond_Bs"].transpose(0, 2, 1).reshape(COND * RANK2, D)
    W1, W2 = i["L2_ffn_W1"], i["L2_ffn_W2"]
    f["l2l"] = side(cols(A_er), B_er)
    f["l2c"] = side(cols(i["L2_cond_W_base"].T))
    f["l2"] = np.stack([side(cols(W1[:, 256 * a:256 * a + 256]), cols(W2[256 * a:256 * a + 256])) for a in range(4)])

    def mlp(g, u, d):
        return np.stack([side(cols(g[:, 256 * a:256 * a + 256]), cols(u[:, 256 * a:256 * a + 256]),
                              cols(d[256 * a:256 * a + 256])) for a in range(4)])

    f["skill"] = np.stack([mlp(i["L3_cond_skill_gate"][e], i["L3_cond_skill_up"][e], i["L3_cond_skill_down"][e])
                           for e in range(COND)])
    f["shared"] = mlp(i["L3_cond_shared_gate"], i["L3_cond_shared_up"], i["L3_cond_shared_down"])
    up = i["L3_ffn_Wup"].reshape(L3LAT, HEADS, 2, HD3)
    kv = np.zeros((P, 2 * D), np.float32)
    kv[:L3LAT] = side(up[:, :, 0].reshape(L3LAT, D), up[:, :, 1].reshape(L3LAT, D))
    f["l3p"] = side(cols(i["L3_ffn_Wq"]), cols(i["L3_ffn_Wdown"]), kv)
    we = i["L3_ffn_We"].transpose(1, 0, 2).reshape(D, E3 * D)
    we = [side(cols(we[:, 512 * a:512 * a + 512])) for a in range(4)]
    f["l3oe"] = side(cols(i["L3_ffn_Wo"]), we[0])
    f["l3e"] = np.stack(we[1:])
    bup = i["L3_ffn_bup"].reshape(HEADS, 2, HD3)
    bdown = np.zeros(P, np.float32)
    bdown[:L3LAT] = i["L3_ffn_bdown"]
    VEC = [("l1b", percol(i["L1_cond_bias"])), ("eb1", percol(eb1.reshape(-1))), ("l2b", percol(i["L2_cond_b_base"])),
           ("b1", percol(i["L2_ffn_b1"])), ("b2", percol(i["L2_ffn_b2"])), ("gamma1", percol(i["L3_ffn_gamma1"])),
           ("gamma2", percol(i["L3_ffn_gamma2"])), ("bdown", percol(bdown)), ("bo", percol(i["L3_ffn_bo"])),
           ("eps", np.full((P, 1), EPS3, np.float32))]
    bq, bk, bv = i["L3_ffn_bq"], bup[:, 0].reshape(-1), bup[:, 1].reshape(-1)
    ROW = [("iota", np.arange(16, dtype=np.float32)), ("gates", i["L0_ffn_gates"]), ("rb", i["L1_ffn_router_b"]),
           ("bg", i["L3_ffn_bg"]), ("bq", bq), ("bkv", np.concatenate([bk, bv]))]
    router = np.concatenate([np.zeros((D, 1), np.float32), i["L1_ffn_router_W"]], axis=1)
    SMALL = [("sim", side(cols(i["L0_ffn_sim_matrix"]))), ("router", side(cols(router))),
             ("wg", side(cols(i["L3_ffn_Wg"]))),
             ("wr", np.repeat(percol(i["L2_ffn_w_router"]), P, axis=1))]
    offs = {}
    for name, parts in (("vecs", VEC), ("rows", [(n, np.broadcast_to(r.reshape(1, -1), (P, r.size))) for n, r in ROW]),
                        ("small", SMALL)):
        f[name] = np.concatenate([p for _, p in parts], axis=1)
        at = np.cumsum([0] + [p.shape[1] for _, p in parts]).tolist()
        offs[name] = {n: a for (n, _), a in zip(parts, at)}
    f["ident"] = np.eye(P, dtype=np.float32)
    p, j = np.arange(P)[:, None], np.arange(384 + T)[None] - 384
    f["causal"] = np.where(j[:, :T] <= p, 0.0, -1e30).astype(np.float32)
    f["before"] = (j < p).astype(np.float32)
    return {n: np.ascontiguousarray(a, dtype=np.float32) for n, a in f.items()}, offs


def kernel(**inputs):
    import concourse.bacc as bacc
    from concourse.bass_utils import run_bass_kernel_spmd

    arrays, offs = layouts({n: np.asarray(a) for n, a in inputs.items()})
    nc = bacc.Bacc("TRN2", target_bir_lowering=False, num_devices=1)
    A = {n: nc.dram_tensor(f"in_{n}", a.shape, F32, kind="ExternalInput").ap() for n, a in arrays.items()}
    A["out"] = nc.dram_tensor("out_x", (BATCH, P, KD, T), F32, kind="ExternalOutput").ap()
    A["VEC"], A["ROW"], A["SMALL"] = offs["vecs"], offs["rows"], offs["small"]
    A["widths"] = WIDTHS
    nc.disable_value_cache = True
    build(nc, A)
    r = run_bass_kernel_spmd(nc, [{f"in_{n}": a for n, a in arrays.items()}], core_ids=[0])
    out = r.results[0]["out_x"]
    return np.ascontiguousarray(out.transpose(0, 2, 1, 3).reshape(BATCH, D, T).transpose(0, 2, 1))
```
